# Optimizing a Trainium2 kernel written in Bass

```python
import numpy as np
import jax
import jax.numpy as jnp

def _softmax(x, axis=-1):
    return jax.nn.softmax(x, axis=axis)

def _gelu(x):
    return jax.nn.gelu(x, approximate=True)

def _silu(x):
    return jax.nn.silu(x)

def _sigmoid(x):
    return jax.nn.sigmoid(x)

def _layernorm(x, axis=-1, eps=1e-05):
    m = jnp.mean(x, axis=axis, keepdims=True)
    v = jnp.var(x, axis=axis, keepdims=True)
    return (x - m) / jnp.sqrt(v + eps)

def _scatter_add(tgt, idx, src, axis=0):
    return tgt.at[idx].add(src)

def _segment_sum(src, seg, n):
    return jax.ops.segment_sum(src, seg, n)
kernel_name = 'mk_sandwich_d1_jaxref_r4_ac2704'

def setup_inputs(seed: int=0):
    np.random.seed(seed)
    _w = jnp.asarray

    def _L0_attn_setup():
        import jax, jax.numpy as jnp
        import numpy as np
        DIM = 256
        HEADS = 16
        EPS = 1e-12
        key = jax.random.key(seed)
        ks = jax.random.split(key, 6)
        b, n, dim, h = (2, 512, DIM, HEADS)
        x = jax.random.normal(ks[0], (b, n, dim), dtype=jnp.float32)
        w_qkv = jax.random.normal(ks[1], (3 * dim, dim), dtype=jnp.float32) / np.sqrt(dim)
        w_out = jax.random.normal(ks[2], (dim, dim), dtype=jnp.float32) / np.sqrt(dim)
        b_out = jax.random.normal(ks[3], (dim,), dtype=jnp.float32) * 0.02
        norm_g = jnp.ones((1, h, 1, 1), dtype=jnp.float32)
        norm_b = jnp.zeros((1, h, 1, 1), dtype=jnp.float32)
        return {'x': x, 'w_qkv': w_qkv, 'w_out': w_out, 'b_out': b_out, 'norm_g': norm_g, 'norm_b': norm_b}
    _L0_attn_in = _L0_attn_setup()

    def _L0_ffn_setup():
        import jax, jax.numpy as jnp
        import numpy as np
        B, SEQ, DIM = (2, 1024, 256)
        E, S = (8, 128)
        HID = 4 * DIM
        SCALE = DIM ** 0.5

        def rmsnorm(x, gamma):
            n = jnp.linalg.norm(x, axis=-1, keepdims=True)
            return x / jnp.maximum(n, 1e-12) * SCALE * gamma
        key = jax.random.key(seed)
        ks = jax.random.split(key, 4)
        w_init = lambda k, shape: jax.random.normal(k, shape, dtype=jnp.float32) * 0.02
        return {'x': jax.random.normal(ks[0], (B, SEQ, DIM), dtype=jnp.float32), 'norm_gamma': jnp.ones((DIM,), jnp.float32), 'slot_norm_gamma': jnp.ones((DIM,), jnp.float32), 'slot_embeds': jax.random.normal(ks[1], (E, S, DIM), dtype=jnp.float32), 'w1': w_init(ks[2], (E, DIM, HID)), 'b1': jnp.zeros((E, HID), jnp.float32), 'w2': w_init(ks[3], (E, HID, DIM)), 'b2': jnp.zeros((E, DIM), jnp.float32)}
    _L0_ffn_in = _L0_ffn_setup()
    _d = {'L0_attn_x': _L0_attn_in['x'], 'L0_attn_w_qkv': _L0_attn_in['w_qkv'], 'L0_attn_w_out': _L0_attn_in['w_out'], 'L0_attn_b_out': _L0_attn_in['b_out'], 'L0_attn_norm_g': _L0_attn_in['norm_g'], 'L0_attn_norm_b': _L0_attn_in['norm_b'], 'L0_ffn_norm_gamma': _L0_ffn_in['norm_gamma'], 'L0_ffn_slot_norm_gamma': _L0_ffn_in['slot_norm_gamma'], 'L0_ffn_slot_embeds': _L0_ffn_in['slot_embeds'], 'L0_ffn_w1': _L0_ffn_in['w1'], 'L0_ffn_b1': _L0_ffn_in['b1'], 'L0_ffn_w2': _L0_ffn_in['w2'], 'L0_ffn_b2': _L0_ffn_in['b2']}
    _x0 = _d['L0_attn_x']
    _d['L0_attn_x'] = jax.random.normal(jax.random.fold_in(jax.random.key(seed), 1), (8, 512, 256), dtype=_x0.dtype)
    del _x0
    return _d

def reference(L0_attn_x, L0_attn_w_qkv, L0_attn_w_out, L0_attn_b_out, L0_attn_norm_g, L0_attn_norm_b, L0_ffn_norm_gamma, L0_ffn_slot_norm_gamma, L0_ffn_slot_embeds, L0_ffn_w1, L0_ffn_b1, L0_ffn_w2, L0_ffn_b2):

    def _L0_attn_ref(x, w_qkv, w_out, b_out, norm_g, norm_b):
        import jax, jax.numpy as jnp
        import numpy as np
        DIM = 256
        HEADS = 16
        EPS = 1e-12
        b, n, dim = x.shape
        h = HEADS
        d = dim // h
        qkv = jnp.einsum('bnm,om->bno', x, w_qkv)
        qkv = qkv.reshape(b, n, 3, h, d)
        q, k, v = [jnp.transpose(qkv[:, :, i], (0, 2, 1, 3)) for i in range(3)]
        dots = jnp.einsum('bhid,bhjd->bhij', q, k)
        norm = jnp.sqrt(jnp.sum(dots * dots, axis=-1, keepdims=True))
        attn = dots / jnp.maximum(norm, EPS) * norm_g + norm_b
        out = jnp.einsum('bhij,bhjd->bhid', attn, v)
        out = jnp.transpose(out, (0, 2, 1, 3)).reshape(b, n, dim)
        return jnp.einsum('bnm,om->bno', out, w_out) + b_out

    def _L0_ffn_ref(x, norm_gamma, slot_norm_gamma, slot_embeds, w1, b1, w2, b2):
        import jax, jax.numpy as jnp
        import numpy as np
        B, SEQ, DIM = (2, 1024, 256)
        E, S = (8, 128)
        HID = 4 * DIM
        SCALE = DIM ** 0.5

        def rmsnorm(x, gamma):
            n = jnp.linalg.norm(x, axis=-1, keepdims=True)
            return x / jnp.maximum(n, 1e-12) * SCALE * gamma
        xn = rmsnorm(x, norm_gamma)
        sn = rmsnorm(slot_embeds, slot_norm_gamma)
        logits = jnp.einsum('bnd,esd->bnes', xn, sn)
        dispatch = jax.nn.softmax(logits, axis=1)
        b, n, e, s = logits.shape
        combine = jax.nn.softmax(logits.reshape(b, n, e * s), axis=-1)
        slots = jnp.einsum('bnd,bnes->besd', xn, dispatch)
        h = jnp.einsum('besd,edh->besh', slots, w1) + b1[None, :, None, :]
        h = jax.nn.gelu(h, approximate=False)
        eo = jnp.einsum('besh,ehd->besd', h, w2) + b2[None, :, None, :]
        eo = eo.reshape(b, e * s, DIM)
        out = jnp.einsum('bmd,bnm->bnd', eo, combine)
        return out
    x = L0_attn_x
    x = x + _layernorm(_L0_attn_ref(_layernorm(x, axis=-1), L0_attn_w_qkv, L0_attn_w_out, L0_attn_b_out, L0_attn_norm_g, L0_attn_norm_b), axis=-1)
    x = x + _layernorm(_L0_ffn_ref(_layernorm(x, axis=-1), L0_ffn_norm_gamma, L0_ffn_slot_norm_gamma, L0_ffn_slot_embeds, L0_ffn_w1, L0_ffn_b1, L0_ffn_w2, L0_ffn_b2), axis=-1)
    return x

_drawn_inputs = setup_inputs


def setup_inputs(seed=0):
    import zlib

    import numpy as np

    out = dict(_drawn_inputs(seed))
    spreads = {'L0_attn_norm_g': (1.0, 0.2),
     'L0_attn_norm_b': (0.0, 0.1),
     'L0_ffn_norm_gamma': (1.0, 0.2),
     'L0_ffn_slot_norm_gamma': (1.0, 0.2),
     'L0_ffn_b1': (0.0, 0.1),
     'L0_ffn_b2': (0.0, 0.1)}
    factors = {'L0_attn_b_out': 4.533}
    for name, (base, spread) in spreads.items():
        noise = np.random.default_rng([zlib.crc32(name.encode()), seed]).standard_normal(out[name].shape)
        drawn = base * np.exp(spread * noise) if base else spread * noise
        out[name] = jnp.asarray(drawn.astype(out[name].dtype))
    for name, factor in factors.items():
        out[name] = (out[name] * factor).astype(out[name].dtype)
    return out
```

```python
from contextlib import ExitStack

import concourse.bass as bass
from concourse import mybir
from concourse.bass import ds

F32 = mybir.dt.float32
F32R = mybir.dt.float32r
ALU = mybir.AluOpType
ACT = mybir.ActivationFunctionType
AX = mybir.AxisListType


def attention_then_soft_moe(nc, x, wqkv_t, wout_t, bout, norm_g, norm_b, gamma, slot_gamma,
                            slots_in, w1, b1, w2, b2, identity, head_mask, out):
    P = 128
    B, N, D = x.shape
    E, _, HID = w1.shape
    S = slots_in.shape[1]
    NT = N // P
    KD = D // P
    KH = HID // P
    HALVES = 2
    EH = E // HALVES
    BH = B // HALVES
    HALF = BH * S
    DZ = D + 2
    RING = 4
    LN_EPS = 1e-5
    NORM_EPS = 1e-12
    ROOT_D = float(D) ** 0.5
    PASSES = [(0, 0), (0, 1), (1, 0)]
    assert S == P and N == 512 and D == 256 and B == 8 and E == 8 and HALF == 512

    x2_dram = nc.dram_tensor("x2_scratch", [B, N, D], F32, kind="Internal").ap()
    comb_dram = nc.dram_tensor("combine_scratch", [B, E, P, N], F32, kind="Internal").ap()

    def token_tiles(ap):
        return ap.rearrange("b (t p) d -> p (b t) d", p=P)

    x_v, x2_v, out_v = token_tiles(x), token_tiles(x2_dram), token_tiles(out)
    comb_v = comb_dram.rearrange("b e p n -> p (b e) n")
    w1_v = w1.rearrange("e (k p) h -> p (e k) h", p=P)
    w2_v = w2.rearrange("e (k p) d -> p (e k) d", p=P)

    with ExitStack() as ctx:
        def sem(name):
            return ctx.enter_context(nc.semaphore(name))

        def sb_in(scope):
            return lambda name, shape, dt=F32: scope.enter_context(nc.sbuf_tensor(name, shape, dt))

        sb = sb_in(ctx)
        slots_eo = sb("slots_eo", [P, E * HALVES, KD * HALF])
        ident = sb("ident", [P, P])
        ones_r = sb("ones_r", [P, P], F32R)
        ones_f = sb("ones_f", [P, P])
        eps_ln = sb("eps_ln", [P, 1])
        zero_col = sb("zero_col", [P, 1])
        gam = sb("gam", [P, KD])
        sgam = sb("sgam", [P, KD])
        both_gam = sb("both_gam", [P, KD])
        b1_sb = sb("b1_sb", [P, E * KH])
        b2_bc = sb("b2_bc", [P, E, D])
        snT = sb("snT", [P, 2, KD, E * S], F32R)

        with ExitStack() as scope:
            sb = sb_in(scope)
            wqkvT = sb("wqkvT", [P, KD, 3 * D])
            woutT = sb("woutT", [P, KD, D])
            bout_bc = sb("bout_bc", [P, D])
            g_col = sb("g_col", [P, KD])
            b_col = sb("b_col", [P, KD])
            mask = sb("mask", [P, P])
            se = sb("se", [P, E, D])
            se_sq = sb("se_sq", [P, D])
            se_sum = sb("se_sum", [P, E])
            se_scale = sb("se_scale", [P, E])
            xin = sb("xin", [P, 4 * NT, D])
            xn = sb("xn", [P, 2, NT, D])
            xnT = sb("xnT", [P, 2, KD, N])
            xsum = sb("xsum", [P, 2, KD])
            gram = sb("gram", [P, 2, KD, D])
            cw = sb("cw", [P, 2, KD, 2 * D])
            heads = sb("heads", [P, 2, KD, 2, P])
            vb = sb("vb", [P, 2, KD])
            qT = sb("qT", [P, 2, KD, N])
            qGq = sb("qGq", [P, 2, KD, N])
            nrm = sb("nrm", [P, 2, KD, N])
            oT = sb("oT", [P, 2, KD, N])
            proj = sb("proj", [P, 2, NT, D])
            st = sb("st", [P, 2, NT, 6])
            mv = sb("mv", [P, 2, NT, 2])
            rstd = sb("rstd", [P, 2, NT])
            st2 = sb("st2", [P, 2, NT, 6])
            mv2 = sb("mv2", [P, 2, NT, 2])
            rstd2 = sb("rstd2", [P, 2, NT])

        with ExitStack() as scope:
            sb = sb_in(scope)
            x2 = sb("x2", [P, NT, D])
            y = sb("y", [P, NT, D])
            y_r = sb("y_r", [P, 2, NT, D], F32R)
            yT_r = sb("yT_r", [P, 2, KD, N], F32R)
            st_b = sb("st_b", [P, NT, 6])
            mv_b = sb("mv_b", [P, NT, 2])
            roots = sb("roots", [P, 2, NT])
            sc_b = sb("sc_b", [P, 3, NT])
            neg_lt = sb("neg_lt", [P, E, N])
            neg_max = sb("neg_max", [P, E])
            z_disp = sb("z_disp", [P, E])
            rz_disp = sb("rz_disp", [P, E])
            disp = sb("disp", [P, RING, N])
            disp_r = sb("disp_r", [P, 2, HALVES, NT, EH * S], F32R)
            run_min = sb("run_min", [P, N])
            tok_min = sb("tok_min", [P, NT])
            diag = sb("diag", [P, NT, P], F32R)
            shift_bc = sb("shift_bc", [P, N])
            comb = sb("comb", [P, RING, N])

        with ExitStack() as scope:
            sb = sb_in(scope)
            w1_raw = sb("w1_raw", [P, KD, HID])
            w2_raw = sb("w2_raw", [P, KH, D])
            w1_r = sb("w1_r", [P, 2, 2, KD, HID], F32R)
            w2_r = sb("w2_r", [P, 2, 2, KH, D], F32R)
            sl_r = sb("sl_r", [P, HALVES, 2, KD, HALF], F32R)
            act = sb("act", [P, 2, HALF])
            act_r = sb("act_r", [P, RING, 2, HALF], F32R)

        with ExitStack() as scope:
            sb = sb_in(scope)
            comb_in = sb("comb_in", [P, 2, E, N])
            comb_r = sb("comb_r", [P, RING, 2, N], F32R)
            eo_r = sb("eo_r", [P, 2, 2, E, DZ], F32R)
            x2_d = sb("x2_d", [P, 2, NT, D])
            mix = sb("mix", [P, 2, NT, D])
            rz_d = sb("rz_d", [P, 2, NT])
            st_d = sb("st_d", [P, 2, NT, 6])
            mv_d = sb("mv_d", [P, 2, NT, 2])
            rstd_d = sb("rstd_d", [P, 2, NT])

        bank = [ctx.enter_context(nc.psum_tensor(f"bank{i}", [P, 512], F32)) for i in range(8)]

        consts_loaded = sem("consts_loaded")
        se_loaded = sem("se_loaded")
        x_loaded = [sem(f"x_loaded{u}") for u in range(2)]
        x2_stored = [sem(f"x2_stored{u}") for u in range(2)]
        x2_loaded = sem("x2_loaded")
        comb_stored = [sem(f"comb_stored{r}") for r in range(RING)]
        w_loaded = sem("w_loaded")
        comb_loaded = [sem(f"comb_loaded{u}") for u in range(2)]
        x2d_loaded = [sem(f"x2d_loaded{u}") for u in range(2)]
        out_stored = [sem(f"out_stored{u}") for u in range(2)]
        consts_set = sem("consts_set")
        se_squared = sem("se_squared")
        se_rooted = sem("se_rooted")
        se_step = sem("se_step")
        se_normed = sem("se_normed")
        seT_in_psum = sem("seT_in_psum")
        snT_hi = sem("snT_hi")
        snT_ready = sem("snT_ready")
        x_stats = sem("x_stats")
        x_aggr = sem("x_aggr")
        x_std = sem("x_std")
        x_rstd = sem("x_rstd")
        xn_ready = sem("xn_ready")
        xnT_in_psum = sem("xnT_in_psum")
        xnT_ready = sem("xnT_ready")
        gram_in_psum = sem("gram_in_psum")
        gram_ready = sem("gram_ready")
        cw_in_psum = sem("cw_in_psum")
        cw_ready = sem("cw_ready")
        heads_in_psum = sem("heads_in_psum")
        heads_ready = sem("heads_ready")
        qT_in_psum = sem("qT_in_psum")
        qT_ready = sem("qT_ready")
        gq_in_psum = sem("gq_in_psum")
        qGq_ready = sem("qGq_ready")
        norm_in_psum = sem("norm_in_psum")
        norm_clamped = sem("norm_clamped")
        norm_rooted = sem("norm_rooted")
        norm_inverted = sem("norm_inverted")
        o_scaled = sem("o_scaled")
        oT_ready = sem("oT_ready")
        proj_in_psum = sem("proj_in_psum")
        proj_ready = sem("proj_ready")
        p_stats = sem("p_stats")
        p_aggr = sem("p_aggr")
        p_std = sem("p_std")
        p_rstd = sem("p_rstd")
        p_normed = sem("p_normed")
        x2_ready = sem("x2_ready")
        y_stats = sem("y_stats")
        y_aggr = sem("y_aggr")
        y_rooted = sem("y_rooted")
        y_step = sem("y_step")
        y_scaled = sem("y_scaled")
        y_ready = sem("y_ready")
        y_hi = sem("y_hi")
        y_split = sem("y_split")
        yT_in_psum = sem("yT_in_psum")
        yT_hi = sem("yT_hi")
        yT_ready = sem("yT_ready")
        logits_in_psum = sem("logits_in_psum")
        logits_kept = sem("logits_kept")
        disp_exp = sem("disp_exp")
        disp_inv = sem("disp_inv")
        disp_normed = sem("disp_normed")
        dispT_in_psum = sem("dispT_in_psum")
        disp_hi = sem("disp_hi")
        disp_split = sem("disp_split")
        slots_in_psum = sem("slots_in_psum")
        slots_ready = sem("slots_ready")
        run_min_step = sem("run_min_step")
        min_in_psum = sem("min_in_psum")
        tok_min_ready = sem("tok_min_ready")
        diag_ready = sem("diag_ready")
        shift_in_psum = sem("shift_in_psum")
        shift_ready = sem("shift_ready")
        comb_shifted = sem("comb_shifted")
        comb_exp = sem("comb_exp")
        w_hi = sem("w_hi")
        w_split = sem("w_split")
        sl_hi = sem("sl_hi")
        sl_split = sem("sl_split")
        h_in_psum = sem("h_in_psum")
        h_act = sem("h_act")
        h_hi = sem("h_hi")
        h_split = sem("h_split")
        eo_steps = sem("eo_steps")
        eo_ready = sem("eo_ready")
        eo_padded = sem("eo_padded")
        eor_hi = sem("eor_hi")
        eor_split = sem("eor_split")
        comb_hi = sem("comb_hi")
        comb_split = sem("comb_split")
        comb_used = sem("comb_used")
        z_inv = sem("z_inv")
        mix_ready = sem("mix_ready")
        m_stats = sem("m_stats")
        m_aggr = sem("m_aggr")
        m_std = sem("m_std")
        m_rstd = sem("m_rstd")
        m_normed = sem("m_normed")
        out_ready = sem("out_ready")

        N_CONSTS = 11
        PAIRS = B // 2

        def attention_finished(eng):
            eng.wait_ge(x2_ready, B)
            for u in range(2):
                eng.wait_ge(x2_stored[u], 16 * PAIRS)
            eng.wait_ge(snT_ready, KD * HALVES)

        def weights_finished(eng):
            eng.wait_ge(slots_ready, B * HALVES)
            eng.wait_ge(comb_exp, B * E)
            for r in range(RING):
                eng.wait_ge(comb_stored[r], 16 * B * E // RING)

        def experts_finished(eng):
            eng.wait_ge(eo_steps, E * HALVES * KH)
            eng.wait_ge(eo_ready, E * HALVES)

        def alone(eng):
            eng.nop(nofuse=True)

        block = ctx.enter_context(nc.Block())

        @block.sync
        def _(sp):
            sp.dma_start(ident[:], identity).then_inc(consts_loaded, 16)
            sp.dma_start(mask[:], head_mask).then_inc(consts_loaded, 16)

            def load_x(it, u):
                sp.dma_start(xin[:, ds((it % 2) * 2 * NT + u * NT, NT), :],
                             x_v[:, ds((2 * it + u) * NT, NT), :]).then_inc(x_loaded[u], 16)

            load_x(0, 0)
            load_x(0, 1)
            sp.dma_start(wqkvT[:], wqkv_t.rearrange("(k p) o -> p k o", p=P)).then_inc(consts_loaded, 16)
            sp.dma_start(woutT[:], wout_t.rearrange("(k p) o -> p k o", p=P)).then_inc(consts_loaded, 16)
            sp.dma_start(g_col[:], norm_g).then_inc(consts_loaded, 16)
            sp.dma_start(b_col[:], norm_b).then_inc(consts_loaded, 16)
            sp.dma_start(bout_bc[:], bout.to_broadcast([P, D])).then_inc(consts_loaded, 16)
            sp.dma_start(gam[:], gamma).then_inc(consts_loaded, 16)
            sp.dma_start(sgam[:], slot_gamma).then_inc(consts_loaded, 16)
            sp.dma_start(b1_sb[:], b1).then_inc(consts_loaded, 16)
            sp.dma_start(b2_bc[:], b2.to_broadcast([P, E, D])).then_inc(consts_loaded, 16)
            sp.dma_start(se[:], slots_in.rearrange("e s d -> s e d")).then_inc(se_loaded, 16)

            def store_x2(it, u):
                sp.wait_ge(x2_ready, 2 * it + u + 1)
                sp.dma_start(x2_v[:, ds((2 * it + u) * NT, NT), :], proj[:, u]).then_inc(x2_stored[u], 16)

            with sp.Fori(0, PAIRS - 1) as it:
                sp.wait_ge(x2_ready, 2 * it)
                load_x(it + 1, 0)
                load_x(it + 1, 1)
                store_x2(it, 0)
                store_x2(it, 1)
            store_x2(PAIRS - 1, 0)
            store_x2(PAIRS - 1, 1)
            attention_finished(sp)

            def load_x2(b):
                sp.dma_start(x2[:], x2_v[:, ds(b * NT, NT), :]).then_inc(x2_loaded, 16)

            def store_combine(b, m):
                sp.wait_ge(comb_exp, b * E + m + 1)
                sp.dma_start(comb_v[:, ds(b * E + m, 1), :], comb[:, m % RING:m % RING + 1, :])\
                    .then_inc(comb_stored[m % RING], 16)

            load_x2(0)
            sp.wait_ge(y_ready, 1)
            load_x2(1)
            with sp.Fori(1, B - 1) as b:
                sp.wait_ge(y_ready, b + 1)
                load_x2(b + 1)
                for m in range(E):
                    store_combine(b - 1, m)
            for b in (B - 2, B - 1):
                for m in range(E):
                    store_combine(b, m)
            weights_finished(sp)

            def load_weights(e):
                sp.dma_start(w1_raw[:], w1_v[:, ds(e * KD, KD), :]).then_inc(w_loaded, 16)
                sp.dma_start(w2_raw[:], w2_v[:, ds(e * KH, KH), :]).then_inc(w_loaded, 16)

            load_weights(0)
            with sp.Fori(1, E) as e:
                sp.wait_ge(w_split, 2 * e)
                load_weights(e)
            experts_finished(sp)

            def load_combine(b, u):
                sp.dma_start(comb_in[:, u], comb_v[:, ds(b * E, E), :]).then_inc(comb_loaded[u], 16)

            def load_residual(b, u):
                sp.dma_start(x2_d[:, u], x2_v[:, ds(b * NT, NT), :]).then_inc(x2d_loaded[u], 16)

            def store_out(b, u):
                sp.wait_ge(out_ready, b + 1)
                sp.dma_start(out_v[:, ds(b * NT, NT), :], mix[:, u]).then_inc(out_stored[u], 16)

            for u in range(2):
                load_combine(u, u)
                load_residual(u, u)
            with sp.Fori(0, PAIRS - 1) as it:
                for u in range(2):
                    sp.wait_ge(comb_split, (2 * it + u + 1) * E)
                    load_combine(2 * it + u + 2, u)
                    store_out(2 * it + u, u)
                    load_residual(2 * it + u + 2, u)
            for u in range(2):
                store_out(B - 2 + u, u)
            for u in range(2):
                sp.wait_ge(out_stored[u], 16 * PAIRS)
                sp.wait_ge(x2_stored[u], 16 * PAIRS)
            for r in range(RING):
                sp.wait_ge(comb_stored[r], 16 * B * E // RING)

        @block.gpsimd
        def _(pool):
            attention_finished(pool)

            def normalise_dispatch(b, m):
                pool.wait_ge(disp_inv, b * E + m + 1)
                alone(pool)
                nc.gpsimd.tensor_scalar(disp[:, m % RING, :], disp[:, m % RING, :], rz_disp[:, m:m + 1], 1.0,
                                        ALU.mult, ALU.mult).then_inc(disp_normed, 1)

            with pool.Fori(0, B) as b:
                for m in range(E):
                    normalise_dispatch(b, m)

        @block.tensor
        def _(pe):
            pe.wait_ge(consts_loaded, 16 * N_CONSTS)
            pe.wait_ge(consts_set, 1)
            for h in range(HALVES):
                pe.wait_ge(se_normed, h + 1)
                for k in range(KD):
                    for e in range(EH):
                        last = pe.transpose(bank[2 * h + k][:, e * S:(e + 1) * S],
                                            se[:, h * EH + e, k * P:(k + 1) * P], ident[:])
                    last.then_inc(seT_in_psum, 1)

            def transpose_xn(it, u):
                pe.wait_ge(xn_ready, 2 * it + u + 1)
                pe.wait_ge(o_scaled, 2 * it)
                for k in range(KD):
                    for t in range(NT):
                        last = pe.transpose(bank[4 * u + k][:, t * P:(t + 1) * P],
                                            xn[:, u, t, k * P:(k + 1) * P], ident[:])
                last.then_inc(xnT_in_psum, 1)

            def gram_of_x(it, u):
                pe.wait_ge(proj_ready, 2 * it)
                for m in range(KD):
                    for t in range(NT):
                        last = pe.matmul(bank[4 * u + 2][:, m * D:(m + 1) * D], xn[:, u, t, m * P:(m + 1) * P],
                                         xn[:, u, t, :], start=(t == 0), stop=(t == NT - 1))
                last.then_inc(gram_in_psum, 1)

            def gram_times_kv(it, u):
                pe.wait_ge(gram_ready, 2 * it + u + 1)
                pe.wait_ge(xnT_ready, 2 * it + u + 1)
                for m in range(KD):
                    for k in range(KD):
                        last = pe.matmul(bank[4 * u + m][:, :], gram[:, u, k, m * P:(m + 1) * P],
                                         wqkvT[:, k, D:3 * D], start=(k == 0), stop=(k == KD - 1))
                last.then_inc(cw_in_psum, 1)

            def head_products(it, u):
                pe.wait_ge(cw_ready, 2 * it + u + 1)
                for h in range(KD):
                    for k in range(KD):
                        both = cw[:, u, k, :].rearrange("p (a c) -> p a c", a=2)[:, :, h * P:(h + 1) * P]
                        pe.matmul(bank[4 * u + 2][:, h * D:(h + 1) * D].rearrange("p (a c) -> p a c", a=2),
                                  wqkvT[:, k, D + h * P:D + (h + 1) * P], both, start=(k == 0), stop=(k == KD - 1))
                for h in range(KD):
                    for k in range(KD):
                        last = pe.matmul(bank[4 * u + 3][:, h:h + 1],
                                         wqkvT[:, k, 2 * D + h * P:2 * D + (h + 1) * P], xsum[:, u, k:k + 1],
                                         start=(k == 0), stop=(k == KD - 1))
                last.then_inc(heads_in_psum, 1)

            def queries(it, u):
                pe.wait_ge(cw_ready, 2 * it + u + 1)
                for h in range(KD):
                    for k in range(KD):
                        last = pe.matmul(bank[4 * u + h][:, :], wqkvT[:, k, h * P:(h + 1) * P], xnT[:, u, k, :],
                                         start=(k == 0), stop=(k == KD - 1))
                last.then_inc(qT_in_psum, 1)

            def gram_times_q(it, u):
                pe.wait_ge(heads_ready, 2 * it + u + 1)
                pe.wait_ge(qT_ready, 2 * it + u + 1)
                for h in range(KD):
                    last = pe.matmul(bank[4 * u + 2 + h][:, :], heads[:, u, h, 0, :], qT[:, u, h, :],
                                     start=True, stop=True)
                last.then_inc(gq_in_psum, 1)

            def norms_and_outputs(it, u):
                for h in range(KD):
                    pe.matmul(bank[4 * u + h][:, :], heads[:, u, h, 1, :], qT[:, u, h, :], start=True, stop=True)
                pe.wait_ge(qGq_ready, 2 * it + u + 1)
                for h in range(KD):
                    last = pe.matmul(bank[4 * u + 2 + h][:, :], mask[:], qGq[:, u, h, :], start=True, stop=True)
                last.then_inc(norm_in_psum, 1)

            def projection(it, u):
                pe.wait_ge(oT_ready, 2 * it + u + 1)
                pe.wait_ge(norm_clamped, 2 * it + u + 1)
                for t in range(NT):
                    for h in range(KD):
                        last = pe.matmul(bank[4 * u + 2 + t // 2][:, (t % 2) * D:(t % 2 + 1) * D],
                                         oT[:, u, h, t * P:(t + 1) * P], woutT[:, h, :],
                                         start=(h == 0), stop=(h == KD - 1))
                last.then_inc(proj_in_psum, 1)

            pe.wait_ge(snT_ready, KD * HALVES)
            with pe.Fori(0, PAIRS) as it:
                for step in (transpose_xn, gram_of_x, gram_times_kv, head_products, queries, gram_times_q,
                             norms_and_outputs, projection):
                    for u in range(2):
                        step(it, u)
            attention_finished(pe)

            def transpose_y(b):
                pe.wait_ge(y_ready, b + 1)
                pe.wait_ge(shift_ready, b)
                for k in range(KD):
                    for t in range(NT):
                        last = pe.transpose(bank[6 + k][:, t * P:(t + 1) * P], y[:, t, k * P:(k + 1) * P], ident[:])
                last.then_inc(yT_in_psum, 1)

            def logits(b, m):
                if m == 0:
                    pe.wait_ge(yT_ready, (b + 1) * KD)
                if m >= 2:
                    pe.wait_ge(logits_kept, b * E + m - 1)
                else:
                    pe.wait_ge(logits_kept, b * E)
                steps = [(k, i, j) for k in range(KD) for i, j in PASSES]
                for n, (k, i, j) in enumerate(steps):
                    last = pe.matmul(bank[m % 2][:, :], snT[:, i, k, m * S:(m + 1) * S], yT_r[:, j, k, :],
                                     start=(n == 0), stop=(n == len(steps) - 1))
                last.then_inc(logits_in_psum, 1)

            def transpose_dispatch(b, m):
                pe.wait_ge(disp_normed, b * E + m + 1)
                if m >= 2:
                    pe.wait_ge(disp_split, b * E + m - 1)
                else:
                    pe.wait_ge(disp_split, b * E)
                for t in range(NT):
                    last = pe.transpose(bank[2 + m % 2][:, t * S:(t + 1) * S], disp[:, m % RING, t * P:(t + 1) * P],
                                        ident[:])
                last.then_inc(dispT_in_psum, 1)

            def fill_slots(b, h, part):
                if part == 0:
                    pe.wait_ge(disp_split, b * E + (h + 1) * EH)
                    pe.wait_ge(y_split, b + 1)
                    pe.wait_ge(slots_ready, b * HALVES + h)
                steps = [(k, t, i, j) for k in range(KD) for t in range(NT) for i, j in PASSES]
                per = len(steps) // 3
                for n in range(part * per, (part + 1) * per):
                    k, t, i, j = steps[n]
                    last = pe.matmul(bank[4 + k][:, :], y_r[:, i, t, k * P:(k + 1) * P], disp_r[:, j, h, t, :],
                                     start=(n % (len(steps) // KD) == 0),
                                     stop=(n % (len(steps) // KD) == len(steps) // KD - 1))
                if part == 2:
                    last.then_inc(slots_in_psum, 1)

            def transpose_min(b):
                pe.wait_ge(run_min_step, (b + 1) * (E - 1))
                pe.wait_ge(yT_hi, (b + 1) * KD)
                pe.wait_ge(yT_ready, (b + 1) * KD)
                for t in range(NT):
                    last = pe.transpose(bank[6][:, t * P:(t + 1) * P], run_min[:, t * P:(t + 1) * P], ident[:])
                last.then_inc(min_in_psum, 1)

            def spread_shift(b):
                pe.wait_ge(diag_ready, (b + 1) * NT)
                pe.matmul(bank[7][:, :], ones_r[:], diag[:].rearrange("p t n -> p (t n)"), start=True, stop=True)\
                    .then_inc(shift_in_psum, 1)

            def weights_of(b):
                for m in range(3):
                    logits(b, m)
                for m in range(3, 6):
                    transpose_dispatch(b, m - 3)
                    logits(b, m)
                transpose_dispatch(b, 3)
                logits(b, 6)
                fill_slots(b, 0, 0)
                transpose_dispatch(b, 4)
                logits(b, 7)
                fill_slots(b, 0, 1)
                transpose_dispatch(b, 5)
                fill_slots(b, 0, 2)
                transpose_dispatch(b, 6)
                transpose_dispatch(b, 7)
                transpose_min(b)
                fill_slots(b, 1, 0)
                fill_slots(b, 1, 1)
                spread_shift(b)
                fill_slots(b, 1, 2)

            transpose_y(0)
            with pe.Fori(0, B - 1) as b:
                weights_of(b)
                transpose_y(b + 1)
            weights_of(B - 1)
            weights_finished(pe)

            def hidden(e, q, i):
                f, j = divmod(i, KH)
                if i == 0:
                    pe.wait_ge(w_split, 2 * (e + 1))
                if j == 0:
                    pe.wait_ge(sl_split, e * HALVES + f + 1)
                if i >= RING:
                    pe.wait_ge(h_act, e * HALVES * KH + i - RING + 1)
                else:
                    pe.wait_ge(h_act, e * HALVES * KH)
                steps = [(k, a, c) for k in range(KD) for a, c in PASSES]
                for n, (k, a, c) in enumerate(steps):
                    last = pe.matmul(bank[i % RING][:, :], w1_r[:, q, a, k, j * P:(j + 1) * P], sl_r[:, f, c, k, :],
                                     start=(n == 0), stop=(n == len(steps) - 1))
                last.then_inc(h_in_psum, 1)

            def expert_out(e, q, i):
                f, j = divmod(i, KH)
                pe.wait_ge(h_split, e * HALVES * KH + i + 1)
                if j == 0:
                    pe.wait_ge(eo_ready, e * HALVES)
                for c in range(BH):
                    for n, (a, w) in enumerate(PASSES):
                        last = pe.matmul(bank[4 + 2 * f + c // 2][:, (c % 2) * D:(c % 2 + 1) * D],
                                         act_r[:, i % RING, a, c * S:(c + 1) * S], w2_r[:, q, w, j, :],
                                         start=(j == 0 and n == 0 and c % 2 == 0), stop=(j == KH - 1 and n == 2),
                                         skip_group_check=True)
                last.then_inc(eo_steps, 1)

            def expert(e, q):
                steps = HALVES * KH
                for i in range(steps + 2):
                    if i < steps:
                        hidden(e, q, i)
                    if i >= 2:
                        expert_out(e, q, i - 2)

            with pe.Fori(0, E // 2) as it:
                for q in range(2):
                    expert(2 * it + q, q)
            experts_finished(pe)

            def combine(b, u):
                pe.wait_ge(eor_split, b + 1)
                if not (isinstance(b, int) and b < 2):
                    pe.wait_ge(mix_ready, b - 1)
                for m in range(E):
                    pe.wait_ge(comb_split, b * E + m + 1)
                    for t in range(NT):
                        for n, (i, j) in enumerate(PASSES):
                            last = pe.matmul(bank[4 * u + t][:, 0:DZ], comb_r[:, m % RING, i, t * P:(t + 1) * P],
                                             eo_r[:, u, j, m, :], start=(m == 0 and n == 0),
                                             stop=(m == E - 1 and n == 2))
                    last.then_inc(comb_used, 1)

            pe.wait_ge(eo_padded, 2)
            combine(0, 0)
            combine(1, 1)
            with pe.Fori(1, PAIRS) as it:
                for u in range(2):
                    combine(2 * it + u, u)

        @block.scalar
        def _(sc):
            act_fn = nc.scalar.activation
            sc.wait_ge(se_loaded, 16)
            sc.wait_ge(consts_set, 1)
            for e in range(E):
                if e:
                    sc.wait_ge(se_squared, e)
                act_fn(se_sq[:], se[:, e, :], ACT.Square, bias=zero_col[:], accum_out=se_sum[:, e:e + 1])\
                    .then_inc(se_squared, 1)
            sc.wait_ge(se_squared, E)
            act_fn(se_scale[:], se_sum[:], ACT.Sqrt, bias=zero_col[:]).then_inc(se_rooted, 1)
            for h in range(HALVES):
                for k in range(KD):
                    sc.wait_ge(seT_in_psum, h * KD + k + 1)
                    sc.wait_ge(se_step, 3)
                    act_fn(snT[:, 0, k, h * EH * S:(h + 1) * EH * S], bank[2 * h + k][:, :], ACT.Copy,
                           scale=both_gam[:, k:k + 1]).then_inc(snT_hi, 1)

            def root_x(it, u):
                sc.wait_ge(x_aggr, 2 * it + u + 1)
                act_fn(rstd[:, u, :], mv[:, u, :, 1], ACT.Sqrt, bias=eps_ln[:]).then_inc(x_std, 1)

            def keep_xnT(it, u):
                sc.wait_ge(xnT_in_psum, 2 * it + u + 1)
                sc.wait_ge(qT_in_psum, 2 * it)
                for k in range(KD):
                    last = act_fn(xnT[:, u, k, :], bank[4 * u + k][:, :], ACT.Identity, bias=zero_col[:],
                                  accum_out=xsum[:, u, k:k + 1])
                last.then_inc(xnT_ready, 1)

            def keep_cw(it, u):
                sc.wait_ge(cw_in_psum, 2 * it + u + 1)
                for k in range(KD):
                    last = act_fn(cw[:, u, k, :], bank[4 * u + k][:, :], ACT.Copy)
                last.then_inc(cw_ready, 1)

            def keep_qT(it, u):
                sc.wait_ge(qT_in_psum, 2 * it + u + 1)
                sc.wait_ge(norm_in_psum, 2 * it)
                for h in range(KD):
                    last = act_fn(qT[:, u, h, :], bank[4 * u + h][:, :], ACT.Copy)
                last.then_inc(qT_ready, 1)

            def root_norm(it, u):
                sc.wait_ge(norm_clamped, 2 * it + u + 1)
                act_fn(nrm[:, u], nrm[:, u], ACT.Sqrt, bias=zero_col[:]).then_inc(norm_rooted, 1)

            def add_vb(it, u):
                sc.wait_ge(o_scaled, 2 * it + u + 1)
                for h in range(KD):
                    last = act_fn(oT[:, u, h, :], oT[:, u, h, :], ACT.Identity, bias=vb[:, u, h:h + 1])
                last.then_inc(oT_ready, 1)

            def root_proj(it, u):
                sc.wait_ge(p_aggr, 2 * it + u + 1)
                act_fn(rstd2[:, u, :], mv2[:, u, :, 1], ACT.Sqrt, bias=eps_ln[:]).then_inc(p_std, 1)

            for u in range(2):
                root_x(0, u)

            def attention_pair(it, last):
                for step in (keep_xnT, keep_cw, keep_qT):
                    for u in range(2):
                        step(it, u)
                if not last:
                    for u in range(2):
                        root_x(it + 1, u)
                for step in (root_norm, add_vb, root_proj):
                    for u in range(2):
                        step(it, u)

            with sc.Fori(0, PAIRS - 1) as it:
                attention_pair(it, False)
            attention_pair(PAIRS - 1, True)
            attention_finished(sc)

            def root_y(b):
                sc.wait_ge(y_aggr, b + 1)
                act_fn(roots[:, 0, :], mv_b[:, :, 1], ACT.Sqrt, bias=eps_ln[:])
                act_fn(roots[:, 1, :], mv_b[:, :, 1], ACT.Sqrt, bias=zero_col[:]).then_inc(y_rooted, 1)

            def round_yT(b):
                sc.wait_ge(yT_in_psum, b + 1)
                sc.wait_ge(logits_in_psum, b * E)
                for k in range(KD):
                    act_fn(yT_r[:, 0, k, :], bank[6 + k][:, :], ACT.Copy).then_inc(yT_hi, 1)

            def round_y(b):
                sc.wait_ge(y_ready, b + 1)
                sc.wait_ge(slots_in_psum, b * HALVES)
                act_fn(y_r[:, 0], y[:], ACT.Copy).then_inc(y_hi, 1)

            def exp_dispatch(b, m):
                sc.wait_ge(logits_kept, b * E + m + 1)
                if m >= RING:
                    sc.wait_ge(dispT_in_psum, b * E + m - RING + 1)
                else:
                    sc.wait_ge(dispT_in_psum, b * E)
                act_fn(disp[:, m % RING, :], neg_lt[:, m, :], ACT.Exp, bias=neg_max[:, m:m + 1], scale=-1.0,
                       accum_out=z_disp[:, m:m + 1]).then_inc(disp_exp, 1)

            def round_dispatch(b, m):
                sc.wait_ge(dispT_in_psum, b * E + m + 1)
                h = m // EH
                if m % EH == 0:
                    sc.wait_ge(slots_in_psum, b * HALVES)
                act_fn(disp_r[:, 0, h, :, (m % EH) * S:(m % EH + 1) * S],
                       bank[2 + m % 2][:, :].rearrange("p (t s) -> p t s", t=NT), ACT.Copy).then_inc(disp_hi, 1)

            def keep_slots(b, h):
                sc.wait_ge(slots_in_psum, b * HALVES + h + 1)
                alone(sc)
                for k in range(KD):
                    dst = slots_eo[:, h * EH * HALVES:(h + 1) * EH * HALVES, :].rearrange(
                        "p (e f) n -> p e (f n)", f=HALVES)
                    at = b * S + b // BH * (KD * HALF - BH * S) + k * HALF
                    last = act_fn(dst[:, :, ds(at, S)],
                                  bank[4 + k][:, :].rearrange("p (e s) -> p e s", e=EH), ACT.Copy,
                                  scale=gam[:, k:k + 1])
                last.then_inc(slots_ready, 1)

            def keep_shift(b):
                sc.wait_ge(shift_in_psum, b + 1)
                sc.wait_ge(comb_shifted, b * E)
                act_fn(shift_bc[:], bank[7][:, :], ACT.Copy).then_inc(shift_ready, 1)

            def exp_combine(b, m):
                sc.wait_ge(comb_shifted, b * E + m + 1)
                act_fn(comb[:, m % RING, :], comb[:, m % RING, :], ACT.Exp, bias=zero_col[:], scale=-1.0)\
                    .then_inc(comb_exp, 1)

            def weights_of(b, first=False, last=False):
                round_y(b)
                for m in range(E + 2):
                    if m < E:
                        exp_dispatch(b, m)
                        if not first:
                            exp_combine(b - 1, m)
                    if m >= 2:
                        round_dispatch(b, m - 2)
                    if m == 7:
                        keep_slots(b, 0)
                    if m == 5 and not last:
                        root_y(b + 1)
                keep_shift(b)
                keep_slots(b, 1)
                if not last:
                    round_yT(b + 1)

            root_y(0)
            round_yT(0)
            weights_of(0, first=True)
            with sc.Fori(1, B - 1) as b:
                weights_of(b)
            weights_of(B - 1, last=True)
            for m in range(E):
                exp_combine(B - 1, m)
            weights_finished(sc)

            def round_weights(e, q):
                sc.wait_ge(w_loaded, 32 * (e + 1))
                act_fn(w1_r[:, q, 0], w1_raw[:], ACT.Copy).then_inc(w_hi, 1)
                act_fn(w2_r[:, q, 0], w2_raw[:], ACT.Copy).then_inc(w_hi, 1)

            def activate(e, i):
                f, j = divmod(i, KH)
                n = e * HALVES * KH + i
                sc.wait_ge(h_in_psum, n + 1)
                if i >= 2:
                    sc.wait_ge(h_split, n - 1)
                else:
                    sc.wait_ge(h_split, e * HALVES * KH)
                alone(sc)
                act_fn(act[:, i % 2, :], bank[i % RING][:, :], ACT.Gelu, bias=b1_sb[:, ds(e * KH + j, 1)])\
                    .then_inc(h_act, 1)
                sc.wait_ge(h_act, n + 1)
                if i >= RING:
                    sc.wait_ge(eo_steps, n - RING + 1)
                else:
                    sc.wait_ge(eo_steps, e * HALVES * KH)
                act_fn(act_r[:, i % RING, 0, :], act[:, i % 2, :], ACT.Copy).then_inc(h_hi, 1)

            def expert(e, q, last=False):
                for i in range(HALVES * KH):
                    activate(e, i)
                    if i == 5 and not last:
                        sc.wait_ge(eo_steps, e * HALVES * KH)
                        round_weights(e + 1, 1 - q)

            round_weights(0, 0)
            with sc.Fori(0, E // 2 - 1) as it:
                for q in range(2):
                    expert(2 * it + q, q)
            expert(E - 2, 0)
            expert(E - 1, 1, last=True)
            experts_finished(sc)

            def round_combine(b, u, m, first=False):
                if m == 0:
                    sc.wait_ge(comb_loaded[u], 16 * (b // 2 + 1))
                if m >= RING or not first:
                    sc.wait_ge(comb_used, b * E + m - RING + 1)
                act_fn(comb_r[:, m % RING, 0, :], comb_in[:, u, m, :], ACT.Copy).then_inc(comb_hi, 1)

            def keep_mix(b, u):
                sc.wait_ge(z_inv, b + 1)
                sc.wait_ge(out_stored[u], 16 * (b // 2))
                for t in range(NT):
                    last = act_fn(mix[:, u, t, :], bank[4 * u + t][:, 0:D], ACT.Copy, scale=rz_d[:, u, t:t + 1])
                last.then_inc(mix_ready, 1)

            def root_mix(b, u):
                sc.wait_ge(m_aggr, b + 1)
                act_fn(rstd_d[:, u, :], mv_d[:, u, :, 1], ACT.Sqrt, bias=eps_ln[:]).then_inc(m_std, 1)

            def combine(b, u, first=False):
                for m in range(E):
                    round_combine(b, u, m, first)
                    if m == 2 and not first:
                        keep_mix(b - 1, 1 - u)
                    if m == 5 and not first:
                        root_mix(b - 1, 1 - u)

            combine(0, 0, first=True)
            with sc.Fori(0, PAIRS - 1) as it:
                combine(2 * it + 1, 1)
                combine(2 * it + 2, 0)
            combine(B - 1, 1)
            keep_mix(B - 1, 1)
            root_mix(B - 1, 1)

        @block.vector
        def _(dve):
            v = nc.vector
            v.memset(eps_ln[:], LN_EPS)
            v.memset(zero_col[:], 0.0)
            v.memset(ones_f[:], 1.0).then_inc(se_step, 1)
            dve.wait_ge(se_step, 1)
            v.tensor_copy(ones_r[:], ones_f[:]).then_inc(consts_set, 1)
            dve.wait_ge(consts_loaded, 16 * N_CONSTS)
            v.tensor_tensor(both_gam[:], gam[:], sgam[:], ALU.mult).then_inc(se_step, 1)
            dve.wait_ge(se_rooted, 1)
            v.tensor_scalar(se_scale[:], se_scale[:], NORM_EPS, 1.0 / ROOT_D, ALU.max, ALU.mult).then_inc(se_step, 1)
            dve.wait_ge(se_step, 3)
            v.reciprocal(se_scale[:], se_scale[:]).then_inc(se_step, 1)
            dve.wait_ge(se_step, 4)
            for h in range(HALVES):
                for e in range(h * EH, (h + 1) * EH):
                    last = v.tensor_scalar(se[:, e, :], se[:, e, :], se_scale[:, e:e + 1], None, ALU.mult)
                last.then_inc(se_normed, 1)
            for h in range(HALVES):
                for k in range(KD):
                    dve.wait_ge(snT_hi, h * KD + k + 1)
                    cols = slice(h * EH * S, (h + 1) * EH * S)
                    v.scalar_tensor_tensor(out=snT[:, 1, k, cols], in0=bank[2 * h + k][:, :],
                                           scalar=both_gam[:, k:k + 1], in1=snT[:, 0, k, cols].bitcast(F32),
                                           op0=ALU.mult, op1=ALU.subtract).then_inc(snT_ready, 1)

            def norm_x(it, u):
                n = 2 * it + u + 1
                at = (it % 2) * 2 * NT + u * NT
                dve.wait_ge(x_loaded[u], 16 * (it + 1))
                for t in range(NT):
                    last = v.bn_stats(st[:, u, t, :], xin[:, ds(at + t, 1), :])
                last.then_inc(x_stats, 1)
                dve.wait_ge(x_stats, n)
                alone(dve)
                for t in range(NT):
                    last = v.bn_aggr(mv[:, u, t, :], st[:, u, t, :])
                last.then_inc(x_aggr, 1)
                dve.wait_ge(x_std, n)
                v.reciprocal(rstd[:, u, :], rstd[:, u, :]).then_inc(x_rstd, 1)
                dve.wait_ge(x_rstd, n)
                dve.wait_ge(gram_in_psum, 2 * it)
                for t in range(NT):
                    last = v.tensor_scalar(xn[:, u, t:t + 1, :], xin[:, ds(at + t, 1), :], mv[:, u, t, 0:1],
                                           rstd[:, u, t:t + 1], ALU.subtract, ALU.mult)
                last.then_inc(xn_ready, 1)

            def keep_gram(it, u):
                dve.wait_ge(gram_in_psum, 2 * it + u + 1)
                v.tensor_copy(gram[:, u], bank[4 * u + 2][:, :].rearrange("p (k d) -> p k d", k=KD))\
                    .then_inc(gram_ready, 1)

            def keep_heads(it, u):
                dve.wait_ge(heads_in_psum, 2 * it + u + 1)
                dve.wait_ge(norm_in_psum, 2 * it)
                for h in range(KD):
                    src = bank[4 * u + 2]
                    v.tensor_tensor(heads[:, u, h, 0, :], src[:, h * D:h * D + P], mask[:], ALU.mult)
                    v.scalar_tensor_tensor(out=heads[:, u, h, 1, :], in0=src[:, h * D + P:(h + 1) * D],
                                           scalar=g_col[:, h:h + 1], in1=mask[:], op0=ALU.mult, op1=ALU.mult)
                dve.wait_ge(oT_ready, 2 * it)
                v.tensor_tensor(vb[:, u, :], bank[4 * u + 3][:, 0:KD], b_col[:], ALU.mult).then_inc(heads_ready, 1)

            def times_q(it, u):
                dve.wait_ge(gq_in_psum, 2 * it + u + 1)
                for h in range(KD):
                    last = v.tensor_tensor(qGq[:, u, h, :], bank[4 * u + 2 + h][:, :], qT[:, u, h, :], ALU.mult)
                last.then_inc(qGq_ready, 1)

            def clamp_norm(it, u):
                dve.wait_ge(norm_in_psum, 2 * it + u + 1)
                for h in range(KD):
                    last = v.tensor_scalar(nrm[:, u, h, :], bank[4 * u + 2 + h][:, :], NORM_EPS * NORM_EPS, None,
                                           ALU.max)
                last.then_inc(norm_clamped, 1)

            def scale_o(it, u):
                n = 2 * it + u + 1
                dve.wait_ge(norm_rooted, n)
                v.reciprocal(nrm[:, u], nrm[:, u]).then_inc(norm_inverted, 1)
                dve.wait_ge(norm_inverted, n)
                dve.wait_ge(proj_in_psum, 2 * it)
                for h in range(KD):
                    last = v.tensor_tensor(oT[:, u, h, :], bank[4 * u + h][:, :], nrm[:, u, h, :], ALU.mult)
                last.then_inc(o_scaled, 1)

            def add_bias(it, u):
                dve.wait_ge(proj_in_psum, 2 * it + u + 1)
                dve.wait_ge(x2_stored[u], 16 * it)
                for t in range(NT):
                    last = v.tensor_tensor(proj[:, u, t, :],
                                           bank[4 * u + 2 + t // 2][:, (t % 2) * D:(t % 2 + 1) * D], bout_bc[:],
                                           ALU.add)
                last.then_inc(proj_ready, 1)

            def norm_proj(it, u):
                n = 2 * it + u + 1
                at = (it % 2) * 2 * NT + u * NT
                dve.wait_ge(proj_ready, n)
                for t in range(NT):
                    last = v.bn_stats(st2[:, u, t, :], proj[:, u, t, :])
                last.then_inc(p_stats, 1)
                dve.wait_ge(p_stats, n)
                alone(dve)
                for t in range(NT):
                    last = v.bn_aggr(mv2[:, u, t, :], st2[:, u, t, :])
                last.then_inc(p_aggr, 1)
                dve.wait_ge(p_std, n)
                v.reciprocal(rstd2[:, u, :], rstd2[:, u, :]).then_inc(p_rstd, 1)
                dve.wait_ge(p_rstd, n)
                for t in range(NT):
                    last = v.tensor_scalar(proj[:, u, t, :], proj[:, u, t, :], mv2[:, u, t, 0:1],
                                           rstd2[:, u, t:t + 1], ALU.subtract, ALU.mult)
                last.then_inc(p_normed, 1)
                dve.wait_ge(p_normed, n)
                v.tensor_tensor(proj[:, u], proj[:, u], xin[:, ds(at, NT), :], ALU.add).then_inc(x2_ready, 1)

            for u in range(2):
                norm_x(0, u)

            def attention_pair(it, last):
                for step in (keep_gram, keep_heads, times_q):
                    for u in range(2):
                        step(it, u)
                if not last:
                    for u in range(2):
                        norm_x(it + 1, u)
                for step in (clamp_norm, scale_o, add_bias, norm_proj):
                    for u in range(2):
                        step(it, u)

            with dve.Fori(0, PAIRS - 1) as it:
                attention_pair(it, False)
            attention_pair(PAIRS - 1, True)
            attention_finished(dve)

            def norm_y(b):
                dve.wait_ge(x2_loaded, 16 * (b + 1))
                for t in range(NT):
                    last = v.bn_stats(st_b[:, t, :], x2[:, t, :])
                last.then_inc(y_stats, 1)
                dve.wait_ge(y_stats, b + 1)
                alone(dve)
                for t in range(NT):
                    last = v.bn_aggr(mv_b[:, t, :], st_b[:, t, :])
                last.then_inc(y_aggr, 1)

            def scale_y(b):
                dve.wait_ge(y_rooted, b + 1)
                n = 4 * b
                v.reciprocal(sc_b[:, 0, :], roots[:, 0, :]).then_inc(y_step, 1)
                dve.wait_ge(y_step, n + 1)
                v.scalar_tensor_tensor(out=sc_b[:, 1, :], in0=roots[:, 1, :], scalar=ROOT_D, in1=sc_b[:, 0, :],
                                       op0=ALU.mult, op1=ALU.mult).then_inc(y_step, 1)
                dve.wait_ge(y_step, n + 2)
                v.tensor_scalar(sc_b[:, 1, :], sc_b[:, 1, :], NORM_EPS, 1.0 / ROOT_D, ALU.max, ALU.mult)\
                    .then_inc(y_step, 1)
                dve.wait_ge(y_step, n + 3)
                v.reciprocal(sc_b[:, 2, :], sc_b[:, 1, :]).then_inc(y_step, 1)
                dve.wait_ge(y_step, n + 4)
                v.tensor_tensor(sc_b[:, 2, :], sc_b[:, 2, :], sc_b[:, 0, :], ALU.mult).then_inc(y_scaled, 1)
                dve.wait_ge(y_scaled, b + 1)
                dve.wait_ge(y_split, b)
                dve.wait_ge(yT_in_psum, b)
                for t in range(NT):
                    last = v.tensor_scalar(y[:, t, :], x2[:, t, :], mv_b[:, t, 0:1], sc_b[:, 2, t:t + 1],
                                           ALU.subtract, ALU.mult)
                last.then_inc(y_ready, 1)

            def rest_of_y(b):
                dve.wait_ge(y_hi, b + 1)
                v.tensor_tensor(y_r[:, 1], y[:], y_r[:, 0].bitcast(F32), ALU.subtract).then_inc(y_split, 1)

            def rest_of_yT(b):
                for k in range(KD):
                    dve.wait_ge(yT_hi, b * KD + k + 1)
                    v.tensor_tensor(yT_r[:, 1, k, :], bank[6 + k][:, :], yT_r[:, 0, k, :].bitcast(F32),
                                    ALU.subtract).then_inc(yT_ready, 1)

            def keep_logits(b, m, first):
                dve.wait_ge(logits_in_psum, b * E + m + 1)
                dve.wait_ge(disp_exp, b * E)
                if not first:
                    dve.wait_ge(comb_shifted, (b - 1) * E + m + 1)
                v.tensor_scalar(neg_lt[:, m, :], bank[m % 2][:, :], -1.0, None, ALU.mult, ALU.min,
                                accum_out=neg_max[:, m:m + 1]).then_inc(logits_kept, 1)

            def fold_min(b, m):
                n = b * (E - 1) + m
                dve.wait_ge(logits_kept, b * E + m + 1)
                if m == 1:
                    dve.wait_ge(min_in_psum, b)
                    first = neg_lt[:, 0, :]
                else:
                    dve.wait_ge(run_min_step, n - 1)
                    first = run_min[:]
                v.tensor_tensor(run_min[:], first, neg_lt[:, m, :], ALU.min).then_inc(run_min_step, 1)

            def shift_combine(b, m):
                if m == 0:
                    dve.wait_ge(shift_ready, b + 1)
                dve.wait_ge(comb_stored[m % RING], 16 * (b * (E // RING) + m // RING))
                v.tensor_tensor(comb[:, m % RING, :], neg_lt[:, m, :], shift_bc[:], ALU.subtract)\
                    .then_inc(comb_shifted, 1)

            def invert_sum(b, m):
                dve.wait_ge(disp_exp, b * E + m + 1)
                v.reciprocal(rz_disp[:, m:m + 1], z_disp[:, m:m + 1]).then_inc(disp_inv, 1)

            def rest_of_dispatch(b, m):
                dve.wait_ge(disp_hi, b * E + m + 1)
                h, cols = m // EH, slice((m % EH) * S, (m % EH + 1) * S)
                v.tensor_tensor(disp_r[:, 1, h, :, cols], bank[2 + m % 2][:, :].rearrange("p (t s) -> p t s", t=NT),
                                disp_r[:, 0, h, :, cols].bitcast(F32), ALU.subtract).then_inc(disp_split, 1)

            def shift_of_tokens(b):
                dve.wait_ge(min_in_psum, b + 1)
                v.tensor_reduce(tok_min[:], bank[6][:, :].rearrange("p (t n) -> p t n", t=NT), AX.X, ALU.min)\
                    .then_inc(tok_min_ready, 1)
                dve.wait_ge(tok_min_ready, b + 1)
                dve.wait_ge(shift_in_psum, b)
                for t in range(NT):
                    v.tensor_scalar(diag[:, t, :], ident[:], tok_min[:, t:t + 1], None, ALU.mult)\
                        .then_inc(diag_ready, 1)

            def weights_of(b, first=False, last=False):
                if not first:
                    shift_combine(b - 1, 0)
                for m in range(E + 3):
                    if m < E:
                        keep_logits(b, m, first)
                        if m + 1 < E and not first:
                            shift_combine(b - 1, m + 1)
                    if m == 0:
                        rest_of_y(b)
                    if 1 <= m < E + 1:
                        invert_sum(b, m - 1)
                    if 1 <= m < E:
                        fold_min(b, m)
                    if m >= 3:
                        rest_of_dispatch(b, m - 3)
                    if m == 4 and not last:
                        norm_y(b + 1)
                    if m == 6 and not last:
                        scale_y(b + 1)
                shift_of_tokens(b)
                if not last:
                    rest_of_yT(b + 1)

            norm_y(0)
            scale_y(0)
            rest_of_yT(0)
            weights_of(0, first=True)
            with dve.Fori(1, B - 1) as b:
                weights_of(b)
            weights_of(B - 1, last=True)
            for m in range(E):
                shift_combine(B - 1, m)
            weights_finished(dve)

            def rest_of_weights(e, q):
                for n, (raw, parts) in enumerate(((w1_raw, w1_r), (w2_raw, w2_r))):
                    dve.wait_ge(w_hi, 2 * e + n + 1)
                    v.tensor_tensor(parts[:, q, 1], raw[:], parts[:, q, 0].bitcast(F32), ALU.subtract)\
                        .then_inc(w_split, 1)

            def split_slots(e, f, first=False):
                n = e * HALVES + f + 1
                if not first:
                    dve.wait_ge(h_in_psum, e * HALVES * KH - (HALVES - 1 - f) * KH)
                src = slots_eo[:, ds(e * HALVES + f, 1), :].rearrange("p a (k n) -> p (a k) n", k=KD)
                v.tensor_copy(sl_r[:, f, 0], src).then_inc(sl_hi, 1)
                dve.wait_ge(sl_hi, n)
                v.tensor_tensor(sl_r[:, f, 1], src, sl_r[:, f, 0].bitcast(F32), ALU.subtract).then_inc(sl_split, 1)

            def rest_of_act(e, i):
                n = e * HALVES * KH + i
                dve.wait_ge(h_hi, n + 1)
                v.tensor_tensor(act_r[:, i % RING, 1, :], act[:, i % 2, :], act_r[:, i % RING, 0, :].bitcast(F32),
                                ALU.subtract).then_inc(h_split, 1)

            def keep_eo(e, f):
                dve.wait_ge(eo_steps, (e * HALVES + f + 1) * KH)
                for c in range(BH // 2):
                    last = v.tensor_tensor(slots_eo[:, ds(e * HALVES + f, 1), c * 2 * D:(c + 1) * 2 * D]
                                           .rearrange("p a (c d) -> p (a c) d", d=D),
                                           bank[4 + 2 * f + c][:, :].rearrange("p (c d) -> p c d", d=D),
                                           b2_bc[:, ds(e, 1), :].to_broadcast([P, 2, D]), ALU.add)
                last.then_inc(eo_ready, 1)

            def expert(e, q, last=False):
                split_slots(e, 1)
                for i in range(HALVES * KH):
                    rest_of_act(e, i)
                    if i == KH + 2:
                        keep_eo(e, 0)
                    if i == 6 and not last:
                        rest_of_weights(e + 1, 1 - q)
                    if i == KH + 3 and not last:
                        split_slots(e + 1, 0)
                keep_eo(e, 1)

            rest_of_weights(0, 0)
            split_slots(0, 0, first=True)
            with dve.Fori(0, E // 2 - 1) as it:
                for q in range(2):
                    expert(2 * it + q, q)
            expert(E - 2, 0)
            expert(E - 1, 1, last=True)
            experts_finished(dve)

            for u in range(2):
                v.memset(eo_r[:, u, 0, :, D:D + 1].bitcast(F32), 1.0)
                v.memset(eo_r[:, u, 0, :, D + 1:DZ].bitcast(F32), 0.0)
                v.memset(eo_r[:, u, 1, :, D:DZ].bitcast(F32), 0.0).then_inc(eo_padded, 1)

            def split_eo(b, u):
                if not (isinstance(b, int) and b < 2):
                    dve.wait_ge(comb_used, (b - 1) * E)
                src = slots_eo[:].rearrange("p (e f) n -> p e (f n)", f=HALVES)[:, :, ds(b * D, D)]
                v.tensor_copy(eo_r[:, u, 0, :, 0:D], src).then_inc(eor_hi, 1)
                dve.wait_ge(eor_hi, b + 1)
                v.tensor_tensor(eo_r[:, u, 1, :, 0:D], src, eo_r[:, u, 0, :, 0:D].bitcast(F32),
                                ALU.subtract).then_inc(eor_split, 1)

            def rest_of_combine(b, u, m):
                dve.wait_ge(comb_hi, b * E + m + 1)
                v.tensor_tensor(comb_r[:, m % RING, 1, :], comb_in[:, u, m, :], comb_r[:, m % RING, 0, :].bitcast(F32),
                                ALU.subtract).then_inc(comb_split, 1)

            def invert_z(b, u):
                dve.wait_ge(comb_used, (b + 1) * E)
                for t in range(NT):
                    last = v.reciprocal(rz_d[:, u, t:t + 1], bank[4 * u + t][:, D:D + 1])
                last.then_inc(z_inv, 1)

            def stats_of_mix(b, u):
                dve.wait_ge(mix_ready, b + 1)
                for t in range(NT):
                    last = v.bn_stats(st_d[:, u, t, :], mix[:, u, t, :])
                last.then_inc(m_stats, 1)
                dve.wait_ge(m_stats, b + 1)
                alone(dve)
                for t in range(NT):
                    last = v.bn_aggr(mv_d[:, u, t, :], st_d[:, u, t, :])
                last.then_inc(m_aggr, 1)

            def norm_mix(b, u):
                dve.wait_ge(m_std, b + 1)
                v.reciprocal(rstd_d[:, u, :], rstd_d[:, u, :]).then_inc(m_rstd, 1)
                dve.wait_ge(m_rstd, b + 1)
                for t in range(NT):
                    last = v.tensor_scalar(mix[:, u, t, :], mix[:, u, t, :], mv_d[:, u, t, 0:1],
                                           rstd_d[:, u, t:t + 1], ALU.subtract, ALU.mult)
                last.then_inc(m_normed, 1)
                dve.wait_ge(m_normed, b + 1)
                dve.wait_ge(x2d_loaded[u], 16 * (b // 2 + 1))
                v.tensor_tensor(mix[:, u], mix[:, u], x2_d[:, u], ALU.add).then_inc(out_ready, 1)

            def combine(b, u, first=False, last=False):
                for m in range(E):
                    rest_of_combine(b, u, m)
                    if m == 1 and not first:
                        invert_z(b - 1, 1 - u)
                    if m == 4 and not first:
                        stats_of_mix(b - 1, 1 - u)
                    if m == 5 and not last:
                        split_eo(b + 1, 1 - u)
                    if m == 7 and not first:
                        norm_mix(b - 1, 1 - u)

            split_eo(0, 0)
            combine(0, 0, first=True)
            with dve.Fori(0, PAIRS - 1) as it:
                combine(2 * it + 1, 1)
                combine(2 * it + 2, 0)
            combine(B - 1, 1, last=True)
            for step in (invert_z, stats_of_mix, norm_mix):
                step(B - 1, 1)


def kernel(L0_attn_x, L0_attn_w_qkv, L0_attn_w_out, L0_attn_b_out, L0_attn_norm_g, L0_attn_norm_b,
           L0_ffn_norm_gamma, L0_ffn_slot_norm_gamma, L0_ffn_slot_embeds, L0_ffn_w1, L0_ffn_b1, L0_ffn_w2,
           L0_ffn_b2):
    import numpy as np
    import concourse.bacc as bacc
    from concourse.bass_utils import run_bass_kernel_spmd

    P = 128
    x = np.asarray(L0_attn_x)
    D = x.shape[2]
    heads = np.asarray(L0_attn_norm_g).size
    per_head = D // heads

    def by_row(a, rows):
        return np.ascontiguousarray(np.asarray(a).reshape(rows, P).T)

    head_of = np.arange(P) // per_head
    arrays = {
        "x": np.ascontiguousarray(x),
        "wqkv_t": np.ascontiguousarray(np.asarray(L0_attn_w_qkv).T),
        "wout_t": np.ascontiguousarray(np.asarray(L0_attn_w_out).T),
        "bout": np.ascontiguousarray(np.asarray(L0_attn_b_out).reshape(1, D)),
        "norm_g": by_row(np.repeat(np.asarray(L0_attn_norm_g).ravel(), per_head), D // P),
        "norm_b": by_row(np.repeat(np.asarray(L0_attn_norm_b).ravel(), per_head), D // P),
        "gamma": by_row(L0_ffn_norm_gamma, D // P),
        "slot_gamma": by_row(L0_ffn_slot_norm_gamma, D // P),
        "slots_in": np.ascontiguousarray(np.asarray(L0_ffn_slot_embeds)),
        "w1": np.ascontiguousarray(np.asarray(L0_ffn_w1)),
        "b1": by_row(L0_ffn_b1, np.asarray(L0_ffn_b1).size // P),
        "w2": np.ascontiguousarray(np.asarray(L0_ffn_w2)),
        "b2": np.ascontiguousarray(np.asarray(L0_ffn_b2)[None]),
        "identity": np.eye(P, dtype=np.float32),
        "head_mask": (head_of[:, None] == head_of[None, :]).astype(np.float32),
    }
    nc = bacc.Bacc("TRN2", target_bir_lowering=False, num_devices=1)
    args = {k: nc.dram_tensor(f"in_{k}", a.shape, mybir.dt.from_np(a.dtype), kind="ExternalInput").ap()
            for k, a in arrays.items()}
    out = nc.dram_tensor("out_0", x.shape, F32, kind="ExternalOutput").ap()
    attention_then_soft_moe(nc, **args, out=out)
    r = run_bass_kernel_spmd(nc, [{f"in_{k}": a for k, a in arrays.items()}], core_ids=[0])
    return r.results[0]["out_0"]
```

```python
from contextlib import ExitStack

import concourse.bass as bass
from concourse import mybir
from concourse.bass import ds

F32 = mybir.dt.float32
F32R = mybir.dt.float32r
ALU = mybir.AluOpType
ACT = mybir.ActivationFunctionType
AX = mybir.AxisListType


def attention_then_soft_moe(nc, x, wqkv_t, wout_t, bout, norm_g, norm_b, gamma, slot_gamma,
                            slots_in, w1, b1, w2, b2, identity, head_mask, head_pick, out):
    P = 128
    B, N, D = x.shape
    E, _, HID = w1.shape
    S = slots_in.shape[1]
    NT = N // P
    KD = D // P
    KH = HID // P
    HALVES = 2
    EH = E // HALVES
    BH = B // HALVES
    HALF = BH * S
    DZ = D + 2
    HPT = head_pick.shape[1]
    RING = 4
    XRING = 4
    LN_EPS = 1e-5
    NORM_EPS = 1e-12
    ROOT_D = float(D) ** 0.5
    PASSES = [(0, 0), (0, 1), (1, 0)]
    assert S == P and N == 512 and D == 256 and B == 8 and E == 8 and HALF == 512

    x2_dram = nc.dram_tensor("x2_scratch", [B, N, D], F32, kind="Internal").ap()
    comb_dram = nc.dram_tensor("combine_scratch", [B, E, P, N], F32, kind="Internal").ap()

    def token_tiles(ap):
        return ap.rearrange("b (t p) d -> p (b t) d", p=P)

    x_v, x2_v, out_v = token_tiles(x), token_tiles(x2_dram), token_tiles(out)
    comb_v = comb_dram.rearrange("b e p n -> p (b e) n")
    w1_v = w1.rearrange("e (k p) h -> p (e k) h", p=P)
    w2_v = w2.rearrange("e (k p) d -> p (e k) d", p=P)

    with ExitStack() as ctx:
        def sem(name):
            return ctx.enter_context(nc.semaphore(name))

        def sb_in(scope):
            return lambda name, shape, dt=F32: scope.enter_context(nc.sbuf_tensor(name, shape, dt))

        sb = sb_in(ctx)
        slots_eo = sb("slots_eo", [P, E * HALVES, KD * HALF])
        ident = sb("ident", [P, P])
        ones_r = sb("ones_r", [P, P], F32R)
        ones_f = sb("ones_f", [P, P])
        eps_ln = sb("eps_ln", [P, 1])
        zero_col = sb("zero_col", [P, 1])
        gam = sb("gam", [P, KD])
        sgam = sb("sgam", [P, KD])
        both_gam = sb("both_gam", [P, KD])
        b1_sb = sb("b1_sb", [P, E * KH])
        b2_bc = sb("b2_bc", [P, E, D])
        snT = sb("snT", [P, 2, KD, E * S], F32R)

        sc_y = sb("sc_y", [P, B * NT])
        mv_x2 = sb("mv_x2", [P, B * NT, 2])
        stage = sb("stage", [P, E * N])
        w1_raw = stage[:, 0:KD * HID].rearrange("p (k h) -> p k h", k=KD)
        w2_raw = stage[:, KD * HID:].rearrange("p (k d) -> p k d", k=KH)

        with ExitStack() as scope:
            sb = sb_in(scope)
            wqkvT = sb("wqkvT", [P, KD, 3 * D])
            wqkv_r = sb("wqkv_r", [P, 2, KD, 3 * D], F32R)
            woutT = sb("woutT", [P, KD, D])
            wout_r = sb("wout_r", [P, 2, KD, D], F32R)
            bout_bc = sb("bout_bc", [P, D])
            g_col = sb("g_col", [P, KD])
            b_col = sb("b_col", [P, KD])
            mask = sb("mask", [P, P])
            head_sel = sb("head_sel", [P, HPT])
            xin = slots_eo[:, 0:XRING * NT * D // (KD * HALF), :].rearrange("p a (t d) -> p (a t) d", d=D)
            se = slots_eo[:, 8:8 + E * D // (KD * HALF), :].rearrange("p a (t d) -> p (a t) d", d=D)
            se_sq = sb("se_sq", [P, D])
            se_sum = sb("se_sum", [P, E])
            se_scale = sb("se_scale", [P, E])
            st = sb("st", [P, NT, 6])
            mv = sb("mv", [P, NT, 2])
            rstd = sb("rstd", [P, NT])
            xn = sb("xn", [P, NT, D])
            xn_r = sb("xn_r", [P, 2, NT, D], F32R)
            xnT_r = sb("xnT_r", [P, 2, KD, N], F32R)
            xsum = sb("xsum", [P, KD])
            gram_r = sb("gram_r", [P, 2, KD, D], F32R)
            cw = sb("cw", [P, KD, 2 * D])
            heads = sb("heads", [P, KD, 2, P])
            vb = sb("vb", [P, 2, KD])
            qT = sb("qT", [P, KD, N])
            qGq = sb("qGq", [P, KD, N])
            nrm = sb("nrm", [P, NT * KD * HPT])
            o_tok = sb("o_tok", [P, NT, D])
            oT_r = sb("oT_r", [P, 2, KD, N], F32R)
            proj = sb("proj", [P, NT, D])
            st2 = sb("st2", [P, NT, 6])
            mv2 = sb("mv2", [P, NT, 2])
            rstd2 = sb("rstd2", [P, NT])
            st3 = sb("st3", [P, NT, 6])
            mv3 = sb("mv3", [P, NT, 2])

        with ExitStack() as scope:
            sb = sb_in(scope)
            x2 = sb("x2", [P, NT, D])
            y = sb("y", [P, NT, D])
            y_r = sb("y_r", [P, 2, NT, D], F32R)
            yT_r = sb("yT_r", [P, 2, KD, N], F32R)
            roots = sb("roots", [P, 2, B * NT])
            sc_parts = sb("sc_parts", [P, 2, B * NT])
            neg_lt = sb("neg_lt", [P, E, N])
            neg_max = sb("neg_max", [P, E])
            z_disp = sb("z_disp", [P, E])
            rz_disp = sb("rz_disp", [P, E])
            disp = sb("disp", [P, RING, N])
            disp_r = sb("disp_r", [P, 2, HALVES, NT, EH * S], F32R)
            run_min = sb("run_min", [P, N])
            tok_min = sb("tok_min", [P, NT])
            diag = sb("diag", [P, NT, P], F32R)
            comb = sb("comb", [P, RING, N])

        with ExitStack() as scope:
            sb = sb_in(scope)
            w1_r = sb("w1_r", [P, 2, 2, KD, HID], F32R)
            w2_r = sb("w2_r", [P, 2, 2, KH, D], F32R)
            sl_r = sb("sl_r", [P, HALVES, 2, KD, HALF], F32R)
            act = sb("act", [P, 2, HALF])
            act_r = sb("act_r", [P, RING, 2, HALF], F32R)

        with ExitStack() as scope:
            sb = sb_in(scope)
            comb_odd = sb("comb_odd", [P, E * N])
            comb_in = [a[:, :].rearrange("p (e n) -> p e n", e=E) for a in (stage, comb_odd)]
            comb_r = sb("comb_r", [P, RING, 2, N], F32R)
            eo_r = sb("eo_r", [P, 2, 2, E, DZ], F32R)
            x2_d = sb("x2_d", [P, 2, NT, D])
            mix = sb("mix", [P, 2, NT, D])
            rz_d = sb("rz_d", [P, 2, NT])
            st_d = sb("st_d", [P, 2, NT, 6])
            mv_d = sb("mv_d", [P, 2, NT, 2])
            rstd_d = sb("rstd_d", [P, 2, NT])

        bank = [ctx.enter_context(nc.psum_tensor(f"bank{i}", [P, 512], F32)) for i in range(8)]

        consts_loaded = sem("consts_loaded")
        ident_loaded = sem("ident_loaded")
        se_loaded = sem("se_loaded")
        weights_loaded = sem("weights_loaded")
        x_loaded = sem("x_loaded")
        x2_stored = sem("x2_stored")
        x2_loaded = sem("x2_loaded")
        comb_stored = [sem(f"comb_stored{r}") for r in range(RING)]
        w_loaded = sem("w_loaded")
        comb_loaded = [sem(f"comb_loaded{u}") for u in range(2)]
        x2d_loaded = [sem(f"x2d_loaded{u}") for u in range(2)]
        out_stored = [sem(f"out_stored{u}") for u in range(2)]
        consts_set = sem("consts_set")
        se_squared = sem("se_squared")
        se_rooted = sem("se_rooted")
        se_step = sem("se_step")
        se_normed = sem("se_normed")
        seT_in_psum = sem("seT_in_psum")
        snT_hi = sem("snT_hi")
        snT_ready = sem("snT_ready")
        attn_w_hi = sem("attn_w_hi")
        attn_w_split = sem("attn_w_split")
        x_stats = sem("x_stats")
        x_aggr = sem("x_aggr")
        x_std = sem("x_std")
        x_rstd = sem("x_rstd")
        xn_ready = sem("xn_ready")
        xn_hi = sem("xn_hi")
        xn_split = sem("xn_split")
        xnT_in_psum = sem("xnT_in_psum")
        xnT_hi = sem("xnT_hi")
        xnT_split = sem("xnT_split")
        gram_in_psum = sem("gram_in_psum")
        gram_hi = sem("gram_hi")
        gram_split = sem("gram_split")
        cw_in_psum = sem("cw_in_psum")
        cw_ready = sem("cw_ready")
        heads_in_psum = sem("heads_in_psum")
        heads_ready = sem("heads_ready")
        qT_in_psum = sem("qT_in_psum")
        qT_ready = sem("qT_ready")
        gq_in_psum = sem("gq_in_psum")
        qGq_ready = sem("qGq_ready")
        o_in_psum = sem("o_in_psum")
        norm_in_psum = sem("norm_in_psum")
        norm_clamped = sem("norm_clamped")
        norm_rooted = sem("norm_rooted")
        norm_inverted = sem("norm_inverted")
        o_scaled = sem("o_scaled")
        oT_in_psum = sem("oT_in_psum")
        oT_hi = sem("oT_hi")
        oT_split = sem("oT_split")
        proj_in_psum = sem("proj_in_psum")
        proj_ready = sem("proj_ready")
        p_stats = sem("p_stats")
        p_aggr = sem("p_aggr")
        p_std = sem("p_std")
        p_rstd = sem("p_rstd")
        p_normed = sem("p_normed")
        x2_ready = sem("x2_ready")
        x2_stats = sem("x2_stats")
        x2_aggr = sem("x2_aggr")
        x2_kept = sem("x2_kept")
        y_rooted = sem("y_rooted")
        y_step = sem("y_step")
        y_scaled = sem("y_scaled")
        y_ready = sem("y_ready")
        y_hi = sem("y_hi")
        y_split = sem("y_split")
        yT_in_psum = sem("yT_in_psum")
        yT_hi = sem("yT_hi")
        yT_ready = sem("yT_ready")
        logits_in_psum = sem("logits_in_psum")
        logits_kept = sem("logits_kept")
        disp_exp = sem("disp_exp")
        disp_inv = sem("disp_inv")
        disp_normed = sem("disp_normed")
        dispT_in_psum = sem("dispT_in_psum")
        disp_hi = sem("disp_hi")
        disp_split = sem("disp_split")
        slots_in_psum = sem("slots_in_psum")
        slots_ready = sem("slots_ready")
        run_min_step = sem("run_min_step")
        min_in_psum = sem("min_in_psum")
        tok_min_ready = sem("tok_min_ready")
        diag_ready = sem("diag_ready")
        shift_in_psum = sem("shift_in_psum")
        comb_shifted = sem("comb_shifted")
        comb_exp = sem("comb_exp")
        w_hi = sem("w_hi")
        w_split = sem("w_split")
        sl_hi = sem("sl_hi")
        sl_split = sem("sl_split")
        h_in_psum = sem("h_in_psum")
        h_act = sem("h_act")
        h_hi = sem("h_hi")
        h_split = sem("h_split")
        eo_steps = sem("eo_steps")
        eo_ready = sem("eo_ready")
        eo_padded = sem("eo_padded")
        eor_hi = sem("eor_hi")
        eor_split = sem("eor_split")
        comb_hi = sem("comb_hi")
        comb_split = sem("comb_split")
        comb_used = sem("comb_used")
        z_inv = sem("z_inv")
        mix_ready = sem("mix_ready")
        m_stats = sem("m_stats")
        m_aggr = sem("m_aggr")
        m_std = sem("m_std")
        m_rstd = sem("m_rstd")
        m_normed = sem("m_normed")
        out_ready = sem("out_ready")

        N_CONSTS = 9
        N_WEIGHTS = 2
        PAIRS = B // 2

        def attention_finished(eng):
            eng.wait_ge(x2_kept, B)
            eng.wait_ge(x2_stored, 16 * B)
            eng.wait_ge(snT_ready, KD * HALVES)

        def weights_finished(eng):
            eng.wait_ge(slots_ready, B * HALVES)
            eng.wait_ge(comb_exp, B * E)
            for r in range(RING):
                eng.wait_ge(comb_stored[r], 16 * B * E // RING)

        def experts_finished(eng):
            eng.wait_ge(eo_steps, E * HALVES * KH)
            eng.wait_ge(eo_ready, E * HALVES)

        def alone(eng):
            eng.nop(nofuse=True)

        block = ctx.enter_context(nc.Block())

        @block.sync
        def _(sp):
            def load_x(b):
                sp.dma_start(xin[:, ds((b % XRING) * NT, NT), :], x_v[:, ds(b * NT, NT), :]).then_inc(x_loaded, 16)

            load_x(0)
            sp.dma_start(ident[:], identity).then_inc(ident_loaded, 16)
            sp.dma_start(wqkvT[:], wqkv_t.rearrange("(k p) o -> p k o", p=P)).then_inc(weights_loaded, 16)
            sp.wait_ge(x_loaded, 16)
            load_x(1)
            sp.dma_start(woutT[:], wout_t.rearrange("(k p) o -> p k o", p=P)).then_inc(weights_loaded, 16)
            sp.dma_start(mask[:], head_mask).then_inc(consts_loaded, 16)
            sp.dma_start(head_sel[:], head_pick).then_inc(consts_loaded, 16)
            sp.dma_start(g_col[:], norm_g).then_inc(consts_loaded, 16)
            sp.dma_start(b_col[:], norm_b).then_inc(consts_loaded, 16)
            sp.dma_start(bout_bc[:], bout.to_broadcast([P, D])).then_inc(consts_loaded, 16)
            sp.dma_start(gam[:], gamma).then_inc(consts_loaded, 16)
            sp.dma_start(sgam[:], slot_gamma).then_inc(consts_loaded, 16)
            sp.dma_start(se, slots_in.rearrange("e s d -> s e d")).then_inc(se_loaded, 16)
            sp.dma_start(b1_sb[:], b1).then_inc(consts_loaded, 16)
            sp.dma_start(b2_bc[:], b2.to_broadcast([P, E, D])).then_inc(consts_loaded, 16)

            def store_x2(b):
                sp.wait_ge(x2_ready, b + 1)
                sp.dma_start(x2_v[:, ds(b * NT, NT), :], proj[:]).then_inc(x2_stored, 16)

            for b in (2, 3):
                sp.wait_ge(x_loaded, 16 * b)
                load_x(b)
            with sp.Fori(4, B) as b:
                sp.wait_ge(x_loaded, 16 * b)
                alone(sp)
                store_x2(b - 4)
                load_x(b)
            with sp.Fori(B - 4, B) as b:
                store_x2(b)
            attention_finished(sp)

            def load_weights(e):
                sp.dma_start(w1_raw, w1_v[:, ds(e * KD, KD), :]).then_inc(w_loaded, 16)
                sp.dma_start(w2_raw, w2_v[:, ds(e * KH, KH), :]).then_inc(w_loaded, 16)

            def load_x2(b):
                sp.dma_start(x2[:], x2_v[:, ds(b * NT, NT), :]).then_inc(x2_loaded, 16)

            def store_combine(b, m):
                sp.wait_ge(comb_exp, b * E + m + 1)
                sp.dma_start(comb_v[:, ds(b * E + m, 1), :], comb[:, m % RING:m % RING + 1, :])\
                    .then_inc(comb_stored[m % RING], 16)

            load_x2(0)
            sp.wait_ge(y_ready, 1)
            load_x2(1)
            load_weights(0)
            with sp.Fori(1, B - 1) as b:
                sp.wait_ge(y_ready, b + 1)
                load_x2(b + 1)
                for m in range(E):
                    store_combine(b - 1, m)
            for b in (B - 2, B - 1):
                for m in range(E):
                    store_combine(b, m)
            weights_finished(sp)

            with sp.Fori(1, E) as e:
                sp.wait_ge(w_split, 2 * e)
                load_weights(e)
            sp.wait_ge(w_split, 2 * E)

            def load_combine(b, u):
                sp.dma_start(comb_in[u], comb_v[:, ds(b * E, E), :]).then_inc(comb_loaded[u], 16)

            def load_residual(b, u):
                sp.dma_start(x2_d[:, u], x2_v[:, ds(b * NT, NT), :]).then_inc(x2d_loaded[u], 16)

            def store_out(b, u):
                sp.wait_ge(out_ready, b + 1)
                sp.dma_start(out_v[:, ds(b * NT, NT), :], mix[:, u]).then_inc(out_stored[u], 16)

            load_combine(0, 0)
            experts_finished(sp)
            load_combine(1, 1)
            for u in range(2):
                load_residual(u, u)
            with sp.Fori(0, PAIRS - 1) as it:
                for u in range(2):
                    sp.wait_ge(comb_split, (2 * it + u + 1) * E)
                    load_combine(2 * it + u + 2, u)
                    store_out(2 * it + u, u)
                    load_residual(2 * it + u + 2, u)
            for u in range(2):
                store_out(B - 2 + u, u)
            for u in range(2):
                sp.wait_ge(out_stored[u], 16 * PAIRS)
            sp.wait_ge(x2_stored, 16 * B)
            for r in range(RING):
                sp.wait_ge(comb_stored[r], 16 * B * E // RING)

        @block.gpsimd
        def _(pool):
            attention_finished(pool)

            def normalise_dispatch(b, m):
                pool.wait_ge(disp_inv, b * E + m + 1)
                alone(pool)
                nc.gpsimd.tensor_scalar(disp[:, m % RING, :], disp[:, m % RING, :], rz_disp[:, m:m + 1], 1.0,
                                        ALU.mult, ALU.mult).then_inc(disp_normed, 1)

            def rest_of_y(b, first=False):
                pool.wait_ge(y_hi, b + 1)
                if not first:
                    pool.wait_ge(slots_in_psum, b * HALVES)
                alone(pool)
                nc.gpsimd.tensor_tensor(y_r[:, 1], y[:], y_r[:, 0].bitcast(F32), ALU.subtract).then_inc(y_split, 1)

            def weights_of(b, first=False):
                for m in range(E):
                    if m == E - 2:
                        rest_of_y(b, first)
                    normalise_dispatch(b, m)

            weights_of(0, first=True)
            with pool.Fori(1, B) as b:
                weights_of(b)

        @block.tensor
        def _(pe):
            pe.wait_ge(ident_loaded, 16)

            def transpose_xn(b, first):
                pe.wait_ge(xn_ready, b + 1)
                if not first:
                    pe.wait_ge(cw_ready, b)
                for k in range(KD):
                    for t in range(NT):
                        last = pe.transpose(bank[k][:, t * P:(t + 1) * P], xn[:, t, k * P:(k + 1) * P], ident[:])
                last.then_inc(xnT_in_psum, 1)

            def gram_of_x(b, first):
                pe.wait_ge(xn_split, b + 1)
                if not first:
                    pe.wait_ge(heads_ready, b)
                steps = [(t, i, j) for t in range(NT) for i, j in PASSES]
                for m in range(KD):
                    for n, (t, i, j) in enumerate(steps):
                        last = pe.matmul(bank[2][:, m * D:(m + 1) * D], xn_r[:, i, t, m * P:(m + 1) * P],
                                         xn_r[:, j, t, :], start=(n == 0), stop=(n == len(steps) - 1))
                last.then_inc(gram_in_psum, 1)

            def gram_times_kv(b):
                pe.wait_ge(gram_split, b + 1)
                pe.wait_ge(attn_w_split, 1)
                pe.wait_ge(qT_ready, b + 1)
                steps = [(k, i, j) for k in range(KD) for i, j in PASSES]
                for m in range(KD):
                    for n, (k, i, j) in enumerate(steps):
                        last = pe.matmul(bank[m][:, :], gram_r[:, i, k, m * P:(m + 1) * P],
                                         wqkv_r[:, j, k, D:3 * D], start=(n == 0), stop=(n == len(steps) - 1))
                last.then_inc(cw_in_psum, 1)

            def head_products(b):
                pe.wait_ge(cw_ready, b + 1)
                for h in range(KD):
                    for k in range(KD):
                        both = cw[:, k, :].rearrange("p (a c) -> p a c", a=2)[:, :, h * P:(h + 1) * P]
                        pe.matmul(bank[2][:, h * D:(h + 1) * D].rearrange("p (a c) -> p a c", a=2),
                                  wqkvT[:, k, D + h * P:D + (h + 1) * P], both, start=(k == 0), stop=(k == KD - 1))
                for h in range(KD):
                    for k in range(KD):
                        last = pe.matmul(bank[3][:, h:h + 1],
                                         wqkvT[:, k, 2 * D + h * P:2 * D + (h + 1) * P], xsum[:, k:k + 1],
                                         start=(k == 0), stop=(k == KD - 1))
                last.then_inc(heads_in_psum, 1)

            def queries(b):
                pe.wait_ge(xnT_split, b + 1)
                pe.wait_ge(attn_w_split, 1)
                steps = [(k, i, j) for k in range(KD) for i, j in PASSES]
                for h in range(KD):
                    for n, (k, i, j) in enumerate(steps):
                        last = pe.matmul(bank[h][:, :], wqkv_r[:, i, k, h * P:(h + 1) * P], xnT_r[:, j, k, :],
                                         start=(n == 0), stop=(n == len(steps) - 1))
                last.then_inc(qT_in_psum, 1)

            def gram_times_q(b, first):
                pe.wait_ge(heads_ready, b + 1)
                if first:
                    pe.wait_ge(snT_ready, KD * HALVES)
                else:
                    pe.wait_ge(oT_split, b)
                for h in range(KD):
                    last = pe.matmul(bank[4 + h][:, :], heads[:, h, 0, :], qT[:, h, :], start=True, stop=True)
                last.then_inc(gq_in_psum, 1)

            def outputs(b, first):
                if not first:
                    pe.wait_ge(proj_ready, b)
                for t in range(NT):
                    for h in range(KD):
                        at = (t % 2) * D + h * P
                        last = pe.matmul(bank[6 + t // 2][:, at:at + P], qT[:, h, t * P:(t + 1) * P],
                                         heads[:, h, 1, :], start=True, stop=True)
                last.then_inc(o_in_psum, 1)

            def norms(b):
                pe.wait_ge(qGq_ready, b + 1)
                for t in range(NT):
                    for h in range(KD):
                        at = (t * KD + h) * HPT
                        last = pe.matmul(bank[3][:, at:at + HPT], qGq[:, h, t * P:(t + 1) * P], head_sel[:],
                                         start=True, stop=True)
                last.then_inc(norm_in_psum, 1)

            def transpose_o(b):
                pe.wait_ge(o_scaled, b + 1)
                for h in range(KD):
                    for t in range(NT):
                        last = pe.transpose(bank[4 + h][:, t * P:(t + 1) * P], o_tok[:, t, h * P:(h + 1) * P], ident[:])
                last.then_inc(oT_in_psum, 1)

            def projection(b):
                pe.wait_ge(oT_split, b + 1)
                steps = [(h, i, j) for h in range(KD) for i, j in PASSES]
                for t in range(NT):
                    for n, (h, i, j) in enumerate(steps):
                        last = pe.matmul(bank[6 + t // 2][:, (t % 2) * D:(t % 2 + 1) * D],
                                         oT_r[:, i, h, t * P:(t + 1) * P], wout_r[:, j, h, :],
                                         start=(n == 0), stop=(n == len(steps) - 1))
                last.then_inc(proj_in_psum, 1)

            def transpose_slots():
                for h in range(HALVES):
                    pe.wait_ge(se_normed, h + 1)
                    for k in range(KD):
                        for e in range(EH):
                            last = pe.transpose(bank[4 + 2 * h + k][:, e * S:(e + 1) * S],
                                                se[:, h * EH + e, k * P:(k + 1) * P], ident[:])
                        last.then_inc(seT_in_psum, 1)

            def attention(b, front=True, back=True, first_back=False):
                if front:
                    transpose_xn(b, not back)
                    gram_of_x(b, not back)
                if back:
                    gram_times_q(b - 1, first_back)
                    outputs(b - 1, first_back)
                if front:
                    queries(b)
                if back:
                    norms(b - 1)
                if front:
                    gram_times_kv(b)
                if back:
                    transpose_o(b - 1)
                if front:
                    head_products(b)
                if back:
                    projection(b - 1)

            attention(0, back=False)
            transpose_slots()
            pe.wait_ge(consts_loaded, 16 * N_CONSTS)
            attention(1, first_back=True)
            with pe.Fori(2, B) as b:
                attention(b)
            attention(B, front=False)
            attention_finished(pe)

            def transpose_y(b, first=False):
                pe.wait_ge(y_ready, b + 1)
                if not first:
                    pe.wait_ge(logits_kept, b * E)
                for k in range(KD):
                    for t in range(NT):
                        last = pe.transpose(bank[k][:, t * P:(t + 1) * P], y[:, t, k * P:(k + 1) * P], ident[:])
                last.then_inc(yT_in_psum, 1)

            def logits(b, m):
                if m == 0:
                    pe.wait_ge(yT_ready, (b + 1) * KD)
                if m >= 2:
                    pe.wait_ge(logits_kept, b * E + m - 1)
                steps = [(k, i, j) for k in range(KD) for i, j in PASSES]
                for n, (k, i, j) in enumerate(steps):
                    last = pe.matmul(bank[m % 2][:, :], snT[:, i, k, m * S:(m + 1) * S], yT_r[:, j, k, :],
                                     start=(n == 0), stop=(n == len(steps) - 1))
                last.then_inc(logits_in_psum, 1)

            def transpose_dispatch(b, m, first=False):
                pe.wait_ge(disp_normed, b * E + m + 1)
                if m >= 2 or not first:
                    pe.wait_ge(disp_split, b * E + m - 1)
                for t in range(NT):
                    last = pe.transpose(bank[2 + m % 2][:, t * S:(t + 1) * S], disp[:, m % RING, t * P:(t + 1) * P],
                                        ident[:])
                last.then_inc(dispT_in_psum, 1)

            slot_steps = [(k, t, i, j) for k in range(KD) for t in range(NT) for i, j in PASSES]
            FILL = len(slot_steps)

            def fill_slots(b, h, begin, end, first=False):
                if begin == 0:
                    pe.wait_ge(disp_split, b * E + (h + 1) * EH)
                    pe.wait_ge(y_split, b + 1)
                    if h > 0 or not first:
                        pe.wait_ge(slots_ready, b * HALVES + h)
                for n in range(begin, end):
                    k, t, i, j = slot_steps[n]
                    last = pe.matmul(bank[4 + k][:, :], y_r[:, i, t, k * P:(k + 1) * P], disp_r[:, j, h, t, :],
                                     start=(n % (FILL // KD) == 0), stop=(n % (FILL // KD) == FILL // KD - 1))
                if end == FILL:
                    last.then_inc(slots_in_psum, 1)

            def transpose_min(b):
                pe.wait_ge(run_min_step, (b + 1) * (E - 1))
                for t in range(NT):
                    last = pe.transpose(bank[6][:, t * P:(t + 1) * P], run_min[:, t * P:(t + 1) * P], ident[:])
                last.then_inc(min_in_psum, 1)

            def spread_shift(b, first=False):
                pe.wait_ge(diag_ready, (b + 1) * NT)
                if not first:
                    pe.wait_ge(comb_shifted, b * E)
                pe.matmul(bank[7][:, :], ones_r[:], diag[:].rearrange("p t n -> p (t n)"), start=True, stop=True)\
                    .then_inc(shift_in_psum, 1)

            FILL_AT = [0, 0, 5, 10, 15, 20, FILL]
            QUARTER = FILL // 4

            def weights_of(b, first=False, last=False):
                for m in range(E):
                    logits(b, m)
                    if m >= 2:
                        transpose_dispatch(b, m - 2, first)
                    if not first and 1 <= m <= 5:
                        fill_slots(b - 1, 1, FILL_AT[m], FILL_AT[m + 1])
                fill_slots(b, 0, 0, QUARTER, first)
                if not last:
                    transpose_y(b + 1)
                transpose_min(b)
                fill_slots(b, 0, QUARTER, 2 * QUARTER)
                transpose_dispatch(b, 6, first)
                fill_slots(b, 0, 2 * QUARTER, 3 * QUARTER)
                transpose_dispatch(b, 7, first)
                spread_shift(b, first)
                fill_slots(b, 0, 3 * QUARTER, FILL)

            transpose_y(0, first=True)
            weights_of(0, first=True)
            with pe.Fori(1, B - 1) as b:
                weights_of(b)
            weights_of(B - 1, last=True)
            fill_slots(B - 1, 1, 0, FILL)
            weights_finished(pe)

            def hidden(e, q, i, first):
                f, j = divmod(i, KH)
                if i == 0:
                    pe.wait_ge(w_split, 2 * (e + 1))
                if j == 0:
                    pe.wait_ge(sl_split, e * HALVES + f + 1)
                if i >= RING or not first:
                    pe.wait_ge(h_act, e * HALVES * KH + i - RING + 1)
                steps = [(k, a, c) for k in range(KD) for a, c in PASSES]
                for n, (k, a, c) in enumerate(steps):
                    last = pe.matmul(bank[i % RING][:, :], w1_r[:, q, a, k, j * P:(j + 1) * P], sl_r[:, f, c, k, :],
                                     start=(n == 0), stop=(n == len(steps) - 1))
                last.then_inc(h_in_psum, 1)

            def expert_out(e, q, i, first=False):
                f, j = divmod(i, KH)
                pe.wait_ge(h_split, e * HALVES * KH + i + 1)
                if j == 0 and not first:
                    pe.wait_ge(eo_ready, (e - 1) * HALVES + f + 1)
                for c in range(BH):
                    for n, (a, w) in enumerate(PASSES):
                        last = pe.matmul(bank[4 + 2 * f + c // 2][:, (c % 2) * D:(c % 2 + 1) * D],
                                         act_r[:, i % RING, a, c * S:(c + 1) * S], w2_r[:, q, w, j, :],
                                         start=(j == 0 and n == 0 and c % 2 == 0), stop=(j == KH - 1 and n == 2),
                                         skip_group_check=True)
                last.then_inc(eo_steps, 1)

            def expert(e, q, first=False):
                for i in range(HALVES * KH):
                    hidden(e, q, i, first)
                    if i >= 2:
                        expert_out(e, q, i - 2, first)
                    elif not first:
                        expert_out(e - 1, 1 - q, HALVES * KH - 2 + i)

            expert(0, 0, first=True)
            with pe.Fori(0, E // 2 - 1) as it:
                expert(2 * it + 1, 1)
                expert(2 * it + 2, 0)
            expert(E - 1, 1)
            for i in range(2):
                expert_out(E - 1, 1, HALVES * KH - 2 + i)
            experts_finished(pe)

            def combine(b, u):
                pe.wait_ge(eor_split, b + 1)
                if not (isinstance(b, int) and b < 2):
                    pe.wait_ge(mix_ready, b - 1)
                for m in range(E):
                    pe.wait_ge(comb_split, b * E + m + 1)
                    for t in range(NT):
                        for n, (i, j) in enumerate(PASSES):
                            last = pe.matmul(bank[4 * u + t][:, 0:DZ], comb_r[:, m % RING, i, t * P:(t + 1) * P],
                                             eo_r[:, u, j, m, :], start=(m == 0 and n == 0),
                                             stop=(m == E - 1 and n == 2))
                    last.then_inc(comb_used, 1)

            pe.wait_ge(eo_padded, 2)
            combine(0, 0)
            combine(1, 1)
            with pe.Fori(1, PAIRS) as it:
                for u in range(2):
                    combine(2 * it + u, u)

        @block.scalar
        def _(sc):
            act_fn = nc.scalar.activation
            def norm_slots():
                sc.wait_ge(se_loaded, 16)
                for e in range(E):
                    if e:
                        sc.wait_ge(se_squared, e)
                    act_fn(se_sq[:], se[:, e, :], ACT.Square, bias=zero_col[:], accum_out=se_sum[:, e:e + 1])\
                        .then_inc(se_squared, 1)
                sc.wait_ge(se_squared, E)
                act_fn(se_scale[:], se_sum[:], ACT.Sqrt, bias=zero_col[:]).then_inc(se_rooted, 1)

            def round_slots():
                sc.wait_ge(se_step, 3)
                for h in range(HALVES):
                    for k in range(KD):
                        sc.wait_ge(seT_in_psum, h * KD + k + 1)
                        act_fn(snT[:, 0, k, h * EH * S:(h + 1) * EH * S], bank[4 + 2 * h + k][:, :], ACT.Copy,
                               scale=both_gam[:, k:k + 1]).then_inc(snT_hi, 1)

            def root_x(b):
                sc.wait_ge(x_aggr, b + 1)
                act_fn(rstd[:], mv[:, :, 1], ACT.Sqrt, bias=eps_ln[:]).then_inc(x_std, 1)

            def round_xn(b, first=False):
                sc.wait_ge(xn_ready, b + 1)
                if not first:
                    sc.wait_ge(gram_in_psum, b)
                act_fn(xn_r[:, 0], xn[:], ACT.Copy).then_inc(xn_hi, 1)

            def round_xnT(b, first):
                sc.wait_ge(xnT_in_psum, b + 1)
                if not first:
                    sc.wait_ge(qT_in_psum, b)
                    sc.wait_ge(heads_in_psum, b)
                for k in range(KD):
                    last = act_fn(xnT_r[:, 0, k, :], bank[k][:, :], ACT.Identity, bias=zero_col[:],
                                  accum_out=xsum[:, k:k + 1])
                last.then_inc(xnT_hi, 1)

            def round_gram(b, first):
                sc.wait_ge(gram_in_psum, b + 1)
                if not first:
                    sc.wait_ge(cw_in_psum, b)
                act_fn(gram_r[:, 0], bank[2][:, :].rearrange("p (k d) -> p k d", k=KD), ACT.Copy)\
                    .then_inc(gram_hi, 1)

            def keep_cw(b, first):
                sc.wait_ge(cw_in_psum, b + 1)
                if not first:
                    sc.wait_ge(heads_in_psum, b)
                for k in range(KD):
                    last = act_fn(cw[:, k, :], bank[k][:, :], ACT.Copy)
                last.then_inc(cw_ready, 1)

            def keep_qT(b, first):
                sc.wait_ge(qT_in_psum, b + 1)
                if not first:
                    sc.wait_ge(o_in_psum, b)
                    sc.wait_ge(qGq_ready, b)
                for h in range(KD):
                    last = act_fn(qT[:, h, :], bank[h][:, :], ACT.Copy)
                last.then_inc(qT_ready, 1)

            def root_norm(b):
                sc.wait_ge(norm_clamped, b + 1)
                act_fn(nrm[:], nrm[:], ACT.Sqrt, bias=zero_col[:]).then_inc(norm_rooted, 1)

            def round_oT(b, first):
                sc.wait_ge(oT_in_psum, b + 1)
                if not first:
                    sc.wait_ge(proj_in_psum, b)
                alone(sc)
                for h in range(KD):
                    last = act_fn(oT_r[:, 0, h, :], bank[4 + h][:, :], ACT.Identity, bias=vb[:, ds(b % 2, 1), h:h + 1]
                                  .rearrange("p a c -> p (a c)"))
                last.then_inc(oT_hi, 1)

            def root_proj(b):
                sc.wait_ge(p_aggr, b + 1)
                act_fn(rstd2[:], mv2[:, :, 1], ACT.Sqrt, bias=eps_ln[:]).then_inc(p_std, 1)

            def attention(b, front=True, following=True, back=True, end=True, first_back=False):
                if front:
                    round_xnT(b, not back)
                if end:
                    root_proj(b - 2)
                if front:
                    round_gram(b, not back)
                    keep_qT(b, not back)
                if back:
                    root_norm(b - 1)
                if front:
                    keep_cw(b, not back)
                if following:
                    root_x(b + 1)
                if back:
                    round_oT(b - 1, first_back)
                if following:
                    round_xn(b + 1)

            sc.wait_ge(consts_set, 1)
            root_x(0)
            round_xn(0, first=True)
            sc.wait_ge(weights_loaded, 16 * N_WEIGHTS)
            act_fn(wqkv_r[:, 0], wqkvT[:], ACT.Copy)
            act_fn(wout_r[:, 0], woutT[:], ACT.Copy).then_inc(attn_w_hi, 1)
            attention(0, back=False, end=False)
            norm_slots()
            round_slots()
            attention(1, end=False, first_back=True)
            with sc.Fori(2, B - 1) as b:
                attention(b)
            attention(B - 1, following=False)
            attention(B, front=False, following=False)
            attention(B + 1, front=False, following=False, back=False)
            attention_finished(sc)

            act_fn(roots[:, 0, :], mv_x2[:, :, 1], ACT.Sqrt, bias=eps_ln[:])
            act_fn(roots[:, 1, :], mv_x2[:, :, 1], ACT.Sqrt, bias=zero_col[:]).then_inc(y_rooted, 1)

            def round_yT(b, first=False):
                sc.wait_ge(yT_in_psum, b + 1)
                if not first:
                    sc.wait_ge(logits_in_psum, b * E)
                for k in range(KD):
                    act_fn(yT_r[:, 0, k, :], bank[k][:, :], ACT.Copy).then_inc(yT_hi, 1)

            def round_y(b, first=False):
                sc.wait_ge(y_ready, b + 1)
                if not first:
                    sc.wait_ge(slots_in_psum, b * HALVES)
                act_fn(y_r[:, 0], y[:], ACT.Copy).then_inc(y_hi, 1)

            def exp_dispatch(b, m, first):
                sc.wait_ge(logits_kept, b * E + m + 1)
                if m >= RING or not first:
                    sc.wait_ge(dispT_in_psum, b * E + m - RING + 1)
                act_fn(disp[:, m % RING, :], neg_lt[:, m, :], ACT.Exp, bias=neg_max[:, m:m + 1], scale=-1.0,
                       accum_out=z_disp[:, m:m + 1]).then_inc(disp_exp, 1)

            def round_dispatch(b, m, first):
                sc.wait_ge(dispT_in_psum, b * E + m + 1)
                h = m // EH
                if m % EH == 0 and not first:
                    sc.wait_ge(slots_in_psum, (b - 1) * HALVES + h + 1)
                act_fn(disp_r[:, 0, h, :, (m % EH) * S:(m % EH + 1) * S],
                       bank[2 + m % 2][:, :].rearrange("p (t s) -> p t s", t=NT), ACT.Copy).then_inc(disp_hi, 1)

            def keep_slots(b, h):
                sc.wait_ge(slots_in_psum, b * HALVES + h + 1)
                alone(sc)
                for k in range(KD):
                    dst = slots_eo[:, h * EH * HALVES:(h + 1) * EH * HALVES, :].rearrange(
                        "p (e f) n -> p e (f n)", f=HALVES)
                    at = b * S + b // BH * (KD * HALF - BH * S) + k * HALF
                    last = act_fn(dst[:, :, ds(at, S)],
                                  bank[4 + k][:, :].rearrange("p (e s) -> p e s", e=EH), ACT.Copy,
                                  scale=gam[:, k:k + 1])
                last.then_inc(slots_ready, 1)

            def exp_combine(b, m):
                sc.wait_ge(comb_shifted, b * E + m + 1)
                act_fn(comb[:, m % RING, :], comb[:, m % RING, :], ACT.Exp, bias=zero_col[:], scale=-1.0)\
                    .then_inc(comb_exp, 1)

            def weights_of(b, first=False, last=False):
                for m in range(E):
                    exp_dispatch(b, m, first)
                    if m == 1 and not first:
                        keep_slots(b - 1, 0)
                    if m >= 2:
                        round_dispatch(b, m - 2, first)
                    if not first:
                        exp_combine(b - 1, m)
                    if m == 5 and not first:
                        keep_slots(b - 1, 1)
                    if m == 5:
                        round_y(b, first)
                if not last:
                    round_yT(b + 1)
                round_dispatch(b, 6, first)
                round_dispatch(b, 7, first)

            round_yT(0, first=True)
            weights_of(0, first=True)
            with sc.Fori(1, B - 1) as b:
                weights_of(b)
            weights_of(B - 1, last=True)
            keep_slots(B - 1, 0)
            for m in range(E):
                exp_combine(B - 1, m)
            keep_slots(B - 1, 1)
            weights_finished(sc)

            def round_weights(e, q):
                sc.wait_ge(w_loaded, 32 * (e + 1))
                act_fn(w1_r[:, q, 0], w1_raw, ACT.Copy).then_inc(w_hi, 1)
                act_fn(w2_r[:, q, 0], w2_raw, ACT.Copy).then_inc(w_hi, 1)

            def activate(e, i, first):
                n = e * HALVES * KH + i
                sc.wait_ge(h_in_psum, n + 1)
                if i >= 2 or not first:
                    sc.wait_ge(h_split, n - 1)
                alone(sc)
                act_fn(act[:, i % 2, :], bank[i % RING][:, :], ACT.Gelu, bias=b1_sb[:, ds(e * KH + i % KH, 1)])\
                    .then_inc(h_act, 1)
                sc.wait_ge(h_act, n + 1)
                if i >= RING or not first:
                    sc.wait_ge(eo_steps, n - RING + 1)
                act_fn(act_r[:, i % RING, 0, :], act[:, i % 2, :], ACT.Copy).then_inc(h_hi, 1)

            def expert(e, q, first=False, last=False):
                for i in range(HALVES * KH):
                    activate(e, i, first)
                    if i == 6 and not last:
                        if not first:
                            sc.wait_ge(eo_steps, e * HALVES * KH)
                        round_weights(e + 1, 1 - q)

            round_weights(0, 0)
            expert(0, 0, first=True)
            with sc.Fori(0, E // 2 - 1) as it:
                expert(2 * it + 1, 1)
                expert(2 * it + 2, 0)
            expert(E - 1, 1, last=True)
            experts_finished(sc)

            def round_combine(b, u, m, first=False):
                if m == 0:
                    sc.wait_ge(comb_loaded[u], 16 * (b // 2 + 1))
                if m >= RING or not first:
                    sc.wait_ge(comb_used, b * E + m - RING + 1)
                act_fn(comb_r[:, m % RING, 0, :], comb_in[u][:, m, :], ACT.Copy).then_inc(comb_hi, 1)

            def keep_mix(b, u):
                sc.wait_ge(z_inv, b + 1)
                if not (isinstance(b, int) and b < 2):
                    sc.wait_ge(out_stored[u], 16 * (b // 2))
                for t in range(NT):
                    last = act_fn(mix[:, u, t, :], bank[4 * u + t][:, 0:D], ACT.Copy, scale=rz_d[:, u, t:t + 1])
                last.then_inc(mix_ready, 1)

            def root_mix(b, u):
                sc.wait_ge(m_aggr, b + 1)
                act_fn(rstd_d[:, u, :], mv_d[:, u, :, 1], ACT.Sqrt, bias=eps_ln[:]).then_inc(m_std, 1)

            def combine(b, u, first=False):
                for m in range(E):
                    round_combine(b, u, m, first)
                    if m == 2 and not first:
                        keep_mix(b - 1, 1 - u)
                    if m == 5 and not first:
                        root_mix(b - 1, 1 - u)

            combine(0, 0, first=True)
            combine(1, 1)
            combine(2, 0)
            with sc.Fori(1, PAIRS - 1) as it:
                combine(2 * it + 1, 1)
                combine(2 * it + 2, 0)
            combine(B - 1, 1)
            keep_mix(B - 1, 1)
            root_mix(B - 1, 1)

        @block.vector
        def _(dve):
            v = nc.vector
            v.memset(eps_ln[:], LN_EPS)
            v.memset(zero_col[:], 0.0)
            v.memset(ones_f[:], 1.0).then_inc(se_step, 1)
            dve.wait_ge(se_step, 1)
            v.tensor_copy(ones_r[:], ones_f[:]).then_inc(consts_set, 1)
            def scale_slots():
                dve.wait_ge(consts_loaded, 16 * N_CONSTS)
                v.tensor_tensor(both_gam[:], gam[:], sgam[:], ALU.mult).then_inc(se_step, 1)
                dve.wait_ge(se_rooted, 1)
                v.tensor_scalar(se_scale[:], se_scale[:], NORM_EPS, 1.0 / ROOT_D, ALU.max, ALU.mult)\
                    .then_inc(se_step, 1)
                dve.wait_ge(se_step, 3)
                v.reciprocal(se_scale[:], se_scale[:]).then_inc(se_step, 1)
                dve.wait_ge(se_step, 4)
                for h in range(HALVES):
                    for e in range(h * EH, (h + 1) * EH):
                        last = v.tensor_scalar(se[:, e, :], se[:, e, :], se_scale[:, e:e + 1], None, ALU.mult)
                    last.then_inc(se_normed, 1)

            def rest_of_slots():
                for h in range(HALVES):
                    for k in range(KD):
                        dve.wait_ge(snT_hi, h * KD + k + 1)
                        cols = slice(h * EH * S, (h + 1) * EH * S)
                        v.scalar_tensor_tensor(out=snT[:, 1, k, cols], in0=bank[4 + 2 * h + k][:, :],
                                               scalar=both_gam[:, k:k + 1], in1=snT[:, 0, k, cols].bitcast(F32),
                                               op0=ALU.mult, op1=ALU.subtract).then_inc(snT_ready, 1)

            def x_rows(b, t, n):
                return xin[:, ds((b % XRING) * NT + t, n), :]

            def stats_of_x(b):
                dve.wait_ge(x_loaded, 16 * (b + 1))
                for t in range(NT):
                    last = v.bn_stats(st[:, t, :], x_rows(b, t, 1))
                last.then_inc(x_stats, 1)
                dve.wait_ge(x_stats, b + 1)
                alone(dve)
                for t in range(NT):
                    last = v.bn_aggr(mv[:, t, :], st[:, t, :])
                last.then_inc(x_aggr, 1)

            def norm_x(b, first=False):
                dve.wait_ge(x_std, b + 1)
                v.reciprocal(rstd[:], rstd[:]).then_inc(x_rstd, 1)
                dve.wait_ge(x_rstd, b + 1)
                if not first:
                    dve.wait_ge(xnT_in_psum, b)
                    dve.wait_ge(xn_split, b)
                for t in range(NT):
                    last = v.tensor_scalar(xn[:, t:t + 1, :], x_rows(b, t, 1), mv[:, t, 0:1], rstd[:, t:t + 1],
                                           ALU.subtract, ALU.mult)
                last.then_inc(xn_ready, 1)
                dve.wait_ge(xn_hi, b + 1)
                v.tensor_tensor(xn_r[:, 1], xn[:], xn_r[:, 0].bitcast(F32), ALU.subtract).then_inc(xn_split, 1)

            def rest_of_xnT(b):
                dve.wait_ge(xnT_hi, b + 1)
                for k in range(KD):
                    last = v.tensor_tensor(xnT_r[:, 1, k, :], bank[k][:, :], xnT_r[:, 0, k, :].bitcast(F32),
                                           ALU.subtract)
                last.then_inc(xnT_split, 1)

            def rest_of_gram(b):
                dve.wait_ge(gram_hi, b + 1)
                v.tensor_tensor(gram_r[:, 1], bank[2][:, :].rearrange("p (k d) -> p k d", k=KD),
                                gram_r[:, 0].bitcast(F32), ALU.subtract).then_inc(gram_split, 1)

            def keep_heads(b, first):
                dve.wait_ge(heads_in_psum, b + 1)
                if not first:
                    dve.wait_ge(o_in_psum, b)
                for h in range(KD):
                    v.tensor_tensor(heads[:, h, 0, :], bank[2][:, h * D:h * D + P], mask[:], ALU.mult)
                    v.scalar_tensor_tensor(out=heads[:, h, 1, :], in0=bank[2][:, h * D + P:(h + 1) * D],
                                           scalar=g_col[:, h:h + 1], in1=mask[:], op0=ALU.mult, op1=ALU.mult)
                v.tensor_tensor(vb[:, ds(b % 2, 1), :].rearrange("p a c -> p (a c)"), bank[3][:, 0:KD], b_col[:],
                                ALU.mult).then_inc(heads_ready, 1)

            def times_q(b):
                dve.wait_ge(gq_in_psum, b + 1)
                for h in range(KD):
                    last = v.tensor_tensor(qGq[:, h, :], bank[4 + h][:, :], qT[:, h, :], ALU.mult)
                last.then_inc(qGq_ready, 1)

            def clamp_norm(b):
                dve.wait_ge(norm_in_psum, b + 1)
                v.tensor_scalar(nrm[:], bank[3][:, 0:NT * KD * HPT], NORM_EPS * NORM_EPS, None, ALU.max)\
                    .then_inc(norm_clamped, 1)

            def scale_o(b):
                dve.wait_ge(norm_rooted, b + 1)
                v.reciprocal(nrm[:], nrm[:]).then_inc(norm_inverted, 1)
                dve.wait_ge(norm_inverted, b + 1)
                per_head = nrm[:].rearrange("p (c h) -> p c h", c=2)
                for c in range(2):
                    last = v.tensor_tensor(
                        o_tok[:, c * NT // 2:(c + 1) * NT // 2, :].rearrange("p t (h d) -> p (t h) d", h=KD * HPT),
                        bank[6 + c][:, :].rearrange("p (h d) -> p h d", h=KD * HPT * NT // 2),
                        per_head[:, c, :].unsqueeze(2).to_broadcast([P, KD * HPT * NT // 2, D // (KD * HPT)]),
                        ALU.mult)
                last.then_inc(o_scaled, 1)

            def rest_of_oT(b):
                dve.wait_ge(oT_hi, b + 1)
                for h in range(KD):
                    last = v.scalar_tensor_tensor(out=oT_r[:, 1, h, :], in0=bank[4 + h][:, :],
                                                  scalar=vb[:, ds(b % 2, 1), h:h + 1].rearrange("p a c -> p (a c)"),
                                                  in1=oT_r[:, 0, h, :].bitcast(F32),
                                                  op0=ALU.add, op1=ALU.subtract)
                last.then_inc(oT_split, 1)

            def stats_of_proj(b, first):
                dve.wait_ge(proj_in_psum, b + 1)
                if not first:
                    dve.wait_ge(x2_stored, 16 * b)
                    dve.wait_ge(x2_stats, b)
                for c in range(NT // 2):
                    last = v.tensor_tensor(proj[:, 2 * c:2 * c + 2, :],
                                           bank[6 + c][:, :].rearrange("p (t d) -> p t d", t=2),
                                           bout_bc[:].unsqueeze(1).to_broadcast([P, 2, D]), ALU.add)
                last.then_inc(proj_ready, 1)
                dve.wait_ge(proj_ready, b + 1)
                for t in range(NT):
                    last = v.bn_stats(st2[:, t, :], proj[:, t, :])
                last.then_inc(p_stats, 1)
                dve.wait_ge(p_stats, b + 1)
                alone(dve)
                for t in range(NT):
                    last = v.bn_aggr(mv2[:, t, :], st2[:, t, :])
                last.then_inc(p_aggr, 1)

            def norm_proj(b):
                dve.wait_ge(p_std, b + 1)
                v.reciprocal(rstd2[:], rstd2[:]).then_inc(p_rstd, 1)
                dve.wait_ge(p_rstd, b + 1)
                for t in range(NT):
                    last = v.tensor_scalar(proj[:, t, :], proj[:, t, :], mv2[:, t, 0:1], rstd2[:, t:t + 1],
                                           ALU.subtract, ALU.mult)
                last.then_inc(p_normed, 1)
                dve.wait_ge(p_normed, b + 1)
                v.tensor_tensor(proj[:], proj[:], x_rows(b, 0, NT), ALU.add).then_inc(x2_ready, 1)
                dve.wait_ge(x2_ready, b + 1)
                for t in range(NT):
                    last = v.bn_stats(st3[:, t, :], proj[:, t, :])
                last.then_inc(x2_stats, 1)
                dve.wait_ge(x2_stats, b + 1)
                alone(dve)
                for t in range(NT):
                    last = v.bn_aggr(mv3[:, t, :], st3[:, t, :])
                last.then_inc(x2_aggr, 1)
                dve.wait_ge(x2_aggr, b + 1)
                v.tensor_copy(mv_x2[:, ds(b * NT, NT), :], mv3[:]).then_inc(x2_kept, 1)

            def attention(b, front=True, following=True, back=True, end=True, first_end=False):
                if end:
                    stats_of_proj(b - 2, first_end)
                if front:
                    rest_of_xnT(b)
                    rest_of_gram(b)
                if back:
                    times_q(b - 1)
                if end:
                    norm_proj(b - 2)
                if back:
                    clamp_norm(b - 1)
                    scale_o(b - 1)
                if following:
                    stats_of_x(b + 1)
                if back:
                    rest_of_oT(b - 1)
                if front:
                    keep_heads(b, not back)
                if following:
                    norm_x(b + 1)

            stats_of_x(0)
            norm_x(0, first=True)
            dve.wait_ge(attn_w_hi, 1)
            v.tensor_tensor(wqkv_r[:, 1], wqkvT[:], wqkv_r[:, 0].bitcast(F32), ALU.subtract)
            v.tensor_tensor(wout_r[:, 1], woutT[:], wout_r[:, 0].bitcast(F32), ALU.subtract)\
                .then_inc(attn_w_split, 1)
            dve.wait_ge(consts_loaded, 16 * N_CONSTS)
            attention(0, back=False, end=False)
            scale_slots()
            rest_of_slots()
            attention(1, end=False)
            attention(2, first_end=True)
            with dve.Fori(3, B - 1) as b:
                attention(b)
            attention(B - 1, following=False)
            attention(B, front=False, following=False)
            attention(B + 1, front=False, following=False, back=False)
            attention_finished(dve)

            inv_dev, length = sc_parts[:, 0, :], sc_parts[:, 1, :]
            dve.wait_ge(y_rooted, 1)
            v.reciprocal(inv_dev, roots[:, 0, :]).then_inc(y_step, 1)
            dve.wait_ge(y_step, 1)
            v.scalar_tensor_tensor(out=length, in0=roots[:, 1, :], scalar=ROOT_D, in1=inv_dev,
                                   op0=ALU.mult, op1=ALU.mult).then_inc(y_step, 1)
            dve.wait_ge(y_step, 2)
            v.tensor_scalar(length, length, NORM_EPS, 1.0 / ROOT_D, ALU.max, ALU.mult).then_inc(y_step, 1)
            dve.wait_ge(y_step, 3)
            v.reciprocal(length, length).then_inc(y_step, 1)
            dve.wait_ge(y_step, 4)
            v.tensor_tensor(sc_y[:], length, inv_dev, ALU.mult).then_inc(y_scaled, 1)

            dve.wait_ge(ident_loaded, 16)

            def make_y(b, first=False):
                dve.wait_ge(x2_loaded, 16 * (b + 1))
                dve.wait_ge(y_scaled, 1)
                if not first:
                    dve.wait_ge(y_split, b)
                for t in range(NT):
                    at = b * NT + t
                    last = v.tensor_scalar(y[:, t, :], x2[:, t, :], mv_x2[:, ds(at, 1), 0:1].rearrange(
                        "p a c -> p (a c)"), sc_y[:, ds(at, 1)], ALU.subtract, ALU.mult)
                last.then_inc(y_ready, 1)

            def rest_of_yT(b):
                for k in range(KD):
                    dve.wait_ge(yT_hi, b * KD + k + 1)
                    v.tensor_tensor(yT_r[:, 1, k, :], bank[k][:, :], yT_r[:, 0, k, :].bitcast(F32),
                                    ALU.subtract).then_inc(yT_ready, 1)

            def keep_logits(b, m, first):
                dve.wait_ge(logits_in_psum, b * E + m + 1)
                if not first:
                    dve.wait_ge(disp_exp, (b - 1) * E + m + 1)
                    dve.wait_ge(comb_shifted, (b - 1) * E + m + 1)
                    dve.wait_ge(run_min_step, b * (E - 1))
                v.tensor_scalar(neg_lt[:, m, :], bank[m % 2][:, :], -1.0, None, ALU.mult, ALU.min,
                                accum_out=neg_max[:, m:m + 1]).then_inc(logits_kept, 1)

            def fold_min(b, m, first):
                n = b * (E - 1) + m
                dve.wait_ge(logits_kept, b * E + m + 1)
                if m == 1:
                    if not first:
                        dve.wait_ge(min_in_psum, b)
                    before = neg_lt[:, 0, :]
                else:
                    dve.wait_ge(run_min_step, n - 1)
                    before = run_min[:]
                v.tensor_tensor(run_min[:], before, neg_lt[:, m, :], ALU.min).then_inc(run_min_step, 1)

            def shift_combine(b, m, first=False):
                if m == 0:
                    dve.wait_ge(shift_in_psum, b + 1)
                if m >= RING or not first:
                    dve.wait_ge(comb_stored[m % RING], 16 * (b * (E // RING) + m // RING))
                v.tensor_tensor(comb[:, m % RING, :], neg_lt[:, m, :], bank[7][:, :], ALU.subtract)\
                    .then_inc(comb_shifted, 1)

            def invert_sum(b, m):
                dve.wait_ge(disp_exp, b * E + m + 1)
                v.reciprocal(rz_disp[:, m:m + 1], z_disp[:, m:m + 1]).then_inc(disp_inv, 1)

            def rest_of_dispatch(b, m):
                dve.wait_ge(disp_hi, b * E + m + 1)
                h, cols = m // EH, slice((m % EH) * S, (m % EH + 1) * S)
                v.tensor_tensor(disp_r[:, 1, h, :, cols], bank[2 + m % 2][:, :].rearrange("p (t s) -> p t s", t=NT),
                                disp_r[:, 0, h, :, cols].bitcast(F32), ALU.subtract).then_inc(disp_split, 1)

            def shift_of_tokens(b, first):
                dve.wait_ge(min_in_psum, b + 1)
                v.tensor_reduce(tok_min[:], bank[6][:, :].rearrange("p (t n) -> p t n", t=NT), AX.X, ALU.min)\
                    .then_inc(tok_min_ready, 1)
                dve.wait_ge(tok_min_ready, b + 1)
                if not first:
                    dve.wait_ge(shift_in_psum, b)
                for t in range(NT):
                    v.tensor_scalar(diag[:, t, :], ident[:], tok_min[:, t:t + 1], None, ALU.mult)\
                        .then_inc(diag_ready, 1)

            def weights_of(b, first=False, second=False, last=False):
                if not first:
                    shift_combine(b - 1, 0, second)
                for m in range(E):
                    keep_logits(b, m, first)
                    if m:
                        invert_sum(b, m - 1)
                        fold_min(b, m, first)
                    if m + 1 < E and not first:
                        shift_combine(b - 1, m + 1, second)
                    if m >= 3:
                        rest_of_dispatch(b, m - 3)
                    if m == E - 1 and not last:
                        make_y(b + 1)
                invert_sum(b, E - 1)
                rest_of_dispatch(b, 5)
                if not last:
                    rest_of_yT(b + 1)
                shift_of_tokens(b, first)
                rest_of_dispatch(b, 6)
                rest_of_dispatch(b, 7)

            make_y(0, first=True)
            rest_of_yT(0)
            weights_of(0, first=True)
            weights_of(1, second=True)
            with dve.Fori(2, B - 1) as b:
                weights_of(b)
            weights_of(B - 1, last=True)
            for m in range(E):
                shift_combine(B - 1, m)
            weights_finished(dve)

            def rest_of_weights(e, q):
                for n, (raw, parts) in enumerate(((w1_raw, w1_r), (w2_raw, w2_r))):
                    dve.wait_ge(w_hi, 2 * e + n + 1)
                    v.tensor_tensor(parts[:, q, 1], raw, parts[:, q, 0].bitcast(F32), ALU.subtract)\
                        .then_inc(w_split, 1)

            def split_slots(e, f, first=False):
                n = e * HALVES + f + 1
                if not first:
                    dve.wait_ge(h_in_psum, e * HALVES * KH - (HALVES - 1 - f) * KH)
                src = slots_eo[:, ds(e * HALVES + f, 1), :].rearrange("p a (k n) -> p (a k) n", k=KD)
                v.tensor_copy(sl_r[:, f, 0], src).then_inc(sl_hi, 1)
                dve.wait_ge(sl_hi, n)
                v.tensor_tensor(sl_r[:, f, 1], src, sl_r[:, f, 0].bitcast(F32), ALU.subtract).then_inc(sl_split, 1)

            def rest_of_act(e, i):
                n = e * HALVES * KH + i
                dve.wait_ge(h_hi, n + 1)
                v.tensor_tensor(act_r[:, i % RING, 1, :], act[:, i % 2, :], act_r[:, i % RING, 0, :].bitcast(F32),
                                ALU.subtract).then_inc(h_split, 1)

            def keep_eo(e, f):
                dve.wait_ge(eo_steps, (e * HALVES + f + 1) * KH)
                for c in range(BH // 2):
                    last = v.tensor_tensor(slots_eo[:, ds(e * HALVES + f, 1), c * 2 * D:(c + 1) * 2 * D]
                                           .rearrange("p a (c d) -> p (a c) d", d=D),
                                           bank[4 + 2 * f + c][:, :].rearrange("p (c d) -> p c d", d=D),
                                           b2_bc[:, ds(e, 1), :].to_broadcast([P, 2, D]), ALU.add)
                last.then_inc(eo_ready, 1)

            def expert(e, q, first=False, last=False):
                split_slots(e, 1, first)
                for i in range(HALVES * KH):
                    rest_of_act(e, i)
                    if i == 2 and not first:
                        keep_eo(e - 1, 1)
                    if i == KH + 2:
                        keep_eo(e, 0)
                    if i == 7 and not last:
                        rest_of_weights(e + 1, 1 - q)
                    if i == KH + 3 and not last:
                        split_slots(e + 1, 0)

            split_slots(0, 0, first=True)
            rest_of_weights(0, 0)
            expert(0, 0, first=True)
            with dve.Fori(0, E // 2 - 1) as it:
                expert(2 * it + 1, 1)
                expert(2 * it + 2, 0)
            expert(E - 1, 1, last=True)
            keep_eo(E - 1, 1)
            experts_finished(dve)

            for u in range(2):
                v.memset(eo_r[:, u, 0, :, D:D + 1].bitcast(F32), 1.0)
                v.memset(eo_r[:, u, 0, :, D + 1:DZ].bitcast(F32), 0.0)
                v.memset(eo_r[:, u, 1, :, D:DZ].bitcast(F32), 0.0).then_inc(eo_padded, 1)

            def split_eo(b, u):
                if not (isinstance(b, int) and b < 2):
                    dve.wait_ge(comb_used, (b - 1) * E)
                src = slots_eo[:].rearrange("p (e f) n -> p e (f n)", f=HALVES)[:, :, ds(b * D, D)]
                v.tensor_copy(eo_r[:, u, 0, :, 0:D], src).then_inc(eor_hi, 1)
                dve.wait_ge(eor_hi, b + 1)
                v.tensor_tensor(eo_r[:, u, 1, :, 0:D], src, eo_r[:, u, 0, :, 0:D].bitcast(F32),
                                ALU.subtract).then_inc(eor_split, 1)

            def rest_of_combine(b, u, m):
                dve.wait_ge(comb_hi, b * E + m + 1)
                v.tensor_tensor(comb_r[:, m % RING, 1, :], comb_in[u][:, m, :], comb_r[:, m % RING, 0, :].bitcast(F32),
                                ALU.subtract).then_inc(comb_split, 1)

            def invert_z(b, u):
                dve.wait_ge(comb_used, (b + 1) * E)
                for t in range(NT):
                    last = v.reciprocal(rz_d[:, u, t:t + 1], bank[4 * u + t][:, D:D + 1])
                last.then_inc(z_inv, 1)

            def stats_of_mix(b, u):
                dve.wait_ge(mix_ready, b + 1)
                for t in range(NT):
                    last = v.bn_stats(st_d[:, u, t, :], mix[:, u, t, :])
                last.then_inc(m_stats, 1)
                dve.wait_ge(m_stats, b + 1)
                alone(dve)
                for t in range(NT):
                    last = v.bn_aggr(mv_d[:, u, t, :], st_d[:, u, t, :])
                last.then_inc(m_aggr, 1)

            def norm_mix(b, u):
                dve.wait_ge(m_std, b + 1)
                v.reciprocal(rstd_d[:, u, :], rstd_d[:, u, :]).then_inc(m_rstd, 1)
                dve.wait_ge(m_rstd, b + 1)
                for t in range(NT):
                    last = v.tensor_scalar(mix[:, u, t, :], mix[:, u, t, :], mv_d[:, u, t, 0:1],
                                           rstd_d[:, u, t:t + 1], ALU.subtract, ALU.mult)
                last.then_inc(m_normed, 1)
                dve.wait_ge(m_normed, b + 1)
                dve.wait_ge(x2d_loaded[u], 16 * (b // 2 + 1))
                v.tensor_tensor(mix[:, u], mix[:, u], x2_d[:, u], ALU.add).then_inc(out_ready, 1)

            def combine(b, u, first=False, last=False):
                for m in range(E):
                    rest_of_combine(b, u, m)
                    if m == 1 and not first:
                        invert_z(b - 1, 1 - u)
                    if m == 4 and not first:
                        stats_of_mix(b - 1, 1 - u)
                    if m == 5 and not last:
                        split_eo(b + 1, 1 - u)
                    if m == 7 and not first:
                        norm_mix(b - 1, 1 - u)

            split_eo(0, 0)
            combine(0, 0, first=True)
            with dve.Fori(0, PAIRS - 1) as it:
                combine(2 * it + 1, 1)
                combine(2 * it + 2, 0)
            combine(B - 1, 1, last=True)
            for step in (invert_z, stats_of_mix, norm_mix):
                step(B - 1, 1)


def kernel(L0_attn_x, L0_attn_w_qkv, L0_attn_w_out, L0_attn_b_out, L0_attn_norm_g, L0_attn_norm_b,
           L0_ffn_norm_gamma, L0_ffn_slot_norm_gamma, L0_ffn_slot_embeds, L0_ffn_w1, L0_ffn_b1, L0_ffn_w2,
           L0_ffn_b2):
    import numpy as np
    import concourse.bacc as bacc
    from concourse.bass_utils import run_bass_kernel_spmd

    P = 128
    x = np.asarray(L0_attn_x)
    D = x.shape[2]
    heads = np.asarray(L0_attn_norm_g).size
    per_head = D // heads

    def by_row(a, rows):
        return np.ascontiguousarray(np.asarray(a).reshape(rows, P).T)

    head_of = np.arange(P) // per_head
    arrays = {
        "x": np.ascontiguousarray(x),
        "wqkv_t": np.ascontiguousarray(np.asarray(L0_attn_w_qkv).T),
        "wout_t": np.ascontiguousarray(np.asarray(L0_attn_w_out).T),
        "bout": np.ascontiguousarray(np.asarray(L0_attn_b_out).reshape(1, D)),
        "norm_g": by_row(np.repeat(np.asarray(L0_attn_norm_g).ravel(), per_head), D // P),
        "norm_b": by_row(np.repeat(np.asarray(L0_attn_norm_b).ravel(), per_head), D // P),
        "gamma": by_row(L0_ffn_norm_gamma, D // P),
        "slot_gamma": by_row(L0_ffn_slot_norm_gamma, D // P),
        "slots_in": np.ascontiguousarray(np.asarray(L0_ffn_slot_embeds)),
        "w1": np.ascontiguousarray(np.asarray(L0_ffn_w1)),
        "b1": by_row(L0_ffn_b1, np.asarray(L0_ffn_b1).size // P),
        "w2": np.ascontiguousarray(np.asarray(L0_ffn_w2)),
        "b2": np.ascontiguousarray(np.asarray(L0_ffn_b2)[None]),
        "identity": np.eye(P, dtype=np.float32),
        "head_pick": (head_of[:, None] == np.arange(P // per_head)[None, :]).astype(np.float32),
        "head_mask": (head_of[:, None] == head_of[None, :]).astype(np.float32),
    }
    nc = bacc.Bacc("TRN2", target_bir_lowering=False, num_devices=1)
    args = {k: nc.dram_tensor(f"in_{k}", a.shape, mybir.dt.from_np(a.dtype), kind="ExternalInput").ap()
            for k, a in arrays.items()}
    out = nc.dram_tensor("out_0", x.shape, F32, kind="ExternalOutput").ap()
    attention_then_soft_moe(nc, **args, out=out)
    r = run_bass_kernel_spmd(nc, [{f"in_{k}": a for k, a in arrays.items()}], core_ids=[0])
    return r.results[0]["out_0"]
```

```python
from contextlib import ExitStack

import concourse.bass as bass
from concourse import mybir
from concourse.bass import ds

F32 = mybir.dt.float32
F32R = mybir.dt.float32r
ALU = mybir.AluOpType
ACT = mybir.ActivationFunctionType
AX = mybir.AxisListType


def attention_then_soft_moe(nc, x, wqkv_t, wout_t, bout, norm_g, norm_b, gamma, slot_gamma,
                            slots_in, w1, b1, w2, b2, identity, head_mask, head_pick, out):
    P = 128
    B, N, D = x.shape
    E, _, HID = w1.shape
    S = slots_in.shape[1]
    NT = N // P
    KD = D // P
    KH = HID // P
    HALVES = 2
    EH = E // HALVES
    BH = B // HALVES
    HALF = BH * S
    DZ = D + 2
    HPT = head_pick.shape[1]
    RING = 4
    XRING = 4
    LN_EPS = 1e-5
    NORM_EPS = 1e-12
    ROOT_D = float(D) ** 0.5
    PASSES = [(0, 0), (0, 1), (1, 0)]
    assert S == P and N == 512 and D == 256 and B == 8 and E == 8 and HALF == 512

    x2_dram = nc.dram_tensor("x2_scratch", [B, N, D], F32, kind="Internal").ap()
    comb_dram = nc.dram_tensor("combine_scratch", [B, E, P, N], F32, kind="Internal").ap()

    def token_tiles(ap):
        return ap.rearrange("b (t p) d -> p (b t) d", p=P)

    x_v, x2_v, out_v = token_tiles(x), token_tiles(x2_dram), token_tiles(out)
    comb_v = comb_dram.rearrange("b e p n -> p (b e) n")
    w1_v = w1.rearrange("e (k p) h -> p (e k) h", p=P)
    w2_v = w2.rearrange("e (k p) d -> p (e k) d", p=P)

    with ExitStack() as ctx:
        def sem(name):
            return ctx.enter_context(nc.semaphore(name))

        def sb_in(scope):
            return lambda name, shape, dt=F32: scope.enter_context(nc.sbuf_tensor(name, shape, dt))

        sb = sb_in(ctx)
        slots_eo = sb("slots_eo", [P, E * HALVES, KD * HALF])
        ident = sb("ident", [P, P])
        ones_r = sb("ones_r", [P, P], F32R)
        ones_f = sb("ones_f", [P, P])
        eps_ln = sb("eps_ln", [P, 1])
        zero_col = sb("zero_col", [P, 1])
        gam = sb("gam", [P, KD])
        sgam = sb("sgam", [P, KD])
        both_gam = sb("both_gam", [P, KD])
        b1_sb = sb("b1_sb", [P, E * KH])
        b2_bc = sb("b2_bc", [P, E, D])
        snT = sb("snT", [P, 2, KD, E * S], F32R)

        sc_y = sb("sc_y", [P, B * NT])
        mv_x2 = sb("mv_x2", [P, B * NT, 2])
        stage = sb("stage", [P, E * N])
        w1_raw = stage[:, 0:KD * HID].rearrange("p (k h) -> p k h", k=KD)
        w2_raw = stage[:, KD * HID:].rearrange("p (k d) -> p k d", k=KH)

        both = ctx.enter_context(ExitStack())
        sb = sb_in(both)
        yT_r = sb("yT_r", [P, 2, KD, N], F32R)
        x2 = sb("x2", [P, NT, D])
        y = sb("y", [P, 2, NT, D])
        roots = sb("roots", [P, 2, B * NT])
        sc_parts = sb("sc_parts", [P, 2, B * NT])
        st2 = sb("st2", [P, NT, 6])
        mv2 = sb("mv2", [P, NT, 2])
        rstd2 = sb("rstd2", [P, NT])
        st3 = sb("st3", [P, NT, 6])
        mv3 = sb("mv3", [P, NT, 2])
        with ExitStack() as scope:
            sb = sb_in(scope)
            at = 0

            def of_stage(*dims):
                nonlocal at
                size = dims[0] * dims[1]
                at += size
                return stage[:, at - size:at].rearrange("p (a b) -> p a b", a=dims[0])

            wqkvT = of_stage(KD, 3 * D)
            wqkv_r = sb("wqkv_r", [P, 2, KD, 3 * D], F32R)
            woutT = of_stage(KD, D)
            wout_r = sb("wout_r", [P, 2, KD, D], F32R)
            bout_bc = of_stage(1, D)[:, 0]
            g_col = sb("g_col", [P, KD])
            b_col = sb("b_col", [P, KD])
            mask = sb("mask", [P, P])
            head_sel = sb("head_sel", [P, HPT])
            xin = slots_eo[:, 0:XRING * NT * D // (KD * HALF), :].rearrange("p a (t d) -> p (a t) d", d=D)
            se = slots_eo[:, 8:8 + E * D // (KD * HALF), :].rearrange("p a (t d) -> p (a t) d", d=D)
            se_sq = of_stage(1, D)[:, 0]
            se_sum = sb("se_sum", [P, E])
            warm = sb("warm", [P, 1])
            se_scale = sb("se_scale", [P, E])
            st = sb("st", [P, NT, 6])
            mv = sb("mv", [P, NT, 2])
            rstd = sb("rstd", [P, NT])
            xn = sb("xn", [P, NT, D])
            xn_r = sb("xn_r", [P, 2, NT, D], F32R)
            xnT_r = sb("xnT_r", [P, 2, KD, N], F32R)
            xsum = sb("xsum", [P, KD])
            gram_r = sb("gram_r", [P, 2, KD, D], F32R)
            cw = sb("cw", [P, KD, 2 * D])
            heads = sb("heads", [P, KD, 2, P])
            vb = sb("vb", [P, 2, KD])
            qT = sb("qT", [P, KD, N])
            qGq = sb("qGq", [P, KD, N])
            nrm = sb("nrm", [P, NT * KD * HPT])
            o_tok = sb("o_tok", [P, NT, D])
            oT_r = sb("oT_r", [P, 2, KD, N], F32R)
            proj = of_stage(NT, D)

        with ExitStack() as scope:
            sb = sb_in(scope)
            disp_r = [sb("disp_r0", [P, 2, NT, EH * S], F32R)]
            disp = sb("disp", [P, RING, N])
            run_min = sb("run_min", [P, N])
            y_r = sb("y_r", [P, 2, NT, D], F32R)
            disp_r.append(sb("disp_r1", [P, 2, NT, EH * S], F32R))
            neg_lt = sb("neg_lt", [P, E, N])
            neg_max = sb("neg_max", [P, E])
            z_disp = sb("z_disp", [P, E])
            rz_disp = sb("rz_disp", [P, E])
            tok_min = sb("tok_min", [P, NT])
            diag = sb("diag", [P, NT, P], F32R)
            comb = sb("comb", [P, RING, N])

        both.close()

        with ExitStack() as scope:
            sb = sb_in(scope)
            w1_r, w2_r, sl_r = [], [], []

            def of_parity(q):
                w1_r.append(sb(f"w1_r{q}", [P, 2, KD, HID], F32R))
                w2_r.append(sb(f"w2_r{q}", [P, 2, KH, D], F32R))

            of_parity(0)
            sl_r.append(sb("sl_r0", [P, 2, KD, HALF], F32R))
            act = sb("act", [P, 2, HALF])
            act_r = sb("act_r", [P, RING, 2, HALF], F32R)
            sl_r.append(sb("sl_r1", [P, 2, KD, HALF], F32R))
            of_parity(1)

        with ExitStack() as scope:
            sb = sb_in(scope)
            eo_r = [sb("eo_r0", [P, 2, E, DZ], F32R)]
            comb_r = sb("comb_r", [P, RING, 2, N], F32R)
            eo_r.append(sb("eo_r1", [P, 2, E, DZ], F32R))
            comb_odd = sb("comb_odd", [P, E * N])
            comb_in = [a[:, :].rearrange("p (e n) -> p e n", e=E) for a in (stage, comb_odd)]
            x2_d = sb("x2_d", [P, 2, NT, D])
            mix = sb("mix", [P, 2, NT, D])
            rz_d = sb("rz_d", [P, 2, NT])
            st_d = sb("st_d", [P, 2, NT, 6])
            mv_d = sb("mv_d", [P, 2, NT, 2])
            rstd_d = sb("rstd_d", [P, 2, NT])

        bank = [ctx.enter_context(nc.psum_tensor(f"bank{i}", [P, 512], F32)) for i in range(8)]

        consts_loaded = sem("consts_loaded")
        ident_loaded = sem("ident_loaded")
        se_loaded = sem("se_loaded")
        weights_loaded = sem("weights_loaded")
        x_loaded = sem("x_loaded")
        x2_stored = sem("x2_stored")
        x2_loaded = sem("x2_loaded")
        comb_stored = [sem(f"comb_stored{r}") for r in range(RING)]
        w_loaded = sem("w_loaded")
        comb_loaded = [sem(f"comb_loaded{u}") for u in range(2)]
        x2d_loaded = [sem(f"x2d_loaded{u}") for u in range(2)]
        out_stored = [sem(f"out_stored{u}") for u in range(2)]
        consts_set = sem("consts_set")
        se_squared = sem("se_squared")
        se_rooted = sem("se_rooted")
        se_step = sem("se_step")
        se_normed = sem("se_normed")
        seT_in_psum = sem("seT_in_psum")
        snT_hi = sem("snT_hi")
        snT_ready = sem("snT_ready")
        attn_w_hi = sem("attn_w_hi")
        attn_w_split = sem("attn_w_split")
        x_stats = sem("x_stats")
        x_aggr = sem("x_aggr")
        x_std = sem("x_std")
        x_rstd = sem("x_rstd")
        xn_ready = sem("xn_ready")
        xn_hi = sem("xn_hi")
        xn_split = sem("xn_split")
        xnT_in_psum = sem("xnT_in_psum")
        xnT_hi = sem("xnT_hi")
        xnT_split = sem("xnT_split")
        gram_in_psum = sem("gram_in_psum")
        gram_hi = sem("gram_hi")
        gram_split = sem("gram_split")
        cw_in_psum = sem("cw_in_psum")
        cw_ready = sem("cw_ready")
        heads_in_psum = sem("heads_in_psum")
        sums_in_psum = sem("sums_in_psum")
        heads_ready = sem("heads_ready")
        qT_in_psum = sem("qT_in_psum")
        qT_ready = sem("qT_ready")
        gq_in_psum = sem("gq_in_psum")
        qGq_ready = sem("qGq_ready")
        o_in_psum = sem("o_in_psum")
        norm_in_psum = sem("norm_in_psum")
        norm_clamped = sem("norm_clamped")
        norm_rooted = sem("norm_rooted")
        norm_inverted = sem("norm_inverted")
        o_scaled = sem("o_scaled")
        oT_in_psum = sem("oT_in_psum")
        oT_hi = sem("oT_hi")
        oT_split = sem("oT_split")
        proj_in_psum = sem("proj_in_psum")
        proj_ready = sem("proj_ready")
        p_stats = sem("p_stats")
        p_aggr = sem("p_aggr")
        p_std = sem("p_std")
        p_rstd = sem("p_rstd")
        p_normed = sem("p_normed")
        x2_ready = sem("x2_ready")
        x2_stats = sem("x2_stats")
        x2_aggr = sem("x2_aggr")
        x2_kept = sem("x2_kept")
        y_rooted = sem("y_rooted")
        y_step = sem("y_step")
        y_scaled = sem("y_scaled")
        y_ready = sem("y_ready")
        y_hi = sem("y_hi")
        y_split = sem("y_split")
        yT_in_psum = sem("yT_in_psum")
        yT_hi = sem("yT_hi")
        yT_ready = sem("yT_ready")
        logits_in_psum = sem("logits_in_psum")
        logits_kept = sem("logits_kept")
        disp_exp = sem("disp_exp")
        disp_inv = sem("disp_inv")
        disp_normed = sem("disp_normed")
        dispT_in_psum = sem("dispT_in_psum")
        disp_hi = sem("disp_hi")
        disp_split = sem("disp_split")
        slots_in_psum = sem("slots_in_psum")
        slots_ready = sem("slots_ready")
        run_min_step = sem("run_min_step")
        min_in_psum = sem("min_in_psum")
        tok_min_ready = sem("tok_min_ready")
        diag_ready = sem("diag_ready")
        shift_in_psum = sem("shift_in_psum")
        comb_shifted = sem("comb_shifted")
        comb_exp = sem("comb_exp")
        w_hi = [sem(f"w{n}_hi") for n in (1, 2)]
        w_split = [sem(f"w{n}_split") for n in (1, 2)]
        sl_hi = sem("sl_hi")
        sl_split = sem("sl_split")
        h_in_psum = sem("h_in_psum")
        h_act = sem("h_act")
        h_hi = sem("h_hi")
        h_split = sem("h_split")
        eo_steps = sem("eo_steps")
        eo_ready = sem("eo_ready")
        eo_padded = sem("eo_padded")
        eor_hi = sem("eor_hi")
        eor_split = [sem(f"eor_split{h}") for h in range(HALVES)]
        comb_hi = sem("comb_hi")
        comb_split = sem("comb_split")
        comb_used = sem("comb_used")
        z_inv = sem("z_inv")
        mix_ready = sem("mix_ready")
        m_stats = sem("m_stats")
        m_aggr = sem("m_aggr")
        m_std = sem("m_std")
        m_rstd = sem("m_rstd")
        m_normed = sem("m_normed")
        out_ready = sem("out_ready")
        end_kept = sem("end_kept")
        end_stats = sem("end_stats")
        end_aggr = sem("end_aggr")
        end_std = sem("end_std")
        end_rstd = sem("end_rstd")
        end_normed = sem("end_normed")
        end_ready = sem("end_ready")
        end_stored = sem("end_stored")

        N_CONSTS = 9
        N_WEIGHTS = 2
        PAIRS = B // 2
        ROUND_AT = [4, 6, 8, 10]
        REST_AT = [5, 7, 9, 12]
        BEGUN = 3

        def attention_finished(eng):
            eng.wait_ge(proj_ready, B)
            eng.wait_ge(snT_ready, KD * HALVES)

        def weights_finished(eng):
            eng.wait_ge(slots_ready, B * HALVES * KD)
            eng.wait_ge(comb_exp, B * E)
            for r in range(RING):
                eng.wait_ge(comb_stored[r], 16 * B * E // RING)

        def experts_finished(eng):
            eng.wait_ge(eo_steps, E * HALVES * KH)
            eng.wait_ge(eo_ready, E * HALVES)

        def alone(eng):
            eng.nop(nofuse=True)

        def x_rows(b, t, n):
            return xin[:, ds((b % XRING) * NT + t, n), :]

        def weight_half(q, n, c):
            parts, raw = ((w1_r[q], w1_raw), (w2_r[q], w2_raw))[n]
            size = raw.shape[1] // 2
            rows = slice(c * size, (c + 1) * size)
            return raw[:, rows], parts[:, 0, rows], parts[:, 1, rows]

        def eo_rows(b):
            return slots_eo[:].rearrange("p (e f) n -> p e (f n)", f=HALVES)[:, :, ds(b * D, D)]

        def rest_of_eo(eng, b, u, h):
            eng.wait_ge(eor_hi, b + 1)
            if not (isinstance(b, int) and b < 2):
                eng.wait_ge(comb_used, (b - 1) * E)
            alone(eng)
            es = slice(h * EH, (h + 1) * EH)
            eng.tensor_tensor(eo_r[u][:, 1, es, 0:D], eo_rows(b)[:, es], eo_r[u][:, 0, es, 0:D].bitcast(F32),
                              ALU.subtract).then_inc(eor_split[h], 1)

        def y_of(b):
            return y[:, ds(b % 2, 1)].rearrange("p a t d -> p (a t) d")

        block = ctx.enter_context(nc.Block())

        @block.sync
        def _(sp):
            def load_x(b):
                sp.dma_start(xin[:, ds((b % XRING) * NT, NT), :], x_v[:, ds(b * NT, NT), :]).then_inc(x_loaded, 16)

            load_x(0)
            sp.dma_start(ident[:], identity).then_inc(ident_loaded, 16)
            sp.dma_start(wqkvT[:], wqkv_t.rearrange("(k p) o -> p k o", p=P)).then_inc(weights_loaded, 16)
            sp.wait_ge(x_loaded, 16)
            load_x(1)
            sp.dma_start(woutT[:], wout_t.rearrange("(k p) o -> p k o", p=P)).then_inc(weights_loaded, 16)
            sp.dma_start(mask[:], head_mask).then_inc(consts_loaded, 16)
            sp.dma_start(head_sel[:], head_pick).then_inc(consts_loaded, 16)
            sp.dma_start(g_col[:], norm_g).then_inc(consts_loaded, 16)
            sp.dma_start(b_col[:], norm_b).then_inc(consts_loaded, 16)
            sp.dma_start(bout_bc[:], bout.to_broadcast([P, D])).then_inc(consts_loaded, 16)
            sp.dma_start(gam[:], gamma).then_inc(consts_loaded, 16)
            sp.dma_start(sgam[:], slot_gamma).then_inc(consts_loaded, 16)
            sp.dma_start(se, slots_in.rearrange("e s d -> s e d")).then_inc(se_loaded, 16)
            sp.dma_start(b1_sb[:], b1).then_inc(consts_loaded, 16)
            sp.dma_start(b2_bc[:], b2.to_broadcast([P, E, D])).then_inc(consts_loaded, 16)

            def store_x2(b):
                sp.wait_ge(x2_ready, b + 1)
                sp.dma_start(x2_v[:, ds(b * NT, NT), :], proj[:]).then_inc(x2_stored, 16)

            for b in (2, 3):
                sp.wait_ge(x_loaded, 16 * b)
                load_x(b)
            with sp.Fori(4, B) as b:
                sp.wait_ge(x_loaded, 16 * b)
                alone(sp)
                store_x2(b - 4)
                load_x(b)
            def load_x2(b):
                sp.dma_start(x2[:], x2_v[:, ds(b * NT, NT), :]).then_inc(x2_loaded, 16)

            sp.wait_ge(x2_stored, 16 * (B - 4))
            load_x2(0)
            with sp.Fori(B - 4, B) as b:
                store_x2(b)
            attention_finished(sp)
            sp.wait_ge(x2_kept, B)
            sp.wait_ge(x2_stored, 16 * B)

            def load_weights(e):
                sp.dma_start(w1_raw, w1_v[:, ds(e * KD, KD), :]).then_inc(w_loaded, 16)
                sp.dma_start(w2_raw, w2_v[:, ds(e * KH, KH), :]).then_inc(w_loaded, 16)

            def store_combine(b, m):
                sp.wait_ge(comb_exp, b * E + m + 1)
                sp.dma_start(comb_v[:, ds(b * E + m, 1), :], comb[:, m % RING:m % RING + 1, :])\
                    .then_inc(comb_stored[m % RING], 16)

            sp.wait_ge(y_ready, 1)
            load_x2(1)
            load_weights(0)
            with sp.Fori(1, B - 1) as b:
                sp.wait_ge(y_ready, b + 1)
                load_x2(b + 1)
                for m in range(E):
                    store_combine(b - 1, m)
            for b in (B - 2, B - 1):
                for m in range(E):
                    store_combine(b, m)
            weights_finished(sp)

            with sp.Fori(1, E) as e:
                for n in range(2):
                    sp.wait_ge(w_split[n], 2 * e)
                load_weights(e)
            for n in range(2):
                sp.wait_ge(w_split[n], 2 * E)

            def load_combine(b, u):
                sp.dma_start(comb_in[u], comb_v[:, ds(b * E, E), :]).then_inc(comb_loaded[u], 16)

            def load_residual(b, u):
                sp.dma_start(x2_d[:, u], x2_v[:, ds(b * NT, NT), :]).then_inc(x2d_loaded[u], 16)

            def store_out(b, u):
                sp.wait_ge(out_ready, b + 1)
                sp.dma_start(out_v[:, ds(b * NT, NT), :], mix[:, u]).then_inc(out_stored[u], 16)

            load_combine(0, 0)
            experts_finished(sp)
            load_combine(1, 1)
            for u in range(2):
                load_residual(u, u)
            def next_combine(b, u):
                sp.wait_ge(comb_split, (b + 1) * E)
                load_combine(b + 2, u)

            def store_and_reload(b, u):
                store_out(b, u)
                load_residual(b + 2, u)

            next_combine(0, 0)
            next_combine(1, 1)
            store_and_reload(0, 0)
            with sp.Fori(1, PAIRS - 1) as it:
                for u in range(2):
                    next_combine(2 * it + u, u)
                    store_and_reload(2 * it + u - 1, 1 - u)
            store_and_reload(B - 3, 1)
            store_out(B - 2, 0)
            for c in range(2):
                sp.wait_ge(end_ready, c + 1)
                at = (B - 1) * NT + c * NT // 2
                sp.dma_start(out_v[:, at:at + NT // 2, :], mix[:, 1, c * NT // 2:(c + 1) * NT // 2, :])\
                    .then_inc(end_stored, 16)
            for u in range(2):
                sp.wait_ge(out_stored[u], 16 * (PAIRS - u))
            sp.wait_ge(end_stored, 32)
            sp.wait_ge(x2_stored, 16 * B)
            for r in range(RING):
                sp.wait_ge(comb_stored[r], 16 * B * E // RING)

        @block.gpsimd
        def _(pool):
            def add_x(b):
                pool.wait_ge(p_normed, b + 1)
                alone(pool)
                nc.gpsimd.tensor_tensor(proj[:], proj[:], x_rows(b, 0, NT), ALU.add).then_inc(x2_ready, 1)

            with pool.Fori(0, B - 1) as b:
                add_x(b)
            attention_finished(pool)

            def normalise_dispatch(b, m):
                pool.wait_ge(disp_inv, b * E + m + 1)
                alone(pool)
                nc.gpsimd.tensor_scalar(disp[:, m % RING, :], disp[:, m % RING, :], rz_disp[:, m:m + 1], 1.0,
                                        ALU.mult, ALU.mult).then_inc(disp_normed, 1)

            def rest_of_y(b, k):
                pool.wait_ge(y_hi, b * KD + k + 1)
                alone(pool)
                cols = slice(k * P, (k + 1) * P)
                nc.gpsimd.tensor_tensor(y_r[:, 1, :, cols], y_of(b)[:, :, cols], y_r[:, 0, :, cols].bitcast(F32),
                                        ALU.subtract).then_inc(y_split, 1)

            def weights_of(b):
                for m in range(E):
                    if m in (4, 6):
                        rest_of_y(b, m // 2 - 2)
                    normalise_dispatch(b, m)

            with pool.Fori(0, B) as b:
                weights_of(b)
            for c in range(2):
                raw, hi, lo = weight_half(0, 1, c)
                pool.wait_ge(w_hi[1], c + 1)
                nc.gpsimd.tensor_tensor(lo, raw, hi.bitcast(F32), ALU.subtract).then_inc(w_split[1], 1)
            experts_finished(pool)

            def add_residual(b, u):
                pool.wait_ge(x2d_loaded[u], 16 * (b // 2 + 1))
                pool.wait_ge(m_normed, b + 1)
                alone(pool)
                nc.gpsimd.tensor_tensor(mix[:, u], mix[:, u], x2_d[:, u], ALU.add).then_inc(out_ready, 1)

            rest_of_eo(pool, 1, 1, 1)
            add_residual(0, 0)
            with pool.Fori(1, PAIRS) as it:
                for u in range(2):
                    rest_of_eo(pool, 2 * it + u, u, 1)
                    add_residual(2 * it + u - 1, 1 - u)

        @block.tensor
        def _(pe):
            pe.wait_ge(ident_loaded, 16)

            def transpose_xn(b, first):
                pe.wait_ge(xn_ready, b + 1)
                if not first:
                    pe.wait_ge(cw_ready, b)
                for k in range(KD):
                    for t in range(NT):
                        last = pe.transpose(bank[k][:, t * P:(t + 1) * P], xn[:, t, k * P:(k + 1) * P], ident[:])
                    last.then_inc(xnT_in_psum, 1)

            def gram_of_x(b, first):
                pe.wait_ge(xn_split, b + 1)
                if not first:
                    pe.wait_ge(heads_ready, b)
                steps = [(t, i, j) for t in range(NT) for i, j in PASSES]
                for m in range(KD):
                    for n, (t, i, j) in enumerate(steps):
                        last = pe.matmul(bank[2][:, m * D:(m + 1) * D], xn_r[:, i, t, m * P:(m + 1) * P],
                                         xn_r[:, j, t, :], start=(n == 0), stop=(n == len(steps) - 1))
                last.then_inc(gram_in_psum, 1)

            def gram_times_kv(b):
                pe.wait_ge(gram_split, b + 1)
                pe.wait_ge(attn_w_split, 1)
                steps = [(k, i, j) for k in range(KD) for i, j in PASSES]
                for m in range(KD):
                    pe.wait_ge(qT_ready, b * KD + m + 1)
                    for n, (k, i, j) in enumerate(steps):
                        last = pe.matmul(bank[m][:, :], gram_r[:, i, k, m * P:(m + 1) * P],
                                         wqkv_r[:, j, k, D:3 * D], start=(n == 0), stop=(n == len(steps) - 1))
                    last.then_inc(cw_in_psum, 1)

            def head_products(b):
                pe.wait_ge(cw_ready, b + 1)
                for h in range(KD):
                    for k in range(KD):
                        both = cw[:, k, :].rearrange("p (a c) -> p a c", a=2)[:, :, h * P:(h + 1) * P]
                        last = pe.matmul(bank[2][:, h * D:(h + 1) * D].rearrange("p (a c) -> p a c", a=2),
                                         wqkvT[:, k, D + h * P:D + (h + 1) * P], both,
                                         start=(k == 0), stop=(k == KD - 1))
                last.then_inc(heads_in_psum, 1)
                for h in range(KD):
                    for k in range(KD):
                        last = pe.matmul(bank[3][:, h:h + 1],
                                         wqkvT[:, k, 2 * D + h * P:2 * D + (h + 1) * P], xsum[:, k:k + 1],
                                         start=(k == 0), stop=(k == KD - 1))
                last.then_inc(sums_in_psum, 1)

            def queries(b):
                pe.wait_ge(xnT_split, b + 1)
                pe.wait_ge(attn_w_split, 1)
                steps = [(k, i, j) for k in range(KD) for i, j in PASSES]
                for h in range(KD):
                    for n, (k, i, j) in enumerate(steps):
                        last = pe.matmul(bank[h][:, :], wqkv_r[:, i, k, h * P:(h + 1) * P], xnT_r[:, j, k, :],
                                         start=(n == 0), stop=(n == len(steps) - 1))
                    last.then_inc(qT_in_psum, 1)

            def gram_times_q(b, first):
                pe.wait_ge(heads_ready, b + 1)
                if first:
                    pe.wait_ge(snT_ready, KD * HALVES)
                else:
                    pe.wait_ge(oT_split, b)
                for h in range(KD):
                    last = pe.matmul(bank[4 + h][:, :], heads[:, h, 0, :], qT[:, h, :], start=True, stop=True)
                last.then_inc(gq_in_psum, 1)

            def outputs(b, first):
                if not first:
                    pe.wait_ge(proj_ready, b)
                for t in range(NT):
                    for h in range(KD):
                        at = (t % 2) * D + h * P
                        last = pe.matmul(bank[6 + t // 2][:, at:at + P], qT[:, h, t * P:(t + 1) * P],
                                         heads[:, h, 1, :], start=True, stop=True)
                last.then_inc(o_in_psum, 1)

            def norms(b):
                pe.wait_ge(qGq_ready, b + 1)
                for t in range(NT):
                    for h in range(KD):
                        at = (t * KD + h) * HPT
                        last = pe.matmul(bank[3][:, at:at + HPT], qGq[:, h, t * P:(t + 1) * P], head_sel[:],
                                         start=True, stop=True)
                last.then_inc(norm_in_psum, 1)

            def transpose_o(b):
                pe.wait_ge(o_scaled, b + 1)
                for h in range(KD):
                    for t in range(NT):
                        last = pe.transpose(bank[4 + h][:, t * P:(t + 1) * P], o_tok[:, t, h * P:(h + 1) * P], ident[:])
                    last.then_inc(oT_in_psum, 1)

            def projection(b):
                pe.wait_ge(oT_split, b + 1)
                steps = [(h, i, j) for h in range(KD) for i, j in PASSES]
                for t in range(NT):
                    for n, (h, i, j) in enumerate(steps):
                        last = pe.matmul(bank[6 + t // 2][:, (t % 2) * D:(t % 2 + 1) * D],
                                         oT_r[:, i, h, t * P:(t + 1) * P], wout_r[:, j, h, :],
                                         start=(n == 0), stop=(n == len(steps) - 1))
                last.then_inc(proj_in_psum, 1)

            def transpose_slots():
                for h in range(HALVES):
                    pe.wait_ge(se_normed, h + 1)
                    for k in range(KD):
                        for e in range(EH):
                            last = pe.transpose(bank[4 + 2 * h + k][:, e * S:(e + 1) * S],
                                                se[:, h * EH + e, k * P:(k + 1) * P], ident[:])
                        last.then_inc(seT_in_psum, 1)

            def attention(b, front=True, back=True, first_back=False, first_y=False):
                if front:
                    transpose_xn(b, not back)
                    gram_of_x(b, not back)
                if back:
                    gram_times_q(b - 1, first_back)
                    outputs(b - 1, first_back)
                    norms(b - 1)
                if front:
                    queries(b)
                if first_y:
                    transpose_y(0, 0, first=True, to=0)
                if back:
                    transpose_o(b - 1)
                if front:
                    gram_times_kv(b)
                if back:
                    projection(b - 1)
                if first_y:
                    for m in range(2):
                        logits(0, m, first=True)
                if front:
                    head_products(b)

            attention(0, back=False)
            transpose_slots()
            pe.wait_ge(consts_loaded, 16 * N_CONSTS)
            attention(1, first_back=True)
            with pe.Fori(2, B) as b:
                attention(b)

            def transpose_y(b, u, first=False, to=6):
                pe.wait_ge(y_ready, b + 1)
                if to == 0:
                    pe.wait_ge(cw_ready, B)
                for k in range(KD):
                    if not first and k == 0:
                        pe.wait_ge(tok_min_ready, b - 1)
                    if not first and k == 1:
                        pe.wait_ge(comb_shifted, (b - 1) * E)
                    for t in range(NT):
                        last = pe.transpose(bank[to + k][:, t * P:(t + 1) * P], y[:, u, t, k * P:(k + 1) * P], ident[:])
                    last.then_inc(yT_in_psum, 1)

            def logits(b, m, first):
                if m >= 2 or not first:
                    pe.wait_ge(logits_kept, b * E + m - 1)
                steps = [(k, i, j) for k in range(KD) for i, j in PASSES]
                for n, (k, i, j) in enumerate(steps):
                    if m == 0 and (i, j) == PASSES[0]:
                        pe.wait_ge(yT_ready, b * KD + k + 1)
                    last = pe.matmul(bank[m % 2][:, :], snT[:, i, k, m * S:(m + 1) * S], yT_r[:, j, k, :],
                                     start=(n == 0), stop=(n == len(steps) - 1))
                last.then_inc(logits_in_psum, 1)

            def transpose_dispatch(b, m, first=False):
                pe.wait_ge(disp_normed, b * E + m + 1)
                if m >= 2 or not first:
                    pe.wait_ge(disp_split, b * E + m - 1)
                for t in range(NT):
                    last = pe.transpose(bank[2 + m % 2][:, t * S:(t + 1) * S], disp[:, m % RING, t * P:(t + 1) * P],
                                        ident[:])
                last.then_inc(dispT_in_psum, 1)

            fill_steps = [(t, i, j) for t in range(NT) for i, j in PASSES]

            def fill_slots(b, h, k, part, first=False):
                if part == 0:
                    pe.wait_ge(disp_split, b * E + (h + 1) * EH)
                    pe.wait_ge(y_split, b * KD + k + 1)
                    if h > 0 or not first:
                        pe.wait_ge(slots_ready, (b * HALVES + h - 1) * KD + k + 1)
                n_part = len(fill_steps) // 2
                for n in range(part * n_part, (part + 1) * n_part):
                    t, i, j = fill_steps[n]
                    last = pe.matmul(bank[4 + k][:, :], y_r[:, i, t, k * P:(k + 1) * P], disp_r[h][:, j, t, :],
                                     start=(n == 0), stop=(n == len(fill_steps) - 1))
                if part == 1:
                    last.then_inc(slots_in_psum, 1)

            def transpose_min(b, last=False):
                pe.wait_ge(run_min_step, (b + 1) * (E - 1))
                if not last:
                    pe.wait_ge(yT_ready, (b + 1) * KD + 1)
                for t in range(NT):
                    done = pe.transpose(bank[6][:, t * P:(t + 1) * P], run_min[:, t * P:(t + 1) * P], ident[:])
                done.then_inc(min_in_psum, 1)

            def spread_shift(b, last=False):
                pe.wait_ge(diag_ready, (b + 1) * NT)
                if last:
                    pe.wait_ge(comb_shifted, b * E)
                else:
                    pe.wait_ge(yT_ready, (b + 2) * KD)
                pe.matmul(bank[7][:, :], ones_r[:], diag[:].rearrange("p t n -> p (t n)"), start=True, stop=True)\
                    .then_inc(shift_in_psum, 1)

            def leftover(b, m, first=False, last=False):
                if m == 0:
                    transpose_min(b, last)
                if m < 2:
                    transpose_dispatch(b, E - 2 + m, first)
                if m < 6:
                    h, k = divmod(m // 2 + 1, KD)
                    fill_slots(b, h, k, m % 2, first)
                if m == 0:
                    spread_shift(b, last)

            def weights_of(b, u, first=False, second=False, last=False):
                for m in range(E):
                    if m >= 2 or not first:
                        logits(b, m, first)
                    if m == E - 1 and not last:
                        transpose_y(b + 1, 1 - u, first)
                    if m >= 2:
                        transpose_dispatch(b, m - 2, first)
                    if not first:
                        leftover(b - 1, m, second)
                    if m >= 6:
                        fill_slots(b, 0, 0, m - 6, first)

            attention(B, front=False, first_y=True)
            attention_finished(pe)
            weights_of(0, 0, first=True)
            weights_of(1, 1, second=True)
            with pe.Fori(1, B // 2 - 1) as it:
                for u in range(2):
                    weights_of(2 * it + u, u)
            weights_of(B - 2, 0)
            weights_of(B - 1, 1, last=True)
            for m in range(6):
                leftover(B - 1, m, last=True)
            pe.wait_ge(logits_kept, B * E)
            pe.wait_ge(disp_split, B * E)

            def hidden(e, q, i, first):
                f, j = divmod(i, KH)
                if i == 0:
                    pe.wait_ge(w_split[0], 2 * (e + 1))
                if j == 0:
                    pe.wait_ge(sl_split, e * HALVES + f + 1)
                if i >= RING or not first:
                    pe.wait_ge(h_act, e * HALVES * KH + i - RING + 1)
                steps = [(k, a, c) for k in range(KD) for a, c in PASSES]
                for n, (k, a, c) in enumerate(steps):
                    last = pe.matmul(bank[i % RING][:, :], w1_r[q][:, a, k, j * P:(j + 1) * P], sl_r[f][:, c, k, :],
                                     start=(n == 0), stop=(n == len(steps) - 1))
                last.then_inc(h_in_psum, 1)

            def expert_out(e, q, i, first=False):
                f, j = divmod(i, KH)
                pe.wait_ge(h_split, e * HALVES * KH + i + 1)
                if i == 0:
                    pe.wait_ge(w_split[1], 2 * (e + 1))
                if j == 0 and first:
                    pe.wait_ge(slots_ready, B * HALVES * KD)
                    pe.wait_ge(comb_shifted, B * E)
                elif j == 0:
                    pe.wait_ge(eo_ready, (e - 1) * HALVES + f + 1)
                for c in range(BH):
                    for n, (a, w) in enumerate(PASSES):
                        last = pe.matmul(bank[4 + 2 * f + c // 2][:, (c % 2) * D:(c % 2 + 1) * D],
                                         act_r[:, i % RING, a, c * S:(c + 1) * S], w2_r[q][:, w, j, :],
                                         start=(j == 0 and n == 0 and c % 2 == 0), stop=(j == KH - 1 and n == 2),
                                         skip_group_check=True)
                last.then_inc(eo_steps, 1)

            def expert(e, q, first=False):
                for i in range(HALVES * KH):
                    hidden(e, q, i, first)
                    if i >= 2:
                        expert_out(e, q, i - 2, first)
                    elif not first:
                        expert_out(e - 1, 1 - q, HALVES * KH - 2 + i)

            expert(0, 0, first=True)
            with pe.Fori(0, E // 2 - 1) as it:
                expert(2 * it + 1, 1)
                expert(2 * it + 2, 0)
            expert(E - 1, 1)
            for i in range(2):
                expert_out(E - 1, 1, HALVES * KH - 2 + i)

            def combine(b, u):
                if not (isinstance(b, int) and b < 2):
                    pe.wait_ge(mix_ready, b - 1)
                for m in range(E):
                    if m % EH == 0:
                        pe.wait_ge(eor_split[m // EH], b + 1)
                    pe.wait_ge(comb_split, b * E + m + 1)
                    for t in range(NT):
                        for n, (i, j) in enumerate(PASSES):
                            last = pe.matmul(bank[4 * u + t][:, 0:DZ], comb_r[:, m % RING, i, t * P:(t + 1) * P],
                                             eo_r[u][:, j, m, :], start=(m == 0 and n == 0),
                                             stop=(m == E - 1 and n == 2))
                    last.then_inc(comb_used, 1)

            pe.wait_ge(h_act, E * HALVES * KH)
            pe.wait_ge(eo_padded, 1)
            combine(0, 0)
            experts_finished(pe)
            pe.wait_ge(eo_padded, 2)
            combine(1, 1)
            with pe.Fori(1, PAIRS) as it:
                for u in range(2):
                    combine(2 * it + u, u)

        @block.scalar
        def _(sc):
            act_fn = nc.scalar.activation

            def square_slots(h):
                sc.wait_ge(se_loaded, 16)
                for e in range(h * EH, (h + 1) * EH):
                    if e:
                        sc.wait_ge(se_squared, e)
                    act_fn(se_sq[:], se[:, e, :], ACT.Square, bias=zero_col[:], accum_out=se_sum[:, e:e + 1])\
                        .then_inc(se_squared, 1)

            def root_slots():
                sc.wait_ge(se_squared, E)
                act_fn(se_scale[:], se_sum[:], ACT.Sqrt, bias=zero_col[:]).then_inc(se_rooted, 1)

            def round_slots():
                sc.wait_ge(se_step, 3)
                for h in range(HALVES):
                    for k in range(KD):
                        sc.wait_ge(seT_in_psum, h * KD + k + 1)
                        act_fn(snT[:, 0, k, h * EH * S:(h + 1) * EH * S], bank[4 + 2 * h + k][:, :], ACT.Copy,
                               scale=both_gam[:, k:k + 1]).then_inc(snT_hi, 1)

            def root_x(b):
                sc.wait_ge(x_aggr, b + 1)
                act_fn(rstd[:], mv[:, :, 1], ACT.Sqrt, bias=eps_ln[:]).then_inc(x_std, 1)

            def round_xn(b, first=False):
                sc.wait_ge(xn_ready, b + 1)
                if not first:
                    sc.wait_ge(gram_in_psum, b)
                act_fn(xn_r[:, 0], xn[:], ACT.Copy).then_inc(xn_hi, 1)

            def round_xnT(b, first):
                if not first:
                    sc.wait_ge(qT_in_psum, b * KD)
                    sc.wait_ge(sums_in_psum, b)
                for k in range(KD):
                    sc.wait_ge(xnT_in_psum, b * KD + k + 1)
                    act_fn(xnT_r[:, 0, k, :], bank[k][:, :], ACT.Identity, bias=zero_col[:],
                           accum_out=xsum[:, k:k + 1]).then_inc(xnT_hi, 1)

            def round_gram(b, first):
                sc.wait_ge(gram_in_psum, b + 1)
                if not first:
                    sc.wait_ge(cw_in_psum, b * KD)
                act_fn(gram_r[:, 0], bank[2][:, :].rearrange("p (k d) -> p k d", k=KD), ACT.Copy)\
                    .then_inc(gram_hi, 1)

            def keep_cw(b, first):
                if not first:
                    sc.wait_ge(heads_in_psum, b)
                for k in range(KD):
                    sc.wait_ge(cw_in_psum, b * KD + k + 1)
                    last = act_fn(cw[:, k, :], bank[k][:, :], ACT.Copy)
                last.then_inc(cw_ready, 1)

            def keep_qT(b, first):
                if not first:
                    sc.wait_ge(o_in_psum, b)
                    sc.wait_ge(qGq_ready, b)
                for h in range(KD):
                    sc.wait_ge(qT_in_psum, b * KD + h + 1)
                    act_fn(qT[:, h, :], bank[h][:, :], ACT.Copy).then_inc(qT_ready, 1)

            def root_norm(b):
                sc.wait_ge(norm_clamped, b + 1)
                act_fn(nrm[:], nrm[:], ACT.Sqrt, bias=zero_col[:]).then_inc(norm_rooted, 1)

            def round_oT(b, first):
                if not first:
                    sc.wait_ge(proj_in_psum, b)
                for h in range(KD):
                    sc.wait_ge(oT_in_psum, b * KD + h + 1)
                    alone(sc)
                    act_fn(oT_r[:, 0, h, :], bank[4 + h][:, :], ACT.Identity, bias=vb[:, ds(b % 2, 1), h:h + 1]
                           .rearrange("p a c -> p (a c)")).then_inc(oT_hi, 1)

            def root_proj(b):
                sc.wait_ge(p_aggr, b + 1)
                act_fn(rstd2[:], mv2[:, :, 1], ACT.Sqrt, bias=eps_ln[:]).then_inc(p_std, 1)

            def attention(b, front=True, following=True, back=True, end=True, first_back=False, slots=False,
                          first_y=False):
                if front:
                    round_xnT(b, not back)
                    round_gram(b, not back)
                if end:
                    root_proj(b - 2)
                if back:
                    root_norm(b - 1)
                if slots:
                    square_slots(0)
                if front:
                    keep_qT(b, not back)
                if slots:
                    square_slots(1)
                    root_slots()
                if back:
                    round_oT(b - 1, first_back)
                if first_y:
                    round_yT(0, first=True, at=0)
                if following:
                    root_x(b + 1)
                if front:
                    keep_cw(b, not back)
                if following:
                    round_xn(b + 1)

            sc.wait_ge(consts_set, 1)
            act_fn(warm[:], zero_col[:], ACT.Sqrt, bias=zero_col[:])
            root_x(0)
            round_xn(0, first=True)
            sc.wait_ge(weights_loaded, 16 * N_WEIGHTS)
            act_fn(wqkv_r[:, 0], wqkvT[:], ACT.Copy)
            act_fn(wout_r[:, 0], woutT[:], ACT.Copy).then_inc(attn_w_hi, 1)
            attention(0, back=False, end=False, slots=True)
            round_slots()
            attention(1, end=False, first_back=True)
            with sc.Fori(2, B - 1) as b:
                attention(b)
            attention(B - 1, following=False)
            def root_x2(begin, end):
                sc.wait_ge(x2_kept, end)
                cols = slice(begin * NT, end * NT)
                act_fn(roots[:, 0, cols], mv_x2[:, cols, 1], ACT.Sqrt, bias=eps_ln[:])
                act_fn(roots[:, 1, cols], mv_x2[:, cols, 1], ACT.Sqrt, bias=zero_col[:]).then_inc(y_rooted, 1)

            def round_yT(b, first=False, at=6):
                for k in range(KD):
                    sc.wait_ge(yT_in_psum, b * KD + k + 1)
                    if k == 0 and not first:
                        sc.wait_ge(logits_in_psum, b * E)
                    act_fn(yT_r[:, 0, k, :], bank[at + k][:, :], ACT.Copy).then_inc(yT_hi, 1)

            def round_y(b, k, first=False):
                if k == 0:
                    sc.wait_ge(y_ready, b + 1)
                if not first:
                    sc.wait_ge(slots_in_psum, (b * HALVES - 1) * KD + k + 1)
                cols = slice(k * P, (k + 1) * P)
                act_fn(y_r[:, 0, :, cols], y_of(b)[:, :, cols], ACT.Copy).then_inc(y_hi, 1)

            def exp_dispatch(b, m, first):
                sc.wait_ge(logits_kept, b * E + m + 1)
                if m >= RING or not first:
                    sc.wait_ge(dispT_in_psum, b * E + m - RING + 1)
                act_fn(disp[:, m % RING, :], neg_lt[:, m, :], ACT.Exp, bias=neg_max[:, m:m + 1], scale=-1.0,
                       accum_out=z_disp[:, m:m + 1]).then_inc(disp_exp, 1)

            def round_dispatch(b, m, first):
                sc.wait_ge(dispT_in_psum, b * E + m + 1)
                h = m // EH
                if m % EH == 0 and not first:
                    sc.wait_ge(slots_in_psum, ((b - 1) * HALVES + h + 1) * KD)
                act_fn(disp_r[h][:, 0, :, (m % EH) * S:(m % EH + 1) * S],
                       bank[2 + m % 2][:, :].rearrange("p (t s) -> p t s", t=NT), ACT.Copy).then_inc(disp_hi, 1)

            def keep_slots(b, h, k):
                sc.wait_ge(slots_in_psum, (b * HALVES + h) * KD + k + 1)
                alone(sc)
                dst = slots_eo[:, h * EH * HALVES:(h + 1) * EH * HALVES, :].rearrange("p (e f) n -> p e (f n)", f=HALVES)
                at = b * S + b // BH * (KD * HALF - BH * S) + k * HALF
                act_fn(dst[:, :, ds(at, S)], bank[4 + k][:, :].rearrange("p (e s) -> p e s", e=EH), ACT.Copy,
                       scale=gam[:, k:k + 1]).then_inc(slots_ready, 1)

            def exp_combine(b, m):
                sc.wait_ge(comb_shifted, b * E + m + 1)
                act_fn(comb[:, m % RING, :], comb[:, m % RING, :], ACT.Exp, bias=zero_col[:], scale=-1.0)\
                    .then_inc(comb_exp, 1)

            def weights_of(b, first=False, second=False, last=False):
                for m in range(E):
                    if m % 2 == 0 and not first:
                        h, k = divmod(m // 2, KD)
                        keep_slots(b - 1, h, k)
                    if m in (4, 6):
                        round_y(b, m // 2 - 2, first)
                    if m == E - 1 and not last:
                        round_yT(b + 1)
                    if m < 2 and not first:
                        round_dispatch(b - 1, E - 2 + m, second)
                    exp_dispatch(b, m, first)
                    if m >= 2:
                        round_dispatch(b, m - 2, first)
                    if not first:
                        exp_combine(b - 1, m)

            root_x2(0, B - 2)
            attention(B, front=False, following=False, first_y=True)
            attention(B + 1, front=False, following=False, back=False)
            attention_finished(sc)
            weights_of(0, first=True)
            root_x2(B - 2, B)
            sc.wait_ge(x2_ready, B)
            weights_of(1, second=True)
            with sc.Fori(2, B - 1) as b:
                weights_of(b)
            weights_of(B - 1, last=True)

            def round_weights(e, q, n, c):
                sc.wait_ge(w_loaded, 32 * (e + 1))
                raw, hi, lo = weight_half(q, n, c)
                act_fn(hi, raw, ACT.Copy).then_inc(w_hi[n], 1)

            for m in range(E):
                if m % 2 == 0:
                    keep_slots(B - 1, *divmod(m // 2, KD))
                if m < 2:
                    round_dispatch(B - 1, E - 2 + m, False)
                if m == 0:
                    sc.wait_ge(logits_in_psum, B * E)
                    sc.wait_ge(y_split, B * KD)
                    for c in range(2):
                        round_weights(0, 0, 0, c)
                if m == 2:
                    sc.wait_ge(slots_in_psum, (B - 1) * HALVES * KD + KD)
                    for c in range(2):
                        round_weights(0, 0, 1, c)
                exp_combine(B - 1, m)

            def activate(e, i, first):
                n = e * HALVES * KH + i
                sc.wait_ge(h_in_psum, n + 1)
                if i >= 2 or not first:
                    sc.wait_ge(h_split, n - 1)
                alone(sc)
                act_fn(act[:, i % 2, :], bank[i % RING][:, :], ACT.Gelu, bias=b1_sb[:, ds(e * KH + i % KH, 1)])\
                    .then_inc(h_act, 1)
                sc.wait_ge(h_act, n + 1)
                if i >= RING or not first:
                    sc.wait_ge(eo_steps, n - RING + 1)
                act_fn(act_r[:, i % RING, 0, :], act[:, i % 2, :], ACT.Copy).then_inc(h_hi, 1)

            def round_combine(b, u, m, first=False):
                if m == 0:
                    sc.wait_ge(comb_loaded[u], 16 * (b // 2 + 1))
                if m >= RING or not first:
                    sc.wait_ge(comb_used, b * E + m - RING + 1)
                act_fn(comb_r[:, m % RING, 0, :], comb_in[u][:, m, :], ACT.Copy).then_inc(comb_hi, 1)

            def round_eo(b, u):
                if not (isinstance(b, int) and b < 2):
                    sc.wait_ge(comb_used, (b - 1) * E)
                act_fn(eo_r[u][:, 0, :, 0:D], eo_rows(b), ACT.Copy).then_inc(eor_hi, 1)

            def expert(e, q, first=False, last=False):
                for i in range(HALVES * KH):
                    activate(e, i, first)
                    if i == ROUND_AT[0] and not last:
                        if not first:
                            sc.wait_ge(eo_steps, e * HALVES * KH)
                        else:
                            weights_finished(sc)
                    if i in ROUND_AT and not last:
                        round_weights(e + 1, 1 - q, *divmod(ROUND_AT.index(i), 2))
                    if last and i == KH + 4:
                        sc.wait_ge(eo_steps, (E - 1) * HALVES * KH)
                        sc.wait_ge(eo_ready, (E - 1) * HALVES + 1)
                        round_eo(0, 0)
                    if last and i > KH + 4:
                        round_combine(0, 0, i - KH - 5, True)

            expert(0, 0, first=True)
            with sc.Fori(0, E // 2 - 1) as it:
                expert(2 * it + 1, 1)
                expert(2 * it + 2, 0)
            expert(E - 1, 1, last=True)
            experts_finished(sc)

            def keep_mix(b, u):
                sc.wait_ge(z_inv, b + 1)
                if not (isinstance(b, int) and b < 2):
                    sc.wait_ge(out_stored[u], 16 * (b // 2))
                for t in range(NT):
                    last = act_fn(mix[:, u, t, :], bank[4 * u + t][:, 0:D], ACT.Copy, scale=rz_d[:, u, t:t + 1])
                last.then_inc(mix_ready, 1)

            def root_mix(b, u):
                sc.wait_ge(m_aggr, b + 1)
                act_fn(rstd_d[:, u, :], mv_d[:, u, :, 1], ACT.Sqrt, bias=eps_ln[:]).then_inc(m_std, 1)

            def combine(b, u, first=False, last=False):
                for m in range(BEGUN if first else 0, E):
                    if m == 5 and not last:
                        round_eo(b + 1, 1 - u)
                    round_combine(b, u, m, first)
                    if m == 2 and not first:
                        keep_mix(b - 1, 1 - u)
                    if m == 5 and not first:
                        root_mix(b - 1, 1 - u)

            combine(0, 0, first=True)
            combine(1, 1)
            combine(2, 0)
            with sc.Fori(1, PAIRS - 1) as it:
                combine(2 * it + 1, 1)
                combine(2 * it + 2, 0)
            combine(B - 1, 1, last=True)
            sc.wait_ge(z_inv, B)
            sc.wait_ge(out_stored[1], 16 * (PAIRS - 1))
            for t in range(NT):
                last = act_fn(mix[:, 1, t, :], bank[4 + t][:, 0:D], ACT.Copy, scale=rz_d[:, 1, t:t + 1])
                if t % 2:
                    last.then_inc(end_kept, 1)
            for c in range(2):
                ts = slice(c * NT // 2, (c + 1) * NT // 2)
                sc.wait_ge(end_aggr, c + 1)
                act_fn(rstd_d[:, 1, ts], mv_d[:, 1, ts, 1], ACT.Sqrt, bias=eps_ln[:]).then_inc(end_std, 1)

        @block.vector
        def _(dve):
            v = nc.vector
            v.memset(eps_ln[:], LN_EPS)
            v.memset(zero_col[:], 0.0)
            v.memset(ones_f[:], 1.0).then_inc(se_step, 1)
            dve.wait_ge(se_step, 1)
            v.tensor_copy(ones_r[:], ones_f[:]).then_inc(consts_set, 1)

            def scale_slots():
                dve.wait_ge(consts_loaded, 16 * N_CONSTS)
                v.tensor_tensor(both_gam[:], gam[:], sgam[:], ALU.mult).then_inc(se_step, 1)
                dve.wait_ge(se_rooted, 1)
                v.tensor_scalar(se_scale[:], se_scale[:], NORM_EPS, 1.0 / ROOT_D, ALU.max, ALU.mult)\
                    .then_inc(se_step, 1)
                dve.wait_ge(se_step, 3)
                v.reciprocal(se_scale[:], se_scale[:]).then_inc(se_step, 1)
                dve.wait_ge(se_step, 4)
                for h in range(HALVES):
                    for e in range(h * EH, (h + 1) * EH):
                        last = v.tensor_scalar(se[:, e, :], se[:, e, :], se_scale[:, e:e + 1], None, ALU.mult)
                    last.then_inc(se_normed, 1)

            def rest_of_slots():
                for h in range(HALVES):
                    for k in range(KD):
                        dve.wait_ge(snT_hi, h * KD + k + 1)
                        cols = slice(h * EH * S, (h + 1) * EH * S)
                        v.scalar_tensor_tensor(out=snT[:, 1, k, cols], in0=bank[4 + 2 * h + k][:, :],
                                               scalar=both_gam[:, k:k + 1], in1=snT[:, 0, k, cols].bitcast(F32),
                                               op0=ALU.mult, op1=ALU.subtract).then_inc(snT_ready, 1)

            def stats_of_x(b):
                dve.wait_ge(x_loaded, 16 * (b + 1))
                for t in range(NT):
                    last = v.bn_stats(st[:, t, :], x_rows(b, t, 1))
                last.then_inc(x_stats, 1)
                dve.wait_ge(x_stats, b + 1)
                alone(dve)
                for t in range(NT):
                    last = v.bn_aggr(mv[:, t, :], st[:, t, :])
                last.then_inc(x_aggr, 1)

            def invert_x_std(b):
                dve.wait_ge(x_std, b + 1)
                v.reciprocal(rstd[:], rstd[:]).then_inc(x_rstd, 1)

            def norm_x(b, first=False):
                dve.wait_ge(x_rstd, b + 1)
                if not first:
                    dve.wait_ge(xnT_in_psum, b * KD)
                    dve.wait_ge(xn_split, b)
                for t in range(NT):
                    last = v.tensor_scalar(xn[:, t:t + 1, :], x_rows(b, t, 1), mv[:, t, 0:1], rstd[:, t:t + 1],
                                           ALU.subtract, ALU.mult)
                last.then_inc(xn_ready, 1)

            def rest_of_xn(b):
                dve.wait_ge(xn_hi, b + 1)
                v.tensor_tensor(xn_r[:, 1], xn[:], xn_r[:, 0].bitcast(F32), ALU.subtract).then_inc(xn_split, 1)

            def rest_of_xnT(b):
                for k in range(KD):
                    dve.wait_ge(xnT_hi, b * KD + k + 1)
                    last = v.tensor_tensor(xnT_r[:, 1, k, :], bank[k][:, :], xnT_r[:, 0, k, :].bitcast(F32),
                                           ALU.subtract)
                last.then_inc(xnT_split, 1)

            def rest_of_gram(b):
                dve.wait_ge(gram_hi, b + 1)
                v.tensor_tensor(gram_r[:, 1], bank[2][:, :].rearrange("p (k d) -> p k d", k=KD),
                                gram_r[:, 0].bitcast(F32), ALU.subtract).then_inc(gram_split, 1)

            def keep_heads(b, first):
                dve.wait_ge(heads_in_psum, b + 1)
                if not first:
                    dve.wait_ge(o_in_psum, b)
                for h in range(KD):
                    v.tensor_tensor(heads[:, h, 0, :], bank[2][:, h * D:h * D + P], mask[:], ALU.mult)
                    v.scalar_tensor_tensor(out=heads[:, h, 1, :], in0=bank[2][:, h * D + P:(h + 1) * D],
                                           scalar=g_col[:, h:h + 1], in1=mask[:], op0=ALU.mult, op1=ALU.mult)
                dve.wait_ge(sums_in_psum, b + 1)
                v.tensor_tensor(vb[:, ds(b % 2, 1), :].rearrange("p a c -> p (a c)"), bank[3][:, 0:KD], b_col[:],
                                ALU.mult).then_inc(heads_ready, 1)

            def times_q(b):
                dve.wait_ge(gq_in_psum, b + 1)
                for h in range(KD):
                    last = v.tensor_tensor(qGq[:, h, :], bank[4 + h][:, :], qT[:, h, :], ALU.mult)
                last.then_inc(qGq_ready, 1)

            def clamp_norm(b):
                dve.wait_ge(norm_in_psum, b + 1)
                v.tensor_scalar(nrm[:], bank[3][:, 0:NT * KD * HPT], NORM_EPS * NORM_EPS, None, ALU.max)\
                    .then_inc(norm_clamped, 1)

            def scale_o(b):
                dve.wait_ge(norm_rooted, b + 1)
                v.reciprocal(nrm[:], nrm[:]).then_inc(norm_inverted, 1)
                dve.wait_ge(norm_inverted, b + 1)
                per_head = nrm[:].rearrange("p (c h) -> p c h", c=2)
                for c in range(2):
                    last = v.tensor_tensor(
                        o_tok[:, c * NT // 2:(c + 1) * NT // 2, :].rearrange("p t (h d) -> p (t h) d", h=KD * HPT),
                        bank[6 + c][:, :].rearrange("p (h d) -> p h d", h=KD * HPT * NT // 2),
                        per_head[:, c, :].unsqueeze(2).to_broadcast([P, KD * HPT * NT // 2, D // (KD * HPT)]),
                        ALU.mult)
                last.then_inc(o_scaled, 1)

            def rest_of_oT(b):
                for h in range(KD):
                    dve.wait_ge(oT_hi, b * KD + h + 1)
                    alone(dve)
                    last = v.scalar_tensor_tensor(out=oT_r[:, 1, h, :], in0=bank[4 + h][:, :],
                                                  scalar=vb[:, ds(b % 2, 1), h:h + 1].rearrange("p a c -> p (a c)"),
                                                  in1=oT_r[:, 0, h, :].bitcast(F32),
                                                  op0=ALU.add, op1=ALU.subtract)
                last.then_inc(oT_split, 1)

            def keep_proj(b, first):
                dve.wait_ge(proj_in_psum, b + 1)
                if not first:
                    dve.wait_ge(x2_stored, 16 * b)
                    dve.wait_ge(x2_stats, b)
                for c in range(NT // 2):
                    last = v.tensor_tensor(proj[:, 2 * c:2 * c + 2, :],
                                           bank[6 + c][:, :].rearrange("p (t d) -> p t d", t=2),
                                           bout_bc[:].unsqueeze(1).to_broadcast([P, 2, D]), ALU.add)
                last.then_inc(proj_ready, 1)

            def stats_of_proj(b):
                dve.wait_ge(proj_ready, b + 1)
                for t in range(NT):
                    last = v.bn_stats(st2[:, t, :], proj[:, t, :])
                last.then_inc(p_stats, 1)
                dve.wait_ge(p_stats, b + 1)
                alone(dve)
                for t in range(NT):
                    last = v.bn_aggr(mv2[:, t, :], st2[:, t, :])
                last.then_inc(p_aggr, 1)

            def norm_proj(b):
                dve.wait_ge(p_std, b + 1)
                v.reciprocal(rstd2[:], rstd2[:]).then_inc(p_rstd, 1)
                dve.wait_ge(p_rstd, b + 1)
                for t in range(NT):
                    last = v.tensor_scalar(proj[:, t, :], proj[:, t, :], mv2[:, t, 0:1], rstd2[:, t:t + 1],
                                           ALU.subtract, ALU.mult)
                last.then_inc(p_normed, 1)

            def add_x(b):
                dve.wait_ge(p_normed, b + 1)
                v.tensor_tensor(proj[:], proj[:], x_rows(b, 0, NT), ALU.add).then_inc(x2_ready, 1)

            def stats_of_x2(b):
                dve.wait_ge(x2_ready, b + 1)
                for t in range(NT):
                    last = v.bn_stats(st3[:, t, :], proj[:, t, :])
                last.then_inc(x2_stats, 1)
                dve.wait_ge(x2_stats, b + 1)
                alone(dve)
                for t in range(NT):
                    last = v.bn_aggr(mv3[:, t, :], st3[:, t, :])
                last.then_inc(x2_aggr, 1)
                dve.wait_ge(x2_aggr, b + 1)
                v.tensor_copy(mv_x2[:, ds(b * NT, NT), :], mv3[:]).then_inc(x2_kept, 1)

            def attention(b, front=True, following=True, back=True, end=True, first_end=False, slots=False,
                          first_y=False):
                if end:
                    keep_proj(b - 2, first_end)
                if front:
                    rest_of_xnT(b)
                if end:
                    stats_of_proj(b - 2)
                if front:
                    rest_of_gram(b)
                if back:
                    times_q(b - 1)
                if end:
                    norm_proj(b - 2)
                if back:
                    clamp_norm(b - 1)
                    scale_o(b - 1)
                if slots:
                    dve.wait_ge(consts_loaded, 16 * N_CONSTS)
                if following:
                    stats_of_x(b + 1)
                if back:
                    rest_of_oT(b - 1)
                if first_y:
                    for k in range(KD):
                        rest_of_yT(0, k, at=0)
                if following:
                    invert_x_std(b + 1)
                    norm_x(b + 1)
                if end:
                    stats_of_x2(b - 2)
                if slots:
                    scale_slots()
                if following:
                    rest_of_xn(b + 1)
                if front:
                    keep_heads(b, not back)

            stats_of_x(0)
            invert_x_std(0)
            norm_x(0, first=True)
            rest_of_xn(0)
            dve.wait_ge(attn_w_hi, 1)
            v.tensor_tensor(wqkv_r[:, 1], wqkvT[:], wqkv_r[:, 0].bitcast(F32), ALU.subtract)
            v.tensor_tensor(wout_r[:, 1], woutT[:], wout_r[:, 0].bitcast(F32), ALU.subtract)\
                .then_inc(attn_w_split, 1)
            attention(0, back=False, end=False, slots=True)
            rest_of_slots()
            attention(1, end=False)
            attention(2, first_end=True)
            with dve.Fori(3, B - 1) as b:
                attention(b)
            attention(B - 1, following=False)

            def scale_y(n, begin, end):
                cols = slice(begin * NT, end * NT)
                inv_dev, length = sc_parts[:, 0, cols], sc_parts[:, 1, cols]
                dve.wait_ge(y_rooted, n + 1)
                v.reciprocal(inv_dev, roots[:, 0, cols]).then_inc(y_step, 1)
                dve.wait_ge(y_step, 4 * n + 1)
                v.scalar_tensor_tensor(out=length, in0=roots[:, 1, cols], scalar=ROOT_D, in1=inv_dev,
                                       op0=ALU.mult, op1=ALU.mult).then_inc(y_step, 1)
                dve.wait_ge(y_step, 4 * n + 2)
                v.tensor_scalar(length, length, NORM_EPS, 1.0 / ROOT_D, ALU.max, ALU.mult).then_inc(y_step, 1)
                dve.wait_ge(y_step, 4 * n + 3)
                v.reciprocal(length, length).then_inc(y_step, 1)
                dve.wait_ge(y_step, 4 * n + 4)
                v.tensor_tensor(sc_y[:, cols], length, inv_dev, ALU.mult).then_inc(y_scaled, 1)

            dve.wait_ge(ident_loaded, 16)

            def make_y(b, free=True):
                dve.wait_ge(x2_loaded, 16 * (b + 1))
                dve.wait_ge(y_scaled, 1)
                if free:
                    dve.wait_ge(y_split, (b - 1) * KD)
                for t in range(NT):
                    at = b * NT + t
                    last = v.tensor_scalar(y_of(b)[:, t, :], x2[:, t, :], mv_x2[:, ds(at, 1), 0:1].rearrange(
                        "p a c -> p (a c)"), sc_y[:, ds(at, 1)], ALU.subtract, ALU.mult)
                last.then_inc(y_ready, 1)

            def rest_of_yT(b, k, at=6):
                dve.wait_ge(yT_hi, b * KD + k + 1)
                v.tensor_tensor(yT_r[:, 1, k, :], bank[at + k][:, :], yT_r[:, 0, k, :].bitcast(F32),
                                ALU.subtract).then_inc(yT_ready, 1)

            def keep_logits(b, m, first):
                dve.wait_ge(logits_in_psum, b * E + m + 1)
                if not first:
                    dve.wait_ge(disp_exp, (b - 1) * E + m + 1)
                    dve.wait_ge(comb_shifted, (b - 1) * E + m + 1)
                    dve.wait_ge(run_min_step, b * (E - 1))
                v.tensor_scalar(neg_lt[:, m, :], bank[m % 2][:, :], -1.0, None, ALU.mult, ALU.min,
                                accum_out=neg_max[:, m:m + 1]).then_inc(logits_kept, 1)

            def fold_min(b, m, first):
                n = b * (E - 1) + m
                dve.wait_ge(logits_kept, b * E + m + 1)
                if m == 1:
                    if not first:
                        dve.wait_ge(min_in_psum, b)
                    before = neg_lt[:, 0, :]
                else:
                    dve.wait_ge(run_min_step, n - 1)
                    before = run_min[:]
                v.tensor_tensor(run_min[:], before, neg_lt[:, m, :], ALU.min).then_inc(run_min_step, 1)

            def shift_combine(b, m, first=False):
                if m == 0:
                    dve.wait_ge(shift_in_psum, b + 1)
                if m >= RING or not first:
                    dve.wait_ge(comb_stored[m % RING], 16 * (b * (E // RING) + m // RING))
                v.tensor_tensor(comb[:, m % RING, :], neg_lt[:, m, :], bank[7][:, :], ALU.subtract)\
                    .then_inc(comb_shifted, 1)

            def invert_sum(b, m):
                dve.wait_ge(disp_exp, b * E + m + 1)
                v.reciprocal(rz_disp[:, m:m + 1], z_disp[:, m:m + 1]).then_inc(disp_inv, 1)

            def rest_of_dispatch(b, m):
                dve.wait_ge(disp_hi, b * E + m + 1)
                h, cols = m // EH, slice((m % EH) * S, (m % EH + 1) * S)
                v.tensor_tensor(disp_r[h][:, 1, :, cols], bank[2 + m % 2][:, :].rearrange("p (t s) -> p t s", t=NT),
                                disp_r[h][:, 0, :, cols].bitcast(F32), ALU.subtract).then_inc(disp_split, 1)

            def shift_of_tokens(b, first):
                dve.wait_ge(min_in_psum, b + 1)
                v.tensor_reduce(tok_min[:], bank[6][:, :].rearrange("p (t n) -> p t n", t=NT), AX.X, ALU.min)\
                    .then_inc(tok_min_ready, 1)
                dve.wait_ge(tok_min_ready, b + 1)
                if not first:
                    dve.wait_ge(shift_in_psum, b)
                for t in range(NT):
                    v.tensor_scalar(diag[:, t, :], ident[:], tok_min[:, t:t + 1], None, ALU.mult)\
                        .then_inc(diag_ready, 1)

            def weights_of(b, first=False, second=False, last=False):
                if not first:
                    invert_sum(b - 1, E - 1)
                    shift_of_tokens(b - 1, second)
                    rest_of_dispatch(b - 1, E - 2)
                    shift_combine(b - 1, 0, second)
                for m in range(E):
                    keep_logits(b, m, first)
                    if first and m == 0:
                        norm_proj(B - 1)
                    if first and m == 2:
                        add_x(B - 1)
                    if first and m == 3:
                        stats_of_x2(B - 1)
                    if m:
                        invert_sum(b, m - 1)
                    if m == 1 and not first:
                        rest_of_dispatch(b - 1, E - 1)
                    if m == E - 1 and not last:
                        for k in range(KD):
                            rest_of_yT(b + 1, k)
                    if m + 1 < E and not first:
                        shift_combine(b - 1, m + 1, second)
                    if m:
                        fold_min(b, m, first)
                    if m >= 2:
                        rest_of_dispatch(b, m - 2)
                    if m == 5 and not last:
                        make_y(b + 1, not first)

            scale_y(0, 0, B - 2)
            make_y(0, False)
            attention(B, front=False, following=False, first_y=True)
            keep_proj(B - 1, False)
            stats_of_proj(B - 1)
            attention_finished(dve)
            weights_of(0, first=True)
            weights_of(1, second=True)
            scale_y(1, B - 2, B)
            dve.wait_ge(y_scaled, 2)
            with dve.Fori(2, B - 1) as b:
                weights_of(b)
            weights_of(B - 1, last=True)

            def rest_of_weights(e, q, n, c):
                raw, hi, lo = weight_half(q, n, c)
                dve.wait_ge(w_hi[n], 2 * e + c + 1)
                v.tensor_tensor(lo, raw, hi.bitcast(F32), ALU.subtract).then_inc(w_split[n], 1)

            def split_slots(e, f, first=False):
                n = e * HALVES + f + 1
                if not first:
                    dve.wait_ge(h_in_psum, e * HALVES * KH - (HALVES - 1 - f) * KH)
                src = slots_eo[:, ds(e * HALVES + f, 1), :].rearrange("p a (k n) -> p (a k) n", k=KD)
                v.tensor_copy(sl_r[f][:, 0], src).then_inc(sl_hi, 1)
                dve.wait_ge(sl_hi, n)
                v.tensor_tensor(sl_r[f][:, 1], src, sl_r[f][:, 0].bitcast(F32), ALU.subtract).then_inc(sl_split, 1)

            invert_sum(B - 1, E - 1)
            shift_of_tokens(B - 1, False)
            for m in range(E):
                if m < 2:
                    rest_of_dispatch(B - 1, E - 2 + m)
                shift_combine(B - 1, m)
                if m == 1:
                    for c in range(2):
                        rest_of_weights(0, 0, 0, c)
                if m == 3:
                    dve.wait_ge(dispT_in_psum, B * E)
                    dve.wait_ge(slots_ready, (B - 1) * HALVES * KD + KD)
                    split_slots(0, 0, first=True)

            def rest_of_act(e, i):
                n = e * HALVES * KH + i
                dve.wait_ge(h_hi, n + 1)
                v.tensor_tensor(act_r[:, i % RING, 1, :], act[:, i % 2, :], act_r[:, i % RING, 0, :].bitcast(F32),
                                ALU.subtract).then_inc(h_split, 1)

            def keep_eo(e, f):
                dve.wait_ge(eo_steps, (e * HALVES + f + 1) * KH)
                for c in range(BH // 2):
                    last = v.tensor_tensor(slots_eo[:, ds(e * HALVES + f, 1), c * 2 * D:(c + 1) * 2 * D]
                                           .rearrange("p a (c d) -> p (a c) d", d=D),
                                           bank[4 + 2 * f + c][:, :].rearrange("p (c d) -> p c d", d=D),
                                           b2_bc[:, ds(e, 1), :].to_broadcast([P, 2, D]), ALU.add)
                last.then_inc(eo_ready, 1)

            def pad_eo(u):
                v.memset(eo_r[u][:, 0, :, D:D + 1].bitcast(F32), 1.0)
                v.memset(eo_r[u][:, 0, :, D + 1:DZ].bitcast(F32), 0.0)
                v.memset(eo_r[u][:, 1, :, D:DZ].bitcast(F32), 0.0).then_inc(eo_padded, 1)

            def rest_of_combine(b, u, m):
                dve.wait_ge(comb_hi, b * E + m + 1)
                v.tensor_tensor(comb_r[:, m % RING, 1, :], comb_in[u][:, m, :], comb_r[:, m % RING, 0, :].bitcast(F32),
                                ALU.subtract).then_inc(comb_split, 1)

            def expert(e, q, first=False, last=False):
                split_slots(e, 1, first)
                for i in range(HALVES * KH):
                    rest_of_act(e, i)
                    if i == 2 and not first:
                        keep_eo(e - 1, 1)
                    if i == KH + 2:
                        keep_eo(e, 0)
                    if first and i == REST_AT[0]:
                        weights_finished(dve)
                    if i in REST_AT and not last:
                        rest_of_weights(e + 1, 1 - q, *divmod(REST_AT.index(i), 2))
                    if i == KH + 3 and not last:
                        split_slots(e + 1, 0)
                    if last and i == KH + 4:
                        dve.wait_ge(eo_steps, (E - 1) * HALVES * KH)
                        pad_eo(0)
                        for h in range(HALVES):
                            rest_of_eo(dve, 0, 0, h)
                    if last and i > KH + 4:
                        rest_of_combine(0, 0, i - KH - 5)

            dve.wait_ge(slots_in_psum, B * HALVES * KD)
            expert(0, 0, first=True)
            with dve.Fori(0, E // 2 - 1) as it:
                expert(2 * it + 1, 1)
                expert(2 * it + 2, 0)
            expert(E - 1, 1, last=True)
            keep_eo(E - 1, 1)
            experts_finished(dve)

            def invert_z(b, u):
                dve.wait_ge(comb_used, (b + 1) * E)
                for t in range(NT):
                    last = v.reciprocal(rz_d[:, u, t:t + 1], bank[4 * u + t][:, D:D + 1])
                last.then_inc(z_inv, 1)

            def stats_of_mix(b, u):
                dve.wait_ge(mix_ready, b + 1)
                for t in range(NT):
                    last = v.bn_stats(st_d[:, u, t, :], mix[:, u, t, :])
                last.then_inc(m_stats, 1)
                dve.wait_ge(m_stats, b + 1)
                alone(dve)
                for t in range(NT):
                    last = v.bn_aggr(mv_d[:, u, t, :], st_d[:, u, t, :])
                last.then_inc(m_aggr, 1)

            def norm_mix(b, u):
                dve.wait_ge(m_std, b + 1)
                v.reciprocal(rstd_d[:, u, :], rstd_d[:, u, :]).then_inc(m_rstd, 1)
                dve.wait_ge(m_rstd, b + 1)
                for t in range(NT):
                    last = v.tensor_scalar(mix[:, u, t, :], mix[:, u, t, :], mv_d[:, u, t, 0:1],
                                           rstd_d[:, u, t:t + 1], ALU.subtract, ALU.mult)
                last.then_inc(m_normed, 1)

            def combine(b, u, first=False, last=False):
                for m in range(BEGUN if first else 0, E):
                    rest_of_combine(b, u, m)
                    if m == 0 and not first:
                        invert_z(b - 1, 1 - u)
                    if m == 4 and not first:
                        stats_of_mix(b - 1, 1 - u)
                    if m == 5 and not last:
                        rest_of_eo(dve, b + 1, 1 - u, 0)
                    if m == 7 and not first:
                        norm_mix(b - 1, 1 - u)

            pad_eo(1)
            combine(0, 0, first=True)
            with dve.Fori(0, PAIRS - 1) as it:
                combine(2 * it + 1, 1)
                combine(2 * it + 2, 0)
            combine(B - 1, 1, last=True)
            invert_z(B - 1, 1)
            for c in range(2):
                dve.wait_ge(end_kept, c + 1)
                for t in (2 * c, 2 * c + 1):
                    last = v.bn_stats(st_d[:, 1, t, :], mix[:, 1, t, :])
                last.then_inc(end_stats, 1)
                dve.wait_ge(end_stats, c + 1)
                for t in (2 * c, 2 * c + 1):
                    last = v.bn_aggr(mv_d[:, 1, t, :], st_d[:, 1, t, :])
                last.then_inc(end_aggr, 1)
            dve.wait_ge(x2d_loaded[1], 16 * PAIRS)
            for c in range(2):
                ts = slice(c * NT // 2, (c + 1) * NT // 2)
                dve.wait_ge(end_std, c + 1)
                v.reciprocal(rstd_d[:, 1, ts], rstd_d[:, 1, ts]).then_inc(end_rstd, 1)
                dve.wait_ge(end_rstd, c + 1)
                for t in (2 * c, 2 * c + 1):
                    last = v.tensor_scalar(mix[:, 1, t, :], mix[:, 1, t, :], mv_d[:, 1, t, 0:1],
                                           rstd_d[:, 1, t:t + 1], ALU.subtract, ALU.mult)
                last.then_inc(end_normed, 1)
                dve.wait_ge(end_normed, c + 1)
                v.tensor_tensor(mix[:, 1, ts], mix[:, 1, ts], x2_d[:, 1, ts], ALU.add).then_inc(end_ready, 1)


def kernel(L0_attn_x, L0_attn_w_qkv, L0_attn_w_out, L0_attn_b_out, L0_attn_norm_g, L0_attn_norm_b,
           L0_ffn_norm_gamma, L0_ffn_slot_norm_gamma, L0_ffn_slot_embeds, L0_ffn_w1, L0_ffn_b1, L0_ffn_w2,
           L0_ffn_b2):
    import numpy as np
    import concourse.bacc as bacc
    from concourse.bass_utils import run_bass_kernel_spmd

    P = 128
    x = np.asarray(L0_attn_x)
    D = x.shape[2]
    heads = np.asarray(L0_attn_norm_g).size
    per_head = D // heads

    def by_row(a, rows):
        return np.ascontiguousarray(np.asarray(a).reshape(rows, P).T)

    head_of = np.arange(P) // per_head
    arrays = {
        "x": np.ascontiguousarray(x),
        "wqkv_t": np.ascontiguousarray(np.asarray(L0_attn_w_qkv).T),
        "wout_t": np.ascontiguousarray(np.asarray(L0_attn_w_out).T),
        "bout": np.ascontiguousarray(np.asarray(L0_attn_b_out).reshape(1, D)),
        "norm_g": by_row(np.repeat(np.asarray(L0_attn_norm_g).ravel(), per_head), D // P),
        "norm_b": by_row(np.repeat(np.asarray(L0_attn_norm_b).ravel(), per_head), D // P),
        "gamma": by_row(L0_ffn_norm_gamma, D // P),
        "slot_gamma": by_row(L0_ffn_slot_norm_gamma, D // P),
        "slots_in": np.ascontiguousarray(np.asarray(L0_ffn_slot_embeds)),
        "w1": np.ascontiguousarray(np.asarray(L0_ffn_w1)),
        "b1": by_row(L0_ffn_b1, np.asarray(L0_ffn_b1).size // P),
        "w2": np.ascontiguousarray(np.asarray(L0_ffn_w2)),
        "b2": np.ascontiguousarray(np.asarray(L0_ffn_b2)[None]),
        "identity": np.eye(P, dtype=np.float32),
        "head_pick": (head_of[:, None] == np.arange(P // per_head)[None, :]).astype(np.float32),
        "head_mask": (head_of[:, None] == head_of[None, :]).astype(np.float32),
    }
    nc = bacc.Bacc("TRN2", target_bir_lowering=False, num_devices=1)
    args = {k: nc.dram_tensor(f"in_{k}", a.shape, mybir.dt.from_np(a.dtype), kind="ExternalInput").ap()
            for k, a in arrays.items()}
    out = nc.dram_tensor("out_0", x.shape, F32, kind="ExternalOutput").ap()
    attention_then_soft_moe(nc, **args, out=out)
    r = run_bass_kernel_spmd(nc, [{f"in_{k}": a for k, a in arrays.items()}], core_ids=[0])
    return r.results[0]["out_0"]
```
